# Optimizing a Trainium2 kernel written in Bass

```python
import numpy as np
import jax
import jax.numpy as jnp

def _softmax(x, axis=-1):
    return jax.nn.softmax(x, axis=axis)

def _gelu(x):
    return jax.nn.gelu(x, approximate=True)

def _silu(x):
    return jax.nn.silu(x)

def _sigmoid(x):
    return jax.nn.sigmoid(x)

def _layernorm(x, axis=-1, eps=1e-05):
    m = jnp.mean(x, axis=axis, keepdims=True)
    v = jnp.var(x, axis=axis, keepdims=True)
    return (x - m) / jnp.sqrt(v + eps)

def _scatter_add(tgt, idx, src, axis=0):
    return tgt.at[idx].add(src)

def _segment_sum(src, seg, n):
    return jax.ops.segment_sum(src, seg, n)
kernel_name = 'mk_gnn_ffn_d1_gnn_r8_2e3fff'

def setup_inputs(seed: int=0):
    np.random.seed(seed)
    _w = jnp.asarray

    def _rec_inputs():
        import jax
        import jax.numpy as jnp
        _gk = jax.random.key(seed)
        x = -0.0002117 + 1 * jax.random.normal(jax.random.fold_in(_gk, 1), (3125, 1024), jnp.float32)
        src = jax.random.randint(jax.random.fold_in(_gk, 2), (50000,), 0, 3125, jnp.int32)
        dst = jax.random.randint(jax.random.fold_in(_gk, 3), (50000,), 0, 3125, jnp.int32)
        _o = jnp.argsort(dst, stable=True)
        src = src[_o]
        dst = dst[_o]
        return (x, src, dst)
    x, src, dst = _rec_inputs()

    def _L0_gnn_setup():
        import jax, jax.numpy as jnp
        import numpy as np
        N = 3125
        E = 50000
        H = 4
        C = 256
        D_IN = 1024
        NEG_SLOPE = 0.2
        key = jax.random.key(seed)
        k1, k2, k3, k4, k5, k6 = jax.random.split(key, 6)
        x = jax.random.normal(k1, (N, D_IN), dtype=jnp.float32)
        edge_index = jax.random.randint(k2, (2, E), 0, N, dtype=jnp.int64)
        scale = 1.0 / np.sqrt(D_IN)
        W = jax.random.normal(k3, (D_IN, H * C), dtype=jnp.float32) * scale
        att_src = jax.random.normal(k4, (H, C), dtype=jnp.float32) * 0.1
        att_dst = jax.random.normal(k5, (H, C), dtype=jnp.float32) * 0.1
        bias = jax.random.normal(k6, (H * C,), dtype=jnp.float32) * 0.01
        return {'x': x, 'edge_index': edge_index, 'W': W, 'att_src': att_src, 'att_dst': att_dst, 'bias': bias}
    _L0_gnn_all = _L0_gnn_setup()
    _L0_gnn_in = {k: v for k, v in _L0_gnn_all.items() if k in ('W', 'att_src', 'att_dst', 'bias')}
    del _L0_gnn_all

    def _L0_ffn_setup():
        import jax, jax.numpy as jnp
        import numpy as np
        BLOCK_SIZE = 32
        FP6_E2M3_MAX = 7.5

        def _build_fp6_e2m3_grid():
            vals = set()
            for bits in range(64):
                s = bits >> 5 & 1
                e = bits >> 3 & 3
                m = bits & 7
                v = m / 8.0 if e == 0 else (1.0 + m / 8.0) * 2.0 ** (e - 1)
                vals.add(-v if s else v)
            return np.array(sorted(vals), dtype=np.float32)
        _GRID = jnp.asarray(_build_fp6_e2m3_grid())

        def _nearest_on_grid(x, grid):
            idx = jnp.clip(jnp.searchsorted(grid, x), 0, grid.shape[0] - 1)
            idx_lo = jnp.maximum(idx - 1, 0)
            v_hi = grid[idx]
            v_lo = grid[idx_lo]
            return jnp.where(jnp.abs(x - v_lo) <= jnp.abs(x - v_hi), v_lo, v_hi)

        def _mx_quantize(t, eps=1e-30):
            rows, K = t.shape
            blocks = t.reshape(rows, K // BLOCK_SIZE, BLOCK_SIZE)
            scales = jnp.maximum(jnp.max(jnp.abs(blocks), axis=-1) / FP6_E2M3_MAX, eps)
            q = _nearest_on_grid(blocks / scales[..., None], _GRID)
            return (q, scales)
        key = jax.random.key(seed)
        k1, k2, k3 = jax.random.split(key, 3)
        x = jax.random.normal(k1, (8, 1024, 1024), dtype=jnp.float32)
        weight = jax.random.normal(k2, (1024, 1024), dtype=jnp.float32) * 0.02
        bias = jax.random.normal(k3, (1024,), dtype=jnp.float32) * 0.02
        return {'x': x, 'weight': weight, 'bias': bias}
    _L0_ffn_all = _L0_ffn_setup()
    _L0_ffn_in = {k: v for k, v in _L0_ffn_all.items() if k in ('weight', 'bias')}
    del _L0_ffn_all
    return {'x': x, 'src': src, 'dst': dst, 'L0_gnn_W': _L0_gnn_in['W'], 'L0_gnn_att_src': _L0_gnn_in['att_src'], 'L0_gnn_att_dst': _L0_gnn_in['att_dst'], 'L0_gnn_bias': _L0_gnn_in['bias'], 'L0_ffn_weight': _L0_ffn_in['weight'], 'L0_ffn_bias': _L0_ffn_in['bias']}

def reference(x, src, dst, L0_gnn_W, L0_gnn_att_src, L0_gnn_att_dst, L0_gnn_bias, L0_ffn_weight, L0_ffn_bias):
    import jax
    import jax.numpy as jnp

    def _L0_gnn_ref(x, edge_index, W, att_src, att_dst, bias):
        import jax, jax.numpy as jnp
        import numpy as np
        N = 3125
        E = 50000
        H = 4
        C = 256
        D_IN = 1024
        NEG_SLOPE = 0.2
        xp = (x @ W).reshape(N, H, C)
        a_src = jnp.einsum('nhc,hc->nh', xp, att_src)
        a_dst = jnp.einsum('nhc,hc->nh', xp, att_dst)
        loops = jnp.arange(N, dtype=edge_index.dtype)
        src = jnp.concatenate([edge_index[0], loops])
        dst = jnp.concatenate([edge_index[1], loops])
        e = jax.nn.leaky_relu(a_src[src] + a_dst[dst], NEG_SLOPE)
        m = jax.ops.segment_max(e, dst, num_segments=N)
        ee = jnp.exp(e - m[dst])
        z = jax.ops.segment_sum(ee, dst, num_segments=N)
        alpha = ee / z[dst]
        msgs = xp[src] * alpha[:, :, None]
        out = jax.ops.segment_sum(msgs, dst, num_segments=N)
        out = out.reshape(N, H * C) + bias
        return jax.nn.relu(out)

    def _L0_ffn_ref(x, weight, bias):
        import jax, jax.numpy as jnp
        import numpy as np
        BLOCK_SIZE = 32
        FP6_E2M3_MAX = 7.5

        def _build_fp6_e2m3_grid():
            vals = set()
            for bits in range(64):
                s = bits >> 5 & 1
                e = bits >> 3 & 3
                m = bits & 7
                v = m / 8.0 if e == 0 else (1.0 + m / 8.0) * 2.0 ** (e - 1)
                vals.add(-v if s else v)
            return np.array(sorted(vals), dtype=np.float32)
        _GRID = jnp.asarray(_build_fp6_e2m3_grid())

        def _nearest_on_grid(x, grid):
            idx = jnp.clip(jnp.searchsorted(grid, x), 0, grid.shape[0] - 1)
            idx_lo = jnp.maximum(idx - 1, 0)
            v_hi = grid[idx]
            v_lo = grid[idx_lo]
            return jnp.where(jnp.abs(x - v_lo) <= jnp.abs(x - v_hi), v_lo, v_hi)

        def _mx_quantize(t, eps=1e-30):
            rows, K = t.shape
            blocks = t.reshape(rows, K // BLOCK_SIZE, BLOCK_SIZE)
            scales = jnp.maximum(jnp.max(jnp.abs(blocks), axis=-1) / FP6_E2M3_MAX, eps)
            q = _nearest_on_grid(blocks / scales[..., None], _GRID)
            return (q, scales)
        batch_shape = x.shape[:-1]
        in_features = x.shape[-1]
        x2 = x.astype(jnp.float32).reshape(-1, in_features)
        w2 = weight.astype(jnp.float32)
        xq, xs = _mx_quantize(x2)
        wq, ws = _mx_quantize(w2)
        xd = (xq * xs[..., None]).reshape(x2.shape)
        wd = (wq * ws[..., None]).reshape(w2.shape)
        out = xd @ wd.T + bias
        return out.reshape(*batch_shape, -1)
    edge_index = jnp.stack([src, dst])
    x = x + _L0_gnn_ref(_layernorm(x, axis=-1), edge_index, L0_gnn_W, L0_gnn_att_src, L0_gnn_att_dst, L0_gnn_bias)
    x = x + _L0_ffn_ref(_layernorm(x, axis=-1)[None], L0_ffn_weight, L0_ffn_bias)[0]
    return x

_drawn_inputs = setup_inputs


def setup_inputs(seed=0):
    import zlib

    import numpy as np

    out = dict(_drawn_inputs(seed))
    spreads = {}
    factors = {'L0_gnn_bias': 5.69, 'L0_ffn_bias': 3.552}
    for name, (base, spread) in spreads.items():
        noise = np.random.default_rng([zlib.crc32(name.encode()), seed]).standard_normal(out[name].shape)
        drawn = base * np.exp(spread * noise) if base else spread * noise
        out[name] = jnp.asarray(drawn.astype(out[name].dtype))
    for name, factor in factors.items():
        out[name] = (out[name] * factor).astype(out[name].dtype)
    return out
```

```python
import concourse.bass as bass
from concourse import mybir
from contextlib import ExitStack

F32 = mybir.dt.float32
BF16 = mybir.dt.bfloat16
I32 = mybir.dt.int32
ALU = mybir.AluOpType
ACT = mybir.ActivationFunctionType
AX = mybir.AxisListType

P = 128
N = 3125
D = 1024
E = 50000
HEADS = 4
C = D // HEADS
KC = D // P
TILES = -(-N // P)
NP = TILES * P
LAST_ROWS = N - (TILES - 1) * P
SUB = 2
ET = -(-E // (SUB * P))
EC = ET * SUB
EP = EC * P
STEPS = -(-(ET + TILES - 1) // 4) * 4
KCOLS = 2 * P
HCOLS = 17
HBATCH = 24
HPAD = HCOLS * HBATCH
GCOLS = 5
GSLOTS = 5
GFILLS = 80
GPAD = GCOLS * (GFILLS + GSLOTS)
BIG = 1e38
FAR = 1 << 20
SLOTS = 2
EPS = 1e-5
SLOPE = 0.2
QBLOCK = 32
QB = D // QBLOCK
QMAX = 7.5
EXPONENT = 0x7F800000
F16 = mybir.dt.float16
NUM_SCALE = 2.0 ** 14
ROW_SCALE = 2.0 ** 9


class Chain:

    def __init__(self, eng, sem):
        self.eng, self.sem, self.base, self.n = eng, sem, 0, 0

    def link(self, ins):
        ins.then_inc(self.sem, 1)
        self.n += 1
        self.eng.wait_ge(self.sem, self.base + self.n)

    def enter(self, i, per):
        back = (self.base, self.n, per)
        self.base = i * per + (self.base + self.n)
        self.n = 0
        return back

    def leave(self, back, turns):
        base, n, per = back
        assert self.n == per, (self.n, per)
        self.base, self.n = base, n + per * turns


def blocks(a):
    return a.rearrange("p (b k) -> p b k", k=QBLOCK)


def spread(a):
    return a.unsqueeze(2).to_broadcast([P, QB, QBLOCK])


def block_scales(nc, chain, src, scale, inv):
    chain.link(nc.vector.tensor_reduce(out=scale, in_=blocks(src), axis=AX.X, op=ALU.max, apply_absolute_value=True))
    chain.link(nc.vector.tensor_scalar(scale, scale, 1.0 / QMAX, 1e-30, ALU.mult, ALU.max))
    return nc.vector.reciprocal(inv, scale)


def round_to_grid(nc, chain, y, step, scale, out):
    chain.link(nc.vector.tensor_scalar(step.bitcast(I32), y.bitcast(I32), EXPONENT, None, ALU.bitwise_and))
    chain.link(nc.vector.tensor_scalar(step, step, 1.0, None, ALU.max))
    chain.link(nc.vector.scalar_tensor_tensor(out=y, in0=step, scalar=6.0625, in1=y, op0=ALU.mult, op1=ALU.subtract))
    chain.link(nc.vector.tensor_scalar(y.bitcast(I32), y.bitcast(I32), -(1 << 18), None, ALU.bitwise_and))
    chain.link(nc.vector.scalar_tensor_tensor(out=y, in0=step, scalar=6.0, in1=y, op0=ALU.mult, op1=ALU.subtract))
    return nc.vector.tensor_tensor(out=blocks(out), in0=blocks(y), in1=spread(scale), op=ALU.mult)


SCALE_LINKS = 2
ROUND_LINKS = 5


def power_scale(nc, chain, largest, low, scale, inverse, top):
    chain.link(nc.vector.tensor_scalar(low, largest, 2.0 ** -100, None, ALU.max))
    chain.link(nc.vector.tensor_scalar(low.bitcast(I32), low.bitcast(I32), EXPONENT, None, ALU.bitwise_and))
    chain.link(nc.vector.tensor_scalar(scale.bitcast(I32), low.bitcast(I32), -1.0, float((254 + top) << 23), ALU.mult, ALU.add))
    chain.link(nc.vector.tensor_scalar(inverse.bitcast(I32), low.bitcast(I32), float(-(top << 23)), None, ALU.add))


def inverse_root(nc, chain, root, value, out, tmp):
    chain.link(nc.vector.reciprocal(out, root))
    chain.link(nc.vector.tensor_scalar(tmp, out, out, value, ALU.mult, ALU.mult))
    chain.link(nc.vector.tensor_scalar(tmp, tmp, -0.5, 1.5, ALU.mult, ALU.add))
    chain.link(nc.vector.tensor_tensor(out=out, in0=out, in1=tmp, op=ALU.mult))


STAT_LINKS = 2
ROOT_LINKS = 4


def program(nc, x, src, dst, W, att_src, att_dst, gnn_bias, ffn_w, ffn_bias, out, upto=4):
    d_xnT = nc.dram_tensor("d_xnT", (TILES, P, D), F32, kind="Internal").ap()
    d_xp = nc.dram_tensor("d_xp", (NP, 2 * D), F16, kind="Internal").ap()
    d_own = nc.dram_tensor("d_own", (NP, D), F32, kind="Internal").ap()
    d_asrc = nc.dram_tensor("d_asrc", (NP, HEADS), F32, kind="Internal").ap()
    d_node = nc.dram_tensor("d_node", (NP, 2 * HEADS), F32, kind="Internal").ap()
    d_src = nc.dram_tensor("d_src", (ET, SUB * P), F32, kind="Internal").ap()
    d_dst = nc.dram_tensor("d_dst", (ET, SUB * P), F32, kind="Internal").ap()
    d_segmax = nc.dram_tensor("d_segmax", (EP, HEADS), F32, kind="Internal").ap()
    d_head = nc.dram_tensor("d_head", (EP, 2 * HEADS), F32, kind="Internal").ap()
    d_num = nc.dram_tensor("d_num", (ET, SUB * P * HEADS), F32, kind="Internal").ap()
    d_tile = nc.dram_tensor("d_tile", (KCOLS,), I32, kind="Internal").ap()

    whole = ExitStack()

    def maker(ctx):
        def sb(name, shape, dt=F32):
            return ctx.enter_context(nc.sbuf_tensor(name, shape, dt))

        def ps(name, shape, dt=F32):
            return ctx.enter_context(nc.psum_tensor(name, shape, dt))

        def sem(name):
            return ctx.enter_context(nc.semaphore(name))
        return sb, ps, sem

    with whole:
        sb, ps, sem = maker(whole)
        ident = sb("ident", [P, P])
        iota = sb("iota", [P, P])
        logits = sb("logits", [P, TILES, 2 * HEADS])
        self_num = sb("self_num", [P, TILES, HEADS])
        tables = sb("tables", [P, 14 * SUB * KCOLS])
        part = lambda a, b: tables[:, a * SUB * KCOLS:b * SUB * KCOLS]
        dstT = part(0, 1)
        srcT = part(1, 2).bitcast(I32)
        numT = part(2, 6).rearrange("p (h k) -> p h k", h=HEADS)
        numT16 = part(6, 14).bitcast(F16).rearrange("p (k v b) -> p k v b", v=2 * HEADS, b=2)
        xp_scale = sb("xp_scale", [P, 1])
        xp_inverse = sb("xp_inverse", [P, 1])
        wd_scale = sb("wd_scale", [P, 1])
        wd_inverse = sb("wd_inverse", [P, 1])
        tile_row = sb("tile_row", [1, KCOLS], I32)
        wdT = sb("wdT", [P, KC, 2, D], F16)
        front = ExitStack()
        with front:
            sb, ps, sem = maker(front)
            w = sb("w", [P, KC, D])
            dst1 = sb("dst1", [P, HPAD], I32)
            src1 = sb("src1", [P, GPAD], I32)
            dfirst = sb("dfirst", [1, ET], I32)
            wf = sb("wf", [P, KC, D])
            largest = sb("largest", [P, 2])
            count = sb("count", [P, TILES])
            ones = sb("ones", [P, P])
            upper = sb("upper", [P, P])
            normalise(nc, maker, locals())
            if upto >= 2:
                project(nc, maker, locals())
        if upto >= 3:
            back = ExitStack()
            with back:
                sb, ps, sem = maker(back)
                acc = sb("acc", [P, TILES, D])
                zsum = sb("zsum", [P, TILES, 2 * HEADS])
                aggregate(nc, maker, locals())
                if upto >= 4:
                    finish(nc, maker, locals())


def normalise(nc, maker, g):
    x, src, dst, W, att_src, att_dst = g["x"], g["src"], g["dst"], g["W"], g["att_src"], g["att_dst"]
    ident, iota, logits = g["ident"], g["iota"], g["logits"]
    w, dst1, src1, dfirst, count, ones, upper = (g[k] for k in ("w", "dst1", "src1", "dfirst", "count", "ones", "upper"))
    ctx = ExitStack()
    with ctx:
        sb, ps, sem = maker(ctx)
        attb = sb("attb", [P, 2, D])
        wa = sb("wa", [P, KC, 2 * HEADS])
        wprod = [sb(f"wprod{j}", [P, D]) for j in range(2)]
        dlo_i = sb("dlo_i", [P, HPAD], I32)
        dlo = sb("dlo", [P, HPAD], BF16)
        dhi = sb("dhi", [P, HPAD], BF16)
        iota_b = sb("iota_b", [P, P], BF16)
        hot_hi = sb("hot_hi", [P, HPAD, 32], BF16)
        hot_lo = [sb(f"hot_lo{j}", [P, HCOLS, P], BF16) for j in range(2)]
        zeros = g["tables"][:, 0:EC * 2 * HEADS]
        xt = [sb(f"xt{j}", [P, D]) for j in range(2)]
        xn = [g["tables"][:, EC * 2 * HEADS + j * D:EC * 2 * HEADS + (j + 1) * D] for j in range(2)]
        xnT = [sb(f"xnT{j}", [P, KC, P]) for j in range(2)]
        stats = sb("stats", [P, 2, 6])
        mv = [sb(f"mv{j}", [P, 2]) for j in range(2)]
        std = [sb(f"std{j}", [P, 1]) for j in range(2)]
        rstd = [sb(f"rstd{j}", [P, 1]) for j in range(2)]
        newton = sb("newton", [P, 1])
        tr_ps = [ps(f"tr_ps{j}", [P, D]) for j in range(2)]
        lg_ps = [ps(f"lg_ps{j}", [P, 512]) for j in range(2)]
        hist_ps = ps("hist_ps", [P, 512])

        made = sem("made")
        pads_set = sem("pads_set")
        edges_in = sem("edges_in")
        att_in = sem("att_in")
        w_in = sem("w_in")
        wf_in = sem("wf_in")
        zeroed = sem("zeroed")
        wprod_ready = sem("wprod_ready")
        wprod_free = sem("wprod_free")
        hi_ready = sem("hi_ready")
        lo_ready = sem("lo_ready")
        lo_free = sem("lo_free")
        x_in = [sem(f"x_in{j}") for j in range(2)]
        var_ready = sem("var_ready")
        std_ready = sem("std_ready")
        xn_ready = sem("xn_ready")
        tr_done = sem("tr_done")
        xnT_ready = sem("xnT_ready")
        xnT_out = [sem(f"xnT_out{j}") for j in range(2)]
        lg_done = sem("lg_done")
        lg_kept = sem("lg_kept")
        dve_own = sem("dve_own1")
        pool_own = sem("pool_own1")
        pool_turn = sem("pool_turn")
        dve_turn = sem("dve_turn")
        block = ctx.enter_context(nc.Block())

        def rows(t, n=P):
            return x[bass.ds(t * P, n), :]

        @block.sync
        def _(sp):
            sp.wait_ge(pads_set, 2)
            cut = (P - 1) * EC
            for tile, vec in ((dst1, dst), (src1, src)):
                sp.dma_start(tile[0:P - 1, 0:EC], vec[0:cut].rearrange("(p c) -> p c", c=EC)).then_inc(edges_in, 16)
                sp.dma_start(tile[P - 1:P, 0:E - cut], vec[cut:E].unsqueeze(0)).then_inc(edges_in, 16)
            sp.dma_start(dfirst[:, :], dst[0:(ET - 1) * SUB * P + 1:SUB * P].unsqueeze(0),
                         allow_slow_non_contiguous=True).then_inc(edges_in, 16)
            sp.dma_start(attb[:, 0, :], att_src.rearrange("h c -> (h c)").partition_broadcast(P)).then_inc(att_in, 16)
            sp.dma_start(attb[:, 1, :], att_dst.rearrange("h c -> (h c)").partition_broadcast(P)).then_inc(att_in, 16)

            def load(t, j, n=P):
                sp.wait_ge(xn_ready, t + 1)
                sp.dma_start(xt[j][0:n, :], rows(t, n)).then_inc(x_in[j], 16)

            load(0, 0)
            load(1, 1)
            sp.dma_start(w[:, :, :], W.rearrange("(c p) n -> p c n", p=P)).then_inc(w_in, 16)

            sp.dma_start(g["wf"][:, :, :], g["ffn_w"].rearrange("(c p) n -> p c n", p=P)).then_inc(wf_in, 16)

            def store(t, j, n):
                sp.wait_ge(xnT_ready, t + 1)
                sp.dma_start(g["d_xnT"][bass.ds(t, 1), :, :].rearrange("o p n -> (o p) n"),
                             xnT[j][:, :, :].rearrange("p c n -> p (c n)")).then_inc(xnT_out[j], 16)

            with sp.Fori(0, TILES // 2 - 1) as i:
                for j in range(2):
                    load(2 * i + j + 2, j)
                    store(2 * i + j, j, i)
            load(TILES - 1, 0, LAST_ROWS)
            for t in range(TILES - 3, TILES):
                store(t, t % 2, t // 2)
            sp.wait_ge(xnT_out[0], 16 * (TILES // 2 + 1))
            sp.wait_ge(xnT_out[1], 16 * (TILES // 2))
            sp.wait_ge(made, 4)
            sp.dma_start(g["d_head"].rearrange("(p c) v -> p (c v)", c=EC), zeros[:, :]).then_inc(zeroed, 16)
            sp.wait_ge(zeroed, 16)

        @block.gpsimd
        def _(pool):
            own = Chain(pool, pool_own)
            own.link(nc.gpsimd.memset(ident[:, :], 0.0))
            nc.gpsimd.affine_select(out=ident[:, :], in_=ident[:, :], compare_op=ALU.not_equal, fill=1.0, base=0,
                                    pattern=[[-1, P]], channel_multiplier=1).then_inc(made, 1)
            nc.gpsimd.iota(iota[:, :], pattern=[[1, P]], base=0, channel_multiplier=0,
                           allow_small_or_imprecise_dtypes=True).then_inc(made, 1)
            own.link(nc.gpsimd.iota(iota_b[:, :], pattern=[[1, P]], base=0, channel_multiplier=0,
                                    allow_small_or_imprecise_dtypes=True))
            own.link(nc.gpsimd.memset(upper[:, :], 1.0))
            nc.gpsimd.affine_select(out=upper[:, :], in_=upper[:, :], compare_op=ALU.is_ge, fill=0.0, base=0,
                                    pattern=[[1, P]], channel_multiplier=-1).then_inc(made, 1)
            nc.gpsimd.memset(zeros[:, :], 0.0).then_inc(made, 1)
            pool.wait_ge(att_in, 32)
            pool.wait_ge(w_in, 16)
            with pool.Fori(0, KC) as i:
                for s in range(2):
                    pool.wait_ge(wprod_free, 2 * i + s + 1)
                    pool.sem_inc(pool_turn, 1)
                    nc.gpsimd.tensor_tensor(out=wprod[s][:, :], in0=w[:, bass.ds(i, 1), :].rearrange("p o n -> p (o n)"),
                                            in1=attb[:, s, :], op=ALU.mult).then_inc(wprod_ready, 1)

        @block.vector
        def _(dve):
            own = Chain(dve, dve_own)
            nc.vector.memset(dst1[:, :], NP - 1).then_inc(pads_set, 1)
            nc.vector.memset(src1[:, :], 0).then_inc(pads_set, 1)
            nc.vector.memset(ones[:, :], 1.0)
            nc.vector.sem_inc(xn_ready, SLOTS)
            nc.vector.sem_inc(wprod_free, SLOTS)
            dve.wait_ge(edges_in, 16 * 5)
            own.link(nc.vector.tensor_scalar(dlo_i[:, :], dst1[:, :], P - 1, None, ALU.bitwise_and))
            own.link(nc.vector.tensor_copy(dlo[:, :], dlo_i[:, :]))
            own.link(nc.vector.memset(dlo[:, EC:HPAD], 255.0))
            own.link(nc.vector.tensor_scalar(dlo_i[:, :], dst1[:, :], 7, None, ALU.logical_shift_right))
            own.link(nc.vector.tensor_copy(dhi[:, :], dlo_i[:, :]))
            dve.wait_ge(made, 4)
            nc.vector.tensor_tensor(
                out=hot_hi[:, :, :], in0=dhi[:, :].unsqueeze(2).to_broadcast([P, HPAD, 32]),
                in1=iota_b[:, 0:32].unsqueeze(1).to_broadcast([P, HPAD, 32]), op=ALU.is_equal).then_inc(hi_ready, 1)

            with dve.Fori(0, KC) as i:
                for s in range(2):
                    dve.wait_ge(wprod_ready, 2 * i + s + 1)
                    nc.vector.tensor_reduce(
                        out=wa[:, bass.ds(i, 1), s * HEADS:(s + 1) * HEADS].rearrange("p o h -> p (o h)"),
                        in_=wprod[s][:, :].rearrange("p (h c) -> p h c", c=C), axis=AX.X, op=ALU.add).then_inc(wprod_free, 1)

            def one_hot(b, j):
                dve.wait_ge(lo_free, b + 1)
                nc.vector.tensor_tensor(
                    out=hot_lo[j][:, :, :],
                    in0=dlo[:, bass.ds(b * HCOLS, HCOLS)].unsqueeze(2).to_broadcast([P, HCOLS, P]),
                    in1=iota_b[:, :].unsqueeze(1).to_broadcast([P, HCOLS, P]),
                    op=ALU.is_equal).then_inc(lo_ready, 1)

            def stat(t, j, n):
                dve.wait_ge(x_in[j], 16 * (n + 1))
                nc.vector.bn_stats(stats[:, 0, :], xt[j][:, 0:512])
                own.link(nc.vector.bn_stats(stats[:, 1, :], xt[j][:, 512:1024]))
                dve.sem_inc(dve_turn, 1)
                own.link(nc.vector.bn_aggr(mv[j][:, :], stats[:, :, :].rearrange("p a b -> p (a b)")))
                nc.vector.tensor_scalar(mv[j][:, 1:2], mv[j][:, 1:2], EPS, None, ALU.add).then_inc(var_ready, 1)

            def norm(t, j):
                dve.wait_ge(std_ready, t + 1)
                inverse_root(nc, own, std[j][:, :], mv[j][:, 1:2], rstd[j][:, :], newton[:, :])
                dve.wait_ge(tr_done, t + 1)
                nc.vector.tensor_scalar(xn[j][:, :], xt[j][:, :], mv[j][:, 0:1], rstd[j][:, :], ALU.subtract,
                                        ALU.mult).then_inc(xn_ready, 1)

            stat(0, 0, 0)
            with dve.Fori(0, TILES // 2) as i:
                back = own.enter(i, 2 * (STAT_LINKS + ROOT_LINKS))
                for j in range(2):
                    stat(2 * i + j + 1, 1 - j, i + j)
                    norm(2 * i + j, j)
                    one_hot(2 * i + j, j)
            own.leave(back, TILES // 2)
            norm(TILES - 1, 0)
            dve.wait_ge(wf_in, 16)
            for n, weight in enumerate((w, g["wf"])):
                nc.vector.tensor_reduce(out=g["largest"][:, n:n + 1], in_=weight[:, :, :].rearrange("p c n -> p (c n)"),
                                        axis=AX.X, op=ALU.max, apply_absolute_value=True)
            dve.wait_ge(lo_free, SLOTS + HBATCH)
            nc.vector.tensor_copy(count[:, :], hist_ps[:, 0:TILES])

        @block.scalar
        def _(act):
            def root(t, j):
                act.wait_ge(var_ready, t + 1)
                nc.scalar.activation(std[j][:, :], mv[j][:, 1:2], ACT.Sqrt).then_inc(std_ready, 1)

            def tile(t, j, n):
                act.wait_ge(tr_done, t + 1 + SLOTS)
                act.wait_ge(lg_done, t + 1)
                if n is not None:
                    act.wait_ge(xnT_out[j], n)
                nc.scalar.activation(xnT[j][:, :, :].rearrange("p c n -> p (c n)"), tr_ps[j][:, :],
                                     ACT.Copy).then_inc(xnT_ready, 1)

            def keep(t, j):
                act.wait_ge(lg_done, t + 1 + SLOTS)
                nc.scalar.activation(logits[:, bass.ds(t, 1), :].rearrange("p o v -> p (o v)"), lg_ps[j][:, 0:2 * HEADS],
                                     ACT.Copy).then_inc(lg_kept, 1)

            root(0, 0)
            root(1, 1)
            tile(0, 0, None)
            root(2, 0)
            tile(1, 1, None)
            keep(0, 0)
            with act.Fori(1, TILES // 2) as i:
                for j in range(2):
                    root(2 * i + j + 1, 1 - j)
                    tile(2 * i + j, j, 16 * i)
                    keep(2 * i + j - 1, 1 - j)
            tile(TILES - 1, 0, 16 * (TILES // 2))
            keep(TILES - 2, 1)
            keep(TILES - 1, 0)

        @block.tensor
        def _(pe):
            pe.sem_inc(tr_done, SLOTS)
            pe.sem_inc(lg_done, SLOTS)
            pe.sem_inc(lo_free, SLOTS)
            pe.wait_ge(made, 4)
            pe.wait_ge(hi_ready, 1)

            def tile(t, j):
                pe.wait_ge(xn_ready, t + 1 + SLOTS)
                for c in range(KC):
                    last = nc.tensor.transpose(tr_ps[j][:, c * P:(c + 1) * P], xn[j][:, c * P:(c + 1) * P], ident[:, :])
                last.then_inc(tr_done, 1)

            def logit(t, j):
                pe.wait_ge(xnT_ready, t + 1)
                for c in range(KC):
                    last = nc.tensor.matmul(lg_ps[j][:, 0:2 * HEADS], xnT[j][:, c, :], wa[:, c, :], start=(c == 0),
                                            stop=(c == KC - 1))
                last.then_inc(lg_done, 1)

            def counts(b, j, start, stop):
                pe.wait_ge(lo_ready, b + 1)
                for c in range(HCOLS):
                    last = nc.tensor.matmul(
                        hist_ps[:, 0:32], hot_lo[j][:, c, :],
                        hot_hi[:, bass.ds(b * HCOLS + c, 1), :].rearrange("p o v -> p (o v)"),
                        start=(start and c == 0), stop=(stop and c == HCOLS - 1))
                last.then_inc(lo_free, 1)

            def both(t, j, start=False, stop=False):
                tile(t, j)
                counts(t, j, start, stop)
                logit(t, j)

            pe.wait_ge(wprod_free, SLOTS + 2 * KC)
            both(0, 0, start=True)
            both(1, 1)
            with pe.Fori(1, TILES // 2 - 1) as i:
                for j in range(2):
                    t = 2 * i + j
                    pe.wait_ge(lg_kept, t - 1)
                    both(t, j)
            for t in range(TILES - 3, TILES - 1):
                pe.wait_ge(lg_kept, t - 1)
                both(t, t % 2, stop=(t == HBATCH - 1))
            pe.wait_ge(lg_kept, TILES - 2)
            tile(TILES - 1, 0)
            logit(TILES - 1, 0)


def project(nc, maker, g):
    ident, logits, self_num = g["ident"], g["logits"], g["self_num"]
    srcT, dstT, numT, tile_row, wdT = (g[k] for k in ("srcT", "dstT", "numT", "tile_row", "wdT"))
    w, dst1, src1, dfirst, count, ones, upper = (g[k] for k in ("w", "dst1", "src1", "dfirst", "count", "ones", "upper"))
    d_xnT, d_xp, d_asrc, d_node, d_src, d_dst = (g[k] for k in ("d_xnT", "d_xp", "d_asrc", "d_node", "d_src", "d_dst"))
    d_segmax, d_head, d_num, d_tile, ffn_w = (g[k] for k in ("d_segmax", "d_head", "d_num", "d_tile", "ffn_w"))
    d_own, wf, largest = g["d_own"], g["wf"], g["largest"]
    numT16, xp_scale, xp_inverse, wd_scale, wd_inverse = (
        g[k] for k in ("numT16", "xp_scale", "xp_inverse", "wd_scale", "wd_inverse"))
    CH = KCOLS // P
    ctx = ExitStack()
    with ctx:
        sb, ps, sem = maker(ctx)
        xnT = [sb(f"pxnT{j}", [P, KC, P]) for j in range(3)]
        xp = [sb(f"xp{j}", [P, 2, D], F16) for j in range(3)]
        own_row = [sb(f"xp_own{j}", [P, D]) for j in range(3)]
        wq = sb("wq", [P, D])
        step = sb("q_step", [P, D])
        scale = sb("q_scale", [P, QB])
        inv = sb("q_inv", [P, QB])
        most = sb("most", [2, 1])
        most_row = sb("most_row", [2, 2])
        low = sb("low", [P, 2])
        dstf = sb("dstf", [P, EC])
        srcf = sb("srcf", [P, EC])
        same = sb("same", [P, EC])
        fence = sb("fence", [P, EC])
        tmp = sb("tmp", [P, EC])
        idx = [sb(f"idx{j}", [P, GCOLS], I32) for j in range(GSLOTS)]
        got = [sb(f"got{j}", [P, GCOLS * HEADS]) for j in range(GSLOTS)]
        asrc = sb("asrc", [P, GCOLS * GFILLS, HEADS])
        segmax = sb("segmax", [P, EC, HEADS])
        tables, at = g["tables"], [EC * 2 * HEADS + n * CH * SUB * P for n in (0, 1, 2, 2 + HEADS)]
        head = tables[:, 0:at[0]].rearrange("p (c v) -> p c v", v=2 * HEADS)
        srow, drow, nrow = (tables[:, a:b].rearrange("p (c e) -> p c e", c=CH) for a, b in zip(at, at[1:]))
        first = sb("first", [P, 2 * HEADS])
        cinc = sb("cinc", [P, TILES])
        zero_t = sb("zero_t", [P, TILES])
        startf = sb("startf", [P, TILES])
        lastf = sb("lastf", [P, TILES])
        has = sb("has", [P, TILES])
        start_i = sb("start_i", [P, TILES], I32)
        last_i = sb("last_i", [P, TILES], I32)
        node = sb("node", [P, TILES, 2 * HEADS])
        nmax = sb("nmax", [P, TILES, HEADS])
        nself = sb("nself", [P, TILES, HEADS])
        tf_i = sb("tf_i", [1, ET], I32)
        tf = sb("tf", [1, ET])
        irow = sb("irow", [1, ET])
        kcol = sb("kcol", [P, CH])
        etile = sb("etile", [P, CH])
        ntile = sb("ntile", [P, CH])
        ntile128 = sb("ntile128", [P, CH])
        step_i = sb("step_i", [P, CH], I32)
        ntile_i = sb("ntile_i", [P, CH], I32)
        far = segmax[:, :, :].rearrange("p c h -> p (c h)")[:, 0:SUB * KCOLS]
        ends = sb("ends", [P, 3, HEADS])
        erow = sb("erow", [HEADS, 3, P])
        whole = sb("whole_run", [HEADS, P])
        joins = sb("joins", [HEADS, P])
        carry = sb("carry", [HEADS, P])
        cin = sb("cin", [HEADS, P])
        cinT = sb("cinT", [P, HEADS])
        xp_ps = [ps(f"xp_ps{j}", [P, D]) for j in range(3)]
        g_ps = ps("g_ps", [P, D])

        asrc_out = sem("asrc_out")
        flat_ready = sem("flat_ready")
        flat_out = sem("flat_out")
        iotas = sem("iotas")
        idx_ready = sem("idx_ready")
        gathered = [sem(f"gathered{j}") for j in range(GSLOTS)]
        xnT_in = [sem(f"pxnT_in{j}") for j in range(3)]
        xp_done = sem("xp_done")
        xp_kept = sem("xp_kept")
        xp_out = [sem(f"xp_out{j}") for j in range(3)]
        most_ready = sem("most_ready")
        most_turned = sem("most_turned")
        most_row_ready = sem("most_row_ready")
        most_spread = sem("most_spread")
        powers_ready = sem("powers_ready")
        xp_low = sem("xp_low")
        wd_high = sem("wd_high")
        num_high = sem("num_high")
        num_low = sem("num_low")
        wq_ready = sem("wq_ready")
        wtr_done = sem("wtr_done")
        wtr_kept = sem("wtr_kept")
        cexc_ready = sem("cexc_ready")
        cum_done = sem("cum_done")
        tf_ready = sem("tf_ready")
        stair_done = sem("stair_done")
        plan_read = sem("plan_read")
        plan_ready = sem("plan_ready")
        tile_out = sem("tile_out")
        ends_ready = sem("ends_ready")
        erow_done = sem("erow_done")
        cin_ready = sem("cin_ready")
        cinT_done = sem("cinT_done")
        segmax_ready = sem("segmax_ready")
        segmax_out = sem("segmax_out")
        nmax_in = sem("nmax_in")
        node_ready = sem("node_ready")
        node_out = sem("node_out")
        scattered = sem("scattered")
        first_in = sem("first_in")
        head_in = sem("head_in")
        nself_ready = sem("nself_ready")
        self_kept = sem("self_kept")
        logit_ready = sem("logit_ready")
        num_ready = sem("num_ready")
        num_out = sem("num_out")
        rows_in = sem("rows_in")
        rows_ready = sem("rows_ready")
        steps_done = sem("steps_done")
        dve_own = sem("dve_own2")
        pool_turn = sem("pool_turn2")
        block = ctx.enter_context(nc.Block())
        lines = lambda d: d.rearrange("i e -> (i e)").rearrange("(p c) -> p c", c=EC)

        @block.sync
        def _(sp):
            def load(t, j):
                sp.wait_ge(xp_done, t + 1)
                sp.dma_start(xnT[j][:, :, :].rearrange("p c n -> p (c n)"),
                             d_xnT[bass.ds(t, 1), :, :].rearrange("o p n -> (o p) n")).then_inc(xnT_in[j], 16)

            def store(t, j):
                sp.wait_ge(xp_low, t + 1 + 3)
                sp.dma_start(d_xp[bass.ds(t * P, P), :], xp[j][:, :, :].rearrange("p a n -> p (a n)")).then_inc(xp_out[j], 16)
                sp.dma_start(d_own[bass.ds(t * P, P), :], own_row[j][:, :]).then_inc(xp_out[j], 16)

            for t in range(3):
                load(t, t)
            with sp.Fori(0, KC - 1) as i:
                for j in range(3):
                    load(3 * i + j + 3, j)
                    store(3 * i + j, j)
            load(TILES - 1, 0)
            for t in range(TILES - 4, TILES):
                store(t, t % 3)
            for j in range(3):
                sp.wait_ge(xp_out[j], 32 * len(range(j, TILES, 3)))

        @block.gpsimd
        def _(pool):
            def gather(out, table, index, signal):
                nc.gpsimd.indirect_dma_start(
                    out=out, out_offset=None, in_=table,
                    in_offset=bass.IndirectOffsetOnAxis(ap=index, axis=0)).then_inc(signal, 16)

            nc.gpsimd.dma_start(d_asrc.rearrange("(t p) h -> p t h", p=P), logits[:, :, 0:HEADS]).then_inc(asrc_out, 16)
            nc.gpsimd.iota(irow[:, :], pattern=[[1, ET]], base=0, channel_multiplier=0,
                           allow_small_or_imprecise_dtypes=True).then_inc(iotas, 1)
            nc.gpsimd.iota(kcol[:, :], pattern=[[P, CH]], base=0, channel_multiplier=1,
                           allow_small_or_imprecise_dtypes=True).then_inc(iotas, 1)
            pool.wait_ge(asrc_out, 16)
            with pool.Fori(0, GFILLS // GSLOTS) as i:
                for s in range(GSLOTS):
                    pool.wait_ge(idx_ready, i * GSLOTS + s + 1)
                    pool.sem_inc(pool_turn, 1)
                    for c in range(GCOLS):
                        gather(got[s][:, c * HEADS:(c + 1) * HEADS], d_asrc, idx[s][:, c:c + 1], gathered[s])
            pool.wait_ge(flat_ready, 1)
            nc.gpsimd.dma_start(lines(d_dst), dstf[:, :]).then_inc(flat_out, 16)
            nc.gpsimd.dma_start(lines(d_src), srcf[:, :]).then_inc(flat_out, 16)
            pool.wait_ge(plan_ready, 1)
            nc.gpsimd.dma_start(d_tile.rearrange("(c p) -> p c", p=P), ntile_i[:, :],
                                allow_slow_non_contiguous=True).then_inc(tile_out, 16)
            pool.wait_ge(flat_out, 32)
            for c in range(CH):
                gather(srow[:, c, :], d_src, step_i[:, c:c + 1], rows_in)
                gather(drow[:, c, :], d_dst, step_i[:, c:c + 1], rows_in)
            pool.wait_ge(tile_out, 16)
            nc.gpsimd.dma_start(tile_row[:, :], d_tile.unsqueeze(0)).then_inc(tile_out, 16)
            pool.wait_ge(segmax_ready, 1)
            nc.gpsimd.dma_start(d_segmax.rearrange("(p c) h -> p (c h)", c=EC),
                                segmax[:, :, :].rearrange("p c h -> p (c h)")).then_inc(segmax_out, 16)
            pool.wait_ge(segmax_out, 16)
            for t in range(TILES):
                gather(nmax[:, t, :], d_segmax, last_i[:, t:t + 1], nmax_in)
            pool.wait_ge(node_ready, 1)
            nc.gpsimd.dma_start(d_node.rearrange("(t p) v -> p t v", p=P), node[:, :, :]).then_inc(node_out, 16)
            for t in range(TILES):
                nc.gpsimd.indirect_dma_start(
                    out=d_head, out_offset=bass.IndirectOffsetOnAxis(ap=start_i[:, t:t + 1], axis=0),
                    in_=node[:, t, :], in_offset=None, bounds_check=EP - 1, oob_is_err=False).then_inc(scattered, 16)
            pool.wait_ge(node_out, 16)
            gather(first[:, :], d_node, dst1[:, 0:1], first_in)
            pool.wait_ge(scattered, 16 * TILES)
            nc.gpsimd.dma_start(head[:, :, :].rearrange("p c v -> p (c v)"),
                                d_head.rearrange("(p c) v -> p (c v)", c=EC)).then_inc(head_in, 16)
            pool.wait_ge(num_ready, 1)
            nc.gpsimd.dma_start(d_num.rearrange("i e -> (i e)").rearrange("(p c) -> p c", c=EC * HEADS),
                                segmax[:, :, :].rearrange("p c h -> p (c h)")).then_inc(num_out, 16)
            pool.wait_ge(num_out, 16)
            for c in range(CH):
                gather(nrow[:, c, :], d_num, step_i[:, c:c + 1], rows_in)
            pool.wait_ge(tile_out, 32)

        @block.vector
        def _(dve):
            own = Chain(dve, dve_own)

            def fill(s, column):
                nc.vector.tensor_copy(idx[s][:, :], src1[:, bass.ds(column, GCOLS)]).then_inc(idx_ready, 1)

            nc.vector.sem_inc(xp_low, 3)
            for s in range(GSLOTS):
                fill(s, s * GCOLS)
            dve.wait_ge(most_turned, 1)
            own.link(nc.vector.tensor_reduce(out=most[:, :], in_=g_ps[0:2, 2 * P:3 * P], axis=AX.X, op=ALU.max))
            nc.vector.tensor_scalar(most_row[:, :], ident[0:2, 0:2], most[:, :], None, ALU.mult).then_inc(most_row_ready, 1)
            dve.wait_ge(most_spread, 1)
            power_scale(nc, own, g_ps[:, 2 * P:2 * P + 1], low[:, 0:1], xp_scale[:, :], xp_inverse[:, :], 4)
            power_scale(nc, own, g_ps[:, 2 * P + 1:2 * P + 2], low[:, 1:2], wd_scale[:, :], wd_inverse[:, :], 13)
            nc.vector.sem_inc(powers_ready, 1)
            nc.vector.memset(zero_t[:, :], 0.0)
            nc.vector.tensor_copy(dstf[:, :], dst1[:, 0:EC])
            own.link(nc.vector.tensor_copy(srcf[:, :], src1[:, 0:EC]))
            nc.vector.sem_inc(flat_ready, 1)
            own.link(nc.vector.tensor_tensor_scan(cinc[:, :], count[:, :], zero_t[:, :], 0.0, ALU.add, ALU.add))
            nc.vector.tensor_tensor(out=cinc[:, :], in0=cinc[:, :], in1=count[:, :], op=ALU.subtract).then_inc(cexc_ready, 1)
            own.link(nc.vector.tensor_scalar(tf_i[:, :], dfirst[:, :], 7, None, ALU.logical_shift_right))
            own.link(nc.vector.tensor_copy(tf[:, :], tf_i[:, :]))
            dve.wait_ge(iotas, 2)
            nc.vector.tensor_tensor(out=tf[:, :], in0=tf[:, :], in1=irow[:, :], op=ALU.add).then_inc(tf_ready, 1)
            dve.wait_ge(cum_done, 1)
            own.link(nc.vector.tensor_scalar(has[:, :], count[:, :], 0.0, None, ALU.is_gt))
            own.link(nc.vector.tensor_tensor(out=startf[:, :], in0=g_ps[:, 0:TILES], in1=count[:, :], op=ALU.subtract))
            own.link(nc.vector.scalar_tensor_tensor(out=startf[:, :], in0=has[:, :], scalar=-float(2 * EP), in1=startf[:, :],
                                                    op0=ALU.mult, op1=ALU.add))
            own.link(nc.vector.tensor_scalar(startf[:, :], startf[:, :], float(2 * EP), None, ALU.add))
            own.link(nc.vector.tensor_scalar(lastf[:, :], g_ps[:, 0:TILES], -1.0, 0.0, ALU.add, ALU.max))
            nc.vector.tensor_copy(start_i[:, :], startf[:, :])
            own.link(nc.vector.tensor_copy(last_i[:, :], lastf[:, :]))
            own.link(nc.vector.tensor_scalar(has[:, :], has[:, :], -1.0, BIG, ALU.add, ALU.mult))
            dve.wait_ge(stair_done, 1)
            for c in range(CH):
                own.link(nc.vector.tensor_scalar(tmp[:, 0:ET], g_ps[:, 512:512 + ET], kcol[:, c:c + 1], None, ALU.is_le))
                own.link(nc.vector.tensor_reduce(out=etile[:, c:c + 1], in_=tmp[:, 0:ET], axis=AX.X, op=ALU.add))
            nc.vector.sem_inc(plan_read, 1)
            own.link(nc.vector.tensor_scalar(etile[:, :], etile[:, :], -1.0, 0.0, ALU.add, ALU.max))
            own.link(nc.vector.tensor_tensor(out=ntile[:, :], in0=kcol[:, :], in1=etile[:, :], op=ALU.subtract))
            nc.vector.tensor_scalar(ntile128[:, :], ntile[:, :], float(P), None, ALU.mult)
            own.link(nc.vector.tensor_scalar(ntile[:, :], ntile[:, :], float(TILES - 1), None, ALU.min))
            nc.vector.tensor_copy(step_i[:, :], etile[:, :])
            own.link(nc.vector.tensor_copy(ntile_i[:, :], ntile[:, :]))
            nc.vector.sem_inc(plan_ready, 1)
            nc.vector.memset(same[:, 0:1], 0.0)
            own.link(nc.vector.tensor_tensor(out=same[:, 1:EC], in0=dstf[:, 1:EC], in1=dstf[:, 0:EC - 1], op=ALU.is_equal))
            own.link(nc.vector.tensor_scalar(fence[:, :], same[:, :], -1.0, BIG, ALU.add, ALU.mult))
            own.link(nc.vector.memset(fence[:, 0:1], 0.0))

            rounds = GFILLS // KC

            def split(t, j):
                dve.wait_ge(xp_kept, t + 1 + 3)
                nc.vector.scalar_tensor_tensor(out=xp[j][:, 1, :], in0=xp_ps[j][:, :], scalar=xp_scale[:, :],
                                               in1=xp[j][:, 0, :], op0=ALU.mult, op1=ALU.subtract).then_inc(xp_low, 1)

            with dve.Fori(0, KC) as o:
                back = own.enter(o, SCALE_LINKS + 2 + ROUND_LINKS)
                row = wf[:, bass.ds(o, 1), :].rearrange("p o n -> p (o n)")
                own.link(block_scales(nc, own, row, scale[:, :], inv[:, :]))
                dve.wait_ge(wtr_done, o + 1)
                own.link(nc.vector.tensor_tensor(out=blocks(wq[:, :]), in0=blocks(row), in1=spread(inv[:, :]), op=ALU.mult))
                round_to_grid(nc, own, wq[:, :], step[:, :], scale[:, :], wq[:, :]).then_inc(wq_ready, 1)
                for f in range(rounds):
                    s = f % GSLOTS
                    dve.wait_ge(gathered[s], 16 * GCOLS * (o * (rounds // GSLOTS) + f // GSLOTS + 1))
                    nc.vector.tensor_copy(
                        asrc[:, bass.ds((o * rounds + f) * GCOLS, GCOLS), :].rearrange("p c h -> p (c h)"), got[s][:, :])
                    fill(s, (o * rounds + f + GSLOTS) * GCOLS)
                    if f % 3 == 2:
                        split(3 * o + f // 3, f // 3)
                dve.wait_ge(wd_high, o + 1)
                cols = bass.ds(o * P, P)
                nc.vector.scalar_tensor_tensor(
                    out=wdT[:, :, 1, cols], in0=g_ps[:, :].rearrange("p (c n) -> p c n", n=P), scalar=wd_scale[:, :],
                    in1=wdT[:, :, 0, cols], op0=ALU.mult, op1=ALU.subtract).then_inc(wtr_kept, 1)
            own.leave(back, KC)
            split(TILES - 1, 0)
            dve.wait_ge(xp_low, TILES + 3)

            for h in range(HEADS):
                last = nc.vector.tensor_tensor_scan(segmax[:, :, h], fence[:, :], asrc[:, 0:EC, h], -BIG, ALU.add, ALU.max)
            own.link(last)
            nc.vector.tensor_copy(ends[:, 0, :], segmax[:, EC - 1, :])
            nc.vector.tensor_copy(ends[:, 1, :], dstf[:, 0:1].to_broadcast([P, HEADS]))
            nc.vector.tensor_copy(ends[:, 2, :], dstf[:, EC - 1:EC].to_broadcast([P, HEADS])).then_inc(ends_ready, 1)
            dve.wait_ge(erow_done, 1)
            own.link(nc.vector.tensor_copy(erow[:, :, :].rearrange("h a p -> h (a p)"), g_ps[0:HEADS, 0:3 * P]))
            nc.vector.memset(joins[:, 0:1], 0.0)
            own.link(nc.vector.tensor_tensor(out=joins[:, 1:P], in0=erow[:, 1, 1:P], in1=erow[:, 2, 0:P - 1], op=ALU.is_equal))
            own.link(nc.vector.tensor_tensor(out=whole[:, :], in0=erow[:, 1, :], in1=erow[:, 2, :], op=ALU.is_equal))
            own.link(nc.vector.tensor_tensor(out=whole[:, :], in0=whole[:, :], in1=joins[:, :], op=ALU.mult))
            own.link(nc.vector.tensor_scalar(whole[:, :], whole[:, :], -1.0, BIG, ALU.add, ALU.mult))
            own.link(nc.vector.tensor_scalar(joins[:, :], joins[:, :], -1.0, BIG, ALU.add, ALU.mult))
            own.link(nc.vector.tensor_tensor_scan(carry[:, :], whole[:, :], erow[:, 0, :], -BIG, ALU.add, ALU.max))
            own.link(nc.vector.memset(cin[:, 0:1], -BIG))
            nc.vector.tensor_tensor(out=cin[:, 1:P], in0=carry[:, 0:P - 1], in1=joins[:, 1:P], op=ALU.add).then_inc(cin_ready, 1)
            dve.wait_ge(cinT_done, 1)
            own.link(nc.vector.tensor_copy(cinT[:, :], g_ps[:, 512:512 + HEADS]))
            for h in range(HEADS):
                last = nc.vector.tensor_tensor_scan(segmax[:, :, h], fence[:, :], asrc[:, 0:EC, h], cinT[:, h:h + 1],
                                                    ALU.add, ALU.max)
            last.then_inc(segmax_ready, 1)
            nself_v, node_src, node_dst = nself[:, :, :], logits[:, :, 0:HEADS], logits[:, :, HEADS:2 * HEADS]
            own.link(nc.vector.tensor_tensor(out=nself_v, in0=node_src, in1=node_dst, op=ALU.add))
            own.link(nc.vector.scalar_tensor_tensor(out=nself_v, in0=nself_v, scalar=SLOPE, in1=nself_v, op0=ALU.mult, op1=ALU.max))
            nc.vector.tensor_copy(node[:, :, 0:HEADS], node_dst)
            dve.wait_ge(nmax_in, 16 * TILES)
            own.link(nc.vector.tensor_tensor(out=nmax[:, :, :], in0=nmax[:, :, :],
                                             in1=has[:, :].unsqueeze(2).to_broadcast([P, TILES, HEADS]), op=ALU.add))
            own.link(nc.vector.tensor_tensor(out=nmax[:, :, :], in0=nmax[:, :, :], in1=node_src, op=ALU.max))
            own.link(nc.vector.tensor_tensor(out=nmax[:, :, :], in0=nmax[:, :, :], in1=node_dst, op=ALU.add))
            own.link(nc.vector.scalar_tensor_tensor(out=node[:, :, HEADS:2 * HEADS], in0=nmax[:, :, :], scalar=SLOPE,
                                                    in1=nmax[:, :, :], op0=ALU.mult, op1=ALU.max))
            nc.vector.sem_inc(node_ready, 1)
            nc.vector.tensor_tensor(out=nself_v, in0=nself_v, in1=node[:, :, HEADS:2 * HEADS],
                                    op=ALU.subtract).then_inc(nself_ready, 1)
            dve.wait_ge(first_in, 16)
            dve.wait_ge(head_in, 16)
            own.link(nc.vector.tensor_copy(head[:, 0, :], first[:, :]))
            for v in range(2 * HEADS):
                last = nc.vector.tensor_tensor_scan(head[:, :, v], same[:, :], head[:, :, v], 0.0, ALU.mult, ALU.add)
            own.link(last)
            edge = asrc[:, 0:EC, :]
            own.link(nc.vector.tensor_tensor(out=edge, in0=edge, in1=head[:, :, 0:HEADS], op=ALU.add))
            own.link(nc.vector.scalar_tensor_tensor(out=edge, in0=edge, scalar=SLOPE, in1=edge, op0=ALU.mult, op1=ALU.max))
            nc.vector.tensor_tensor(out=edge, in0=edge, in1=head[:, :, HEADS:2 * HEADS], op=ALU.subtract).then_inc(logit_ready, 1)
            dve.wait_ge(rows_in, 16 * 3 * CH)
            for c in range(CH):
                last = nc.vector.tensor_scalar(drow[:, c, :], drow[:, c, :], ntile128[:, c:c + 1], None, ALU.subtract)
            last.then_inc(rows_ready, 1)
            dve.wait_ge(steps_done, 1)
            own.link(nc.vector.tensor_copy(dstT, xp_ps[0][:, SUB * KCOLS:2 * SUB * KCOLS]))
            own.link(nc.vector.scalar_tensor_tensor(out=far, in0=dstT, scalar=-float(P - 1), in1=dstT, op0=ALU.add, op1=ALU.mult))
            own.link(nc.vector.tensor_scalar(far, far, 0.0, float(FAR), ALU.is_gt, ALU.mult))
            nc.vector.tensor_tensor(out=srcT, in0=xp_ps[0][:, 0:SUB * KCOLS], in1=far, op=ALU.add)
            by_head = lambda v, b: numT16[:, :, v:v + HEADS, b].rearrange("p k h -> p h k")
            dve.wait_ge(num_high, 1)
            own.link(nc.vector.tensor_copy(by_head(0, 0), numT[:, :, :]))
            nc.vector.tensor_tensor(out=by_head(HEADS, 0), in0=numT[:, :, :], in1=by_head(0, 0),
                                    op=ALU.subtract).then_inc(num_low, 1)

        @block.scalar
        def _(act):
            act.sem_inc(xp_kept, 3)

            def keep(t, j, n):
                act.wait_ge(xp_done, t + 1 + 3)
                if n is not None:
                    act.wait_ge(xp_out[j], n)
                nc.scalar.activation(own_row[j][:, :], xp_ps[j][:, :], ACT.Copy)
                nc.scalar.activation(xp[j][:, 0, :], xp_ps[j][:, :], ACT.Copy, scale=xp_scale[:, :]).then_inc(xp_kept, 1)

            def keep_w(o):
                act.wait_ge(wtr_done, o + 1 + 1)
                nc.scalar.activation(wdT[:, :, 0, bass.ds(o * P, P)], g_ps[:, :].rearrange("p (c n) -> p c n", n=P),
                                     ACT.Copy, scale=wd_scale[:, :]).then_inc(wd_high, 1)

            act.wait_ge(powers_ready, 1)
            for t in range(3):
                keep(t, t, None)
            keep_w(0)
            with act.Fori(1, KC) as i:
                for j in range(3):
                    keep(3 * i + j, j, 32 * i)
                keep_w(i)
            keep(TILES - 1, 0, 32 * KC)
            act.wait_ge(nself_ready, 1)
            nc.scalar.activation(self_num[:, :, :], nself[:, :, :], ACT.Exp)
            act.wait_ge(segmax_out, 16)
            act.wait_ge(logit_ready, 1)
            nc.scalar.activation(segmax[:, :, :], asrc[:, 0:EC, :], ACT.Exp).then_inc(num_ready, 1)
            act.wait_ge(steps_done, 1)
            for h in range(HEADS):
                half = slice((h % 2) * SUB * KCOLS, (h % 2 + 1) * SUB * KCOLS)
                last = nc.scalar.activation(numT[:, h, :], xp_ps[1 + h // 2][:, half], ACT.Copy, scale=NUM_SCALE)
            last.then_inc(num_high, 1)
            act.wait_ge(num_low, 1)
            nc.scalar.activation(numT[:, :, :], numT16[:, :, 0:HEADS, 0].rearrange("p k h -> p h k"), ACT.Copy)
            nc.scalar.activation(numT16[:, :, HEADS:2 * HEADS, 1], numT16[:, :, HEADS:2 * HEADS, 0], ACT.Copy)

        @block.tensor
        def _(pe):
            pe.sem_inc(xp_done, 3)
            pe.sem_inc(wtr_done, 1)
            pe.sem_inc(wtr_kept, 1)
            nc.tensor.transpose(g_ps[0:2, 2 * P:3 * P], largest[:, :], ident[:, :]).then_inc(most_turned, 1)
            pe.wait_ge(most_row_ready, 1)
            nc.tensor.matmul(g_ps[:, 2 * P:2 * P + 2], ones[0:2, :], most_row[:, :], start=True, stop=True).then_inc(most_spread, 1)
            pe.wait_ge(cexc_ready, 1)
            nc.tensor.matmul(g_ps[:, 0:TILES], upper[:, :], count[:, :], start=True, stop=False)
            nc.tensor.matmul(g_ps[:, 0:TILES], ones[:, :], cinc[:, :], start=False, stop=True).then_inc(cum_done, 1)
            pe.wait_ge(tf_ready, 1)
            nc.tensor.matmul(g_ps[:, 512:512 + ET], ones[0:1, :], tf[:, :], start=True, stop=True).then_inc(stair_done, 1)

            def tile(t, j, n):
                pe.wait_ge(xnT_in[j], n)
                pe.wait_ge(xp_low, t + 1)
                for c in range(KC):
                    for half in range(2):
                        last = nc.tensor.matmul(xp_ps[j][:, half * 512:(half + 1) * 512], xnT[j][:, c, :],
                                                w[:, c, half * 512:(half + 1) * 512], start=(c == 0), stop=(c == KC - 1))
                last.then_inc(xp_done, 1)

            pe_tiles = 3
            with pe.Fori(0, KC) as i:
                for j in range(pe_tiles):
                    tile(pe_tiles * i + j, j, 16 * (i + 1))
                pe.wait_ge(plan_read, 1)
                pe.wait_ge(wq_ready, i + 1)
                pe.wait_ge(wtr_kept, i + 1)
                for c in range(KC):
                    last = nc.tensor.transpose(g_ps[:, c * P:(c + 1) * P], wq[:, c * P:(c + 1) * P], ident[:, :])
                last.then_inc(wtr_done, 1)
            tile(TILES - 1, 0, 16 * (KC + 1))

            pe.wait_ge(ends_ready, 1)
            pe.wait_ge(wtr_kept, KC + 1)
            for a in range(3):
                last = nc.tensor.transpose(g_ps[0:HEADS, a * P:(a + 1) * P], ends[:, a, :], ident[:, :])
            last.then_inc(erow_done, 1)
            pe.wait_ge(cin_ready, 1)
            nc.tensor.transpose(g_ps[:, 512:512 + HEADS], cin[:, :], ident[0:HEADS, 0:HEADS]).then_inc(cinT_done, 1)
            pe.wait_ge(rows_ready, 1)
            pe.wait_ge(xp_low, TILES + 3)
            for c in range(CH):
                for u in range(SUB):
                    sub = slice(u * P, (u + 1) * P)
                    at = u * KCOLS + c * P
                    nc.tensor.transpose(xp_ps[0][:, at:at + P], srow[:, c, sub], ident[:, :])
                    nc.tensor.transpose(xp_ps[0][:, SUB * KCOLS + at:SUB * KCOLS + at + P], drow[:, c, sub], ident[:, :])
                    for h in range(HEADS):
                        to = (h % 2) * SUB * KCOLS + at
                        last = nc.tensor.transpose(
                            xp_ps[1 + h // 2][:, to:to + P],
                            nrow[:, c, :].rearrange("p (e h) -> p e h", h=HEADS)[:, sub, h], ident[:, :])
            last.then_inc(steps_done, 1)


def aggregate(nc, maker, g):
    tables, srcT, dstT, numT, numT16, tile_row, acc, zsum, d_xp = (
        g[k] for k in ("tables", "srcT", "dstT", "numT", "numT16", "tile_row", "acc", "zsum", "d_xp"))
    TURN = 4
    V = 2 * HEADS
    ctx = ExitStack()
    with ctx:
        sb, ps, sem = maker(ctx)
        iota16 = sb("iota16", [P, P], F16)
        idx = [sb(f"sidx{j}", [P, SUB], I32) for j in range(TURN)]
        xg = [[sb(f"xg{j}_{u}", [P, 2, D], F16) for u in range(SUB)] for j in range(TURN)]
        hot = [[sb(f"hot{j}_{u}", [P, P], F16) for u in range(SUB)] for j in range(TURN)]
        wgt = [[sb(f"wgt{j}_{u}", [P, V, P], F16) for u in range(SUB)] for j in range(2)]
        sum_ps = [ps(f"sum_ps{j}", [P, D]) for j in range(2)]
        z_ps = [ps(f"z_ps{j}", [P, 512]) for j in range(2)]

        iota_made = sem("iota_made")
        cleared = sem("cleared")
        idx_ready = sem("sidx_ready")
        arrived = [sem(f"arrived{j}") for j in range(TURN)]
        hot_ready = sem("hot_ready")
        low_ready = sem("low_ready")
        high_ready = sem("high_ready")
        mm_done = sem("mm_done")
        added = sem("added")
        pool_turn = sem("pool_turn3")
        block = ctx.enter_context(nc.Block())
        flat = acc[:, :, :].rearrange("p t n -> p (t n)")
        cut = TILES * D // 2
        col = lambda table, u, k, n=1: table.rearrange("p (u k) -> p u k", u=SUB)[:, u, bass.ds(k, n)]

        @block.gpsimd
        def _(pool):
            def gather(s):
                for u in range(SUB):
                    nc.gpsimd.indirect_dma_start(
                        out=xg[s][u][:, :, :].rearrange("p a n -> p (a n)"), out_offset=None, in_=d_xp,
                        in_offset=bass.IndirectOffsetOnAxis(ap=idx[s][:, u:u + 1], axis=0),
                        bounds_check=NP - 1, oob_is_err=False).then_inc(arrived[s], 16)

            def refill(k, s):
                pool.wait_ge(idx_ready, k + 1)
                pool.wait_ge(mm_done, SUB * (k + 1))
                pool.sem_inc(pool_turn, 1)
                gather(s)

            nc.gpsimd.iota(iota16[:, :], pattern=[[1, P]], base=0, channel_multiplier=0,
                           allow_small_or_imprecise_dtypes=True).then_inc(iota_made, 1)
            pool.wait_ge(idx_ready, TURN)
            for s in range(TURN):
                gather(s)
            nc.gpsimd.memset(flat[:, cut:], 0.0).then_inc(cleared, 1)
            with pool.Fori(1, STEPS // TURN) as i:
                for j in range(TURN):
                    refill(TURN * i + j, j)

        @block.vector
        def _(dve):
            def indices(k):
                return srcT.rearrange("p (u k) -> p u k", u=SUB)[:, :, bass.ds(k, 1)].rearrange("p u o -> p (u o)")

            def one_hots(k, j):
                dve.wait_ge(mm_done, SUB * (k + 1))
                for u in range(SUB):
                    nc.vector.tensor_scalar(hot[j][u][:, :], iota16[:, :], col(dstT, u, k), None,
                                            ALU.is_equal).then_inc(hot_ready, 1)

            def weights(k, j, s):
                for u in range(SUB):
                    dve.wait_ge(hot_ready, SUB * k + u + 1)
                    dve.wait_ge(mm_done, SUB * (k + 2) + u + 1)
                    nc.vector.tensor_tensor(
                        out=wgt[s][u][:, HEADS:V, :].rearrange("p v (n b) -> p v n b", b=2),
                        in0=hot[j][u][:, :].rearrange("p (n b) -> p n b", b=2).unsqueeze(1).to_broadcast([P, HEADS, P // 2, 2]),
                        in1=numT16[:, bass.ds(u * KCOLS + k, 1), HEADS:V, :].rearrange("p o v b -> p (o v) b").unsqueeze(2)
                        .to_broadcast([P, HEADS, P // 2, 2]), op=ALU.mult).then_inc(low_ready, 1)

            for k in range(TURN):
                nc.vector.tensor_scalar(idx[k][:, :], indices(k), NP - 1, None, ALU.min).then_inc(idx_ready, 1)
            dve.wait_ge(iota_made, 1)
            one_hots(0, 0)
            one_hots(1, 1)
            weights(0, 0, 0)
            nc.vector.memset(flat[:, 0:cut], 0.0)
            nc.vector.memset(zsum[:, :, :], 0.0).then_inc(cleared, 1)
            dve.wait_ge(cleared, 2)
            with dve.Fori(0, STEPS // TURN) as i:
                for j in range(TURN):
                    k = TURN * i + j
                    one_hots(k + 2, (j + 2) % TURN)
                    weights(k + 1, (j + 1) % TURN, (j + 1) % 2)
                    t = dve.value_load(tile_row[0:1, bass.ds(k, 1)], min_val=0, max_val=TILES - 1)
                    dve.wait_ge(mm_done, SUB * (k + 1 + TURN))
                    nc.vector.tensor_copy(idx[j][:, :], indices(k + TURN)).then_inc(idx_ready, 1)
                    dve.wait_ge(added, k + 2)
                    s_acc = acc[:, bass.ds(t, 1), :].rearrange("p o n -> p (o n)")
                    z_acc = zsum[:, bass.ds(t, 1), :].rearrange("p o n -> p (o n)")
                    nc.vector.tensor_tensor(out=z_acc, in0=z_ps[j % 2][:, 0:V], in1=z_acc, op=ALU.add)
                    nc.vector.tensor_tensor(out=s_acc, in0=sum_ps[j % 2][:, :], in1=s_acc, op=ALU.add).then_inc(added, 1)

        @block.scalar
        def _(act):
            with act.Fori(0, STEPS // TURN) as i:
                for j in range(TURN):
                    k = TURN * i + j
                    for u in range(SUB):
                        act.wait_ge(hot_ready, SUB * k + u + 1)
                        act.wait_ge(mm_done, SUB * (k + 2) + u + 1)
                        for h in range(HEADS):
                            last = nc.scalar.activation(wgt[j % 2][u][:, h, :], hot[j][u][:, :], ACT.Copy,
                                                        scale=col(numT[:, h, :], u, k))
                        last.then_inc(high_ready, 1)

        @block.tensor
        def _(pe):
            pe.sem_inc(mm_done, SUB * TURN)
            pe.sem_inc(added, 2)
            with pe.Fori(0, STEPS // TURN) as i:
                for j in range(TURN):
                    k, s = TURN * i + j, j % 2
                    pe.wait_ge(arrived[j], 16 * SUB * (i + 1))
                    pe.wait_ge(added, k + 1)
                    for u in range(SUB):
                        pe.wait_ge(high_ready, SUB * k + u + 1)
                        pe.wait_ge(low_ready, SUB * k + u + 1)
                        nc.tensor.matmul(z_ps[s][:, 0:V], hot[j][u][:, :],
                                         numT16[:, bass.ds(u * KCOLS + k, 1), :, 0].rearrange("p o v -> p (o v)"),
                                         start=(u == 0), stop=(u == SUB - 1))
                        for h in range(HEADS):
                            for n, (a, b) in enumerate(((0, 0), (0, 1), (1, 0))):
                                last = nc.tensor.matmul(
                                    sum_ps[s][:, h * C:(h + 1) * C], wgt[s][u][:, a * HEADS + h, :],
                                    xg[j][u][:, b, h * C:(h + 1) * C],
                                    start=(u == 0 and h % 2 == 0 and n == 0), stop=(u == SUB - 1 and h % 2 == 1 and n == 2),
                                    skip_group_check=True)
                        last.then_inc(mm_done, 1)


def finish(nc, maker, g):
    x, gnn_bias, ffn_bias, out, d_own = (g[k] for k in ("x", "gnn_bias", "ffn_bias", "out", "d_own"))
    ident, self_num, wdT, acc, zsum, tables = (g[k] for k in ("ident", "self_num", "wdT", "acc", "zsum", "tables"))
    xp_inverse, wd_inverse = g["xp_inverse"], g["wd_inverse"]
    LAST = TILES - 1
    ctx = ExitStack()
    with ctx:
        sb, ps, sem = maker(ctx)
        h1 = [tables[:, j * D:(j + 1) * D] for j in range(2)]
        xn = [tables[:, j * D:(j + 1) * D] for j in range(2, 4)]
        xqT = [tables[:, j * D:(j + 1) * D].bitcast(F16).rearrange("p (v c n) -> p v c n", v=2, c=KC) for j in range(4, 6)]
        step = tables[:, 6 * D:7 * D]
        biasb = sb("biasb", [P, 2, D])
        z32 = sb("z32", [P, TILES, HEADS])
        inv_z = sb("inv_z", [P, TILES, HEADS])
        acc_w = sb("acc_w", [P, TILES, HEADS])
        self_w = sb("self_w", [P, TILES, HEADS])
        out_scale = sb("out_scale", [P, 1])
        xr = [sb(f"xr{j}", [P, D]) for j in range(2)]
        own_row = [sb(f"own_row{j}", [P, D]) for j in range(2)]
        x1b = [sb(f"x1b{j}", [P, D]) for j in range(2)]
        lin = [sb(f"lin{j}", [P, D]) for j in range(2)]
        stats = sb("fstats", [P, 2, 6])
        mv = [sb(f"fmv{j}", [P, 2]) for j in range(2)]
        std = [sb(f"fstd{j}", [P, 1]) for j in range(2)]
        rstd = [sb(f"frstd{j}", [P, 1]) for j in range(2)]
        shift = [sb(f"fshift{j}", [P, 1]) for j in range(2)]
        newton = sb("fnewton", [P, 1])
        scale = [sb(f"fscale{j}", [P, QB]) for j in range(2)]
        inv = [sb(f"finv{j}", [P, QB]) for j in range(2)]
        tr_ps = [ps(f"ftr_ps{j}", [P, D]) for j in range(2)]
        mm_ps = [ps(f"fmm_ps{j}", [P, D]) for j in range(2)]

        bias_in = sem("bias_in")
        x_in = [sem(f"fx_in{j}") for j in range(2)]
        own_in = [sem(f"own_in{j}") for j in range(2)]
        ratios_ready = sem("ratios_ready")
        own_scaled = sem("own_scaled")
        mixed = sem("mixed")
        biased = sem("biased")
        x1_ready = sem("x1_ready")
        x1b_ready = sem("x1b_ready")
        var_ready = sem("fvar_ready")
        std_ready = sem("fstd_ready")
        rstd_ready = sem("frstd_ready")
        xn_ready = sem("fxn_ready")
        scales_ready = sem("scales_ready")
        y_ready = sem("y_ready")
        xq_ready = sem("xq_ready")
        tr_done = sem("ftr_done")
        high_ready = sem("fhigh_ready")
        low_ready = sem("flow_ready")
        mm_done = sem("fmm_done")
        lin_ready = sem("lin_ready")
        summed = sem("summed")
        stored = [sem(f"stored{j}") for j in range(2)]
        dve_own = sem("dve_own4")
        dve_turn = sem("dve_turn4")
        block = ctx.enter_context(nc.Block())

        @block.sync
        def _(sp):
            sp.dma_start(biasb[:, 0, :], gnn_bias.partition_broadcast(P)).then_inc(bias_in, 16)
            sp.dma_start(biasb[:, 1, :], ffn_bias.partition_broadcast(P)).then_inc(bias_in, 16)

            def load(t, j, n=P):
                sp.wait_ge(x1_ready, t + 1)
                sp.dma_start(own_row[j][:, :], d_own[bass.ds(t * P, P), :]).then_inc(own_in[j], 16)
                sp.dma_start(xr[j][0:n, :], x[bass.ds(t * P, n), :]).then_inc(x_in[j], 16)

            def store(t, j, n=P):
                sp.wait_ge(summed, t + 1 + SLOTS)
                sp.dma_start(out[bass.ds(t * P, n), :], lin[j][0:n, :]).then_inc(stored[j], 16)

            for t in range(5):
                load(t, t % 2)
            with sp.Fori(0, TILES // 2 - 3) as i:
                for j in range(2):
                    store(2 * i + j, j)
                    load(2 * i + j + 5, 1 - j)
            store(LAST - 6, 0)
            load(LAST - 1, 1)
            store(LAST - 5, 1)
            load(LAST, 0, LAST_ROWS)
            for t in range(LAST - 4, LAST + 1):
                store(t, t % 2, P if t < LAST else LAST_ROWS)
            sp.wait_ge(stored[0], 16 * (TILES // 2 + 1))
            sp.wait_ge(stored[1], 16 * (TILES // 2))

        @block.gpsimd
        def _(pool):
            def bias(t, j):
                pool.wait_ge(mixed, t + 1)
                nc.gpsimd.tensor_tensor(out=h1[j], in0=h1[j], in1=biasb[:, 0, :], op=ALU.add).then_inc(biased, 1)

            def unscale(t, j):
                pool.wait_ge(scales_ready, t + 1)
                nc.gpsimd.tensor_tensor(out=blocks(xn[j]), in0=blocks(xn[j]), in1=spread(inv[j][:, :]),
                                        op=ALU.mult).then_inc(y_ready, 1)

            def residual(t, j):
                pool.wait_ge(x1_ready, t + 1 + SLOTS)
                pool.wait_ge(summed, t + 1)
                nc.gpsimd.tensor_tensor(out=x1b[j][:, :], in0=h1[j], in1=biasb[:, 1, :], op=ALU.add).then_inc(x1b_ready, 1)

            def total(t, j):
                pool.wait_ge(x1b_ready, t + 1 + SLOTS)
                pool.wait_ge(lin_ready, t + 1 + SLOTS)
                nc.gpsimd.tensor_tensor(out=lin[j][:, :], in0=lin[j][:, :], in1=x1b[j][:, :], op=ALU.add).then_inc(summed, 1)

            pool.sem_inc(x1b_ready, SLOTS)
            pool.sem_inc(summed, SLOTS)
            pool.wait_ge(bias_in, 32)
            bias(0, 0)
            bias(1, 1)
            unscale(0, 0)
            residual(0, 0)
            bias(2, 0)
            unscale(1, 1)
            residual(1, 1)
            with pool.Fori(1, TILES // 2) as i:
                for j in range(2):
                    t = 2 * i + j
                    bias(t + 1, 1 - j)
                    unscale(t, j)
                    total(t - 2, j)
                    residual(t, j)
            unscale(LAST, 0)
            total(LAST - 2, 0)
            residual(LAST, 0)
            total(LAST - 1, 1)
            total(LAST, 0)

        @block.vector
        def _(dve):
            own = Chain(dve, dve_own)
            dve.sem_inc(x1_ready, SLOTS)
            own.link(nc.vector.tensor_tensor(out=z32[:, :, :], in0=zsum[:, :, 0:HEADS], in1=zsum[:, :, HEADS:2 * HEADS], op=ALU.add))
            own.link(nc.vector.scalar_tensor_tensor(out=z32[:, :, :], in0=z32[:, :, :], scalar=1.0 / NUM_SCALE,
                                                    in1=self_num[:, :, :], op0=ALU.mult, op1=ALU.add))
            own.link(nc.vector.reciprocal(inv_z[:, :, :], z32[:, :, :]))
            nc.vector.tensor_scalar(acc_w[:, :, :], inv_z[:, :, :], xp_inverse[:, :], 1.0 / NUM_SCALE, ALU.mult, ALU.mult)
            nc.vector.tensor_scalar(out_scale[:, :], wd_inverse[:, :], 1.0 / ROW_SCALE, None, ALU.mult)
            own.link(nc.vector.tensor_tensor(out=self_w[:, :, :], in0=self_num[:, :, :], in1=inv_z[:, :, :], op=ALU.mult))
            dve.sem_inc(ratios_ready, 1)

            def mix(t, j):
                dve.wait_ge(own_scaled, t + 1)
                dve.wait_ge(x1b_ready, t + 1)
                for h in range(HEADS):
                    cols = slice(h * C, (h + 1) * C)
                    last = nc.vector.scalar_tensor_tensor(
                        out=h1[j][:, cols], in0=acc[:, bass.ds(t, 1), cols].rearrange("p o n -> p (o n)"),
                        scalar=acc_w[:, bass.ds(t, 1), h:h + 1].rearrange("p o h -> p (o h)"),
                        in1=own_row[j][:, cols], op0=ALU.mult, op1=ALU.add)
                last.then_inc(mixed, 1)

            def x1(t, j, n):
                dve.wait_ge(biased, t + 1)
                dve.wait_ge(x_in[j], 16 * (n + 1))
                nc.vector.scalar_tensor_tensor(out=h1[j], in0=h1[j], scalar=0.0, in1=xr[j][:, :], op0=ALU.max,
                                               op1=ALU.add).then_inc(x1_ready, 1)
                dve.wait_ge(x1_ready, t + 1 + SLOTS)
                nc.vector.bn_stats(stats[:, 0, :], h1[j][:, 0:512])
                own.link(nc.vector.bn_stats(stats[:, 1, :], h1[j][:, 512:1024]))
                dve.sem_inc(dve_turn, 1)
                own.link(nc.vector.bn_aggr(mv[j][:, :], stats[:, :, :].rearrange("p a b -> p (a b)")))
                nc.vector.tensor_scalar(mv[j][:, 1:2], mv[j][:, 1:2], EPS, None, ALU.add).then_inc(var_ready, 1)

            def root(t, j):
                dve.wait_ge(std_ready, t + 1)
                inverse_root(nc, own, std[j][:, :], mv[j][:, 1:2], rstd[j][:, :], newton[:, :])
                nc.vector.scalar_tensor_tensor(out=shift[j][:, :], in0=mv[j][:, 0:1], scalar=-1.0, in1=rstd[j][:, :],
                                               op0=ALU.mult, op1=ALU.mult).then_inc(rstd_ready, 1)

            def scales(t, j):
                dve.wait_ge(xn_ready, t + 1)
                block_scales(nc, own, xn[j], scale[j][:, :], inv[j][:, :]).then_inc(scales_ready, 1)

            def grid(t, j):
                dve.wait_ge(y_ready, t + 1)
                round_to_grid(nc, own, xn[j], step, scale[j][:, :], xn[j]).then_inc(xq_ready, 1)

            def low(t, j):
                dve.wait_ge(high_ready, t + 1 + SLOTS)
                nc.vector.scalar_tensor_tensor(
                    out=xqT[j][:, 1, :, :].rearrange("p c n -> p (c n)"), in0=tr_ps[j][:, :], scalar=ROW_SCALE,
                    in1=xqT[j][:, 0, :, :].rearrange("p c n -> p (c n)"), op0=ALU.mult, op1=ALU.subtract).then_inc(low_ready, 1)

            def turn(t, j, n, first=False, last=False):
                if not last:
                    mix(t + 1, 1 - j)
                scales(t, j)
                if not first:
                    low(t - 1, 1 - j)
                if not last:
                    x1(t + 1, 1 - j, n)
                grid(t, j)
                if not last:
                    root(t + 1, 1 - j)

            mix(0, 0)
            x1(0, 0, 0)
            root(0, 0)
            turn(0, 0, 0, first=True)
            links = STAT_LINKS + ROOT_LINKS + SCALE_LINKS + ROUND_LINKS
            with dve.Fori(0, TILES // 2 - 1) as i:
                back = own.enter(i, 2 * links)
                turn(2 * i + 1, 1, i + 1)
                turn(2 * i + 2, 0, i + 1)
            own.leave(back, TILES // 2 - 1)
            turn(LAST - 1, 1, TILES // 2)
            turn(LAST, 0, None, last=True)
            low(LAST, 0)

        @block.scalar
        def _(act):
            act.sem_inc(high_ready, SLOTS)
            act.sem_inc(lin_ready, SLOTS)
            act.wait_ge(ratios_ready, 1)

            def scale_own(t, j, n):
                act.wait_ge(own_in[j], 16 * (n + 1))
                for h in range(HEADS):
                    cols = slice(h * C, (h + 1) * C)
                    last = nc.scalar.activation(own_row[j][:, cols], own_row[j][:, cols], ACT.Copy,
                                                scale=self_w[:, bass.ds(t, 1), h:h + 1].rearrange("p o h -> p (o h)"))
                last.then_inc(own_scaled, 1)

            def norm(t, j):
                act.wait_ge(var_ready, t + 1)
                nc.scalar.activation(std[j][:, :], mv[j][:, 1:2], ACT.Sqrt).then_inc(std_ready, 1)
                act.wait_ge(tr_done, t + 1)
                act.wait_ge(rstd_ready, t + 1)
                nc.scalar.activation(xn[j], h1[j], ACT.Identity, bias=shift[j][:, :], scale=rstd[j][:, :]).then_inc(xn_ready, 1)

            def high(t, j):
                act.wait_ge(tr_done, t + 1 + SLOTS)
                act.wait_ge(mm_done, t + 1)
                nc.scalar.activation(xqT[j][:, 0, :, :].rearrange("p c n -> p (c n)"), tr_ps[j][:, :], ACT.Copy,
                                     scale=ROW_SCALE).then_inc(high_ready, 1)

            def linear(t, j, n):
                act.wait_ge(mm_done, t + 1 + SLOTS)
                if n is not None:
                    act.wait_ge(stored[j], n)
                nc.scalar.activation(lin[j][:, :], mm_ps[j][:, :], ACT.Copy, scale=out_scale[:, :]).then_inc(lin_ready, 1)

            scale_own(0, 0, 0)
            scale_own(1, 1, 0)
            norm(0, 0)
            scale_own(2, 0, 1)
            norm(1, 1)
            high(0, 0)
            scale_own(3, 1, 1)
            norm(2, 0)
            high(1, 1)
            for t in (2, 3):
                linear(t - 2, t % 2, None)
                scale_own(t + 2, t % 2, t // 2 + 1)
                norm(t + 1, (t + 1) % 2)
                high(t, t % 2)
            with act.Fori(2, TILES // 2 - 1) as i:
                for j in range(2):
                    t = 2 * i + j
                    linear(t - 2, j, 16 * (i - 1))
                    scale_own(t + 2, j, i + 1)
                    norm(t + 1, 1 - j)
                    high(t, j)
            for t in (LAST - 2, LAST - 1, LAST):
                linear(t - 2, t % 2, 16 * (t // 2 - 1))
                if t + 2 <= LAST:
                    scale_own(t + 2, t % 2, t // 2 + 1)
                if t + 1 <= LAST:
                    norm(t + 1, (t + 1) % 2)
                high(t, t % 2)
            linear(LAST - 1, 1, 16 * (TILES // 2 - 1))
            linear(LAST, 0, 16 * (TILES // 2))

        @block.tensor
        def _(pe):
            pe.sem_inc(tr_done, SLOTS)
            pe.sem_inc(mm_done, SLOTS)

            def turned(t, j):
                pe.wait_ge(xq_ready, t + 1)
                for c in range(KC):
                    last = nc.tensor.transpose(tr_ps[j][:, c * P:(c + 1) * P], xn[j][:, c * P:(c + 1) * P], ident[:, :])
                last.then_inc(tr_done, 1)

            def products(t, j):
                pe.wait_ge(low_ready, t + 1)
                pe.wait_ge(lin_ready, t + 1)
                for c in range(KC):
                    for a, b in ((0, 0), (0, 1), (1, 0)):
                        for half in range(2):
                            cols = slice(half * 512, (half + 1) * 512)
                            last = nc.tensor.matmul(mm_ps[j][:, cols], xqT[j][:, a, c, :], wdT[:, c, b, cols],
                                                    start=(c == 0 and a + b == 0), stop=(c == KC - 1 and a == 1))
                last.then_inc(mm_done, 1)

            turned(0, 0)
            with pe.Fori(0, TILES // 2) as i:
                for j in range(2):
                    products(2 * i + j, j)
                    turned(2 * i + j + 1, 1 - j)
            products(LAST, 0)


_INS = ['x', 'src', 'dst', 'L0_gnn_W', 'L0_gnn_att_src', 'L0_gnn_att_dst', 'L0_gnn_bias', 'L0_ffn_weight', 'L0_ffn_bias']


def kernel(**inputs):
    import numpy as _np
    import concourse.bacc as _bacc
    from concourse import mybir as _mybir
    from concourse.bass_utils import run_bass_kernel_spmd as _run

    nc = _bacc.Bacc("TRN2", target_bir_lowering=False, num_devices=1)
    arrays, args = {}, []
    for name in _INS:
        a = _np.ascontiguousarray(inputs[name])
        arrays[f"in_{name}_dram"] = a
        args.append(nc.dram_tensor(f"in_{name}_dram", a.shape, _mybir.dt.from_np(a.dtype), kind="ExternalInput").ap())
    args.append(nc.dram_tensor("out_0_dram", (N, D), F32, kind="ExternalOutput").ap())
    program(nc, *args)
    r = _run(nc, [arrays], core_ids=[0])
    return r.results[0]["out_0_dram"]
```

```python
import concourse.bass as bass
from concourse import mybir
from contextlib import ExitStack

F32 = mybir.dt.float32
BF16 = mybir.dt.bfloat16
I32 = mybir.dt.int32
ALU = mybir.AluOpType
ACT = mybir.ActivationFunctionType
AX = mybir.AxisListType

P = 128
N = 3125
D = 1024
E = 50000
HEADS = 4
C = D // HEADS
KC = D // P
TILES = -(-N // P)
NP = TILES * P
LAST_ROWS = N - (TILES - 1) * P
SUB = 2
ET = -(-E // (SUB * P))
EC = ET * SUB
EP = EC * P
STEPS = -(-(ET + TILES - 1) // 4) * 4
KCOLS = 2 * P
HCOLS = 17
HBATCH = 24
HPAD = HCOLS * HBATCH
GCOLS = 5
GSLOTS = 5
GFILLS = 80
GPAD = GCOLS * (GFILLS + GSLOTS)
BIG = 1e38
FAR = 1 << 20
SLOTS = 2
EPS = 1e-5
SLOPE = 0.2
QBLOCK = 32
QB = D // QBLOCK
QMAX = 7.5
EXPONENT = 0x7F800000
F16 = mybir.dt.float16
NUM_SCALE = 2.0 ** 14
ROW_SCALE = 2.0 ** 9


class Chain:

    def __init__(self, eng, sem):
        self.eng, self.sem, self.base, self.n = eng, sem, 0, 0

    def link(self, ins):
        ins.then_inc(self.sem, 1)
        self.n += 1
        self.eng.wait_ge(self.sem, self.base + self.n)

    def enter(self, i, per):
        back = (self.base, self.n, per)
        self.base = i * per + (self.base + self.n)
        self.n = 0
        return back

    def leave(self, back, turns):
        base, n, per = back
        assert self.n == per, (self.n, per)
        self.base, self.n = base, n + per * turns


def blocks(a):
    return a.rearrange("p (b k) -> p b k", k=QBLOCK)


def spread(a):
    return a.unsqueeze(2).to_broadcast([P, QB, QBLOCK])


def block_scales(nc, chain, src, scale, inv):
    chain.link(nc.vector.tensor_reduce(out=scale, in_=blocks(src), axis=AX.X, op=ALU.max, apply_absolute_value=True))
    chain.link(nc.vector.tensor_scalar(scale, scale, 1.0 / QMAX, 1e-30, ALU.mult, ALU.max))
    return nc.vector.reciprocal(inv, scale)


def round_to_grid(nc, chain, y, step):
    chain.link(nc.vector.tensor_scalar(step.bitcast(I32), y.bitcast(I32), EXPONENT, None, ALU.bitwise_and))
    chain.link(nc.vector.tensor_scalar(step, step, 1.0, None, ALU.max))
    chain.link(nc.vector.scalar_tensor_tensor(out=y, in0=step, scalar=6.0625, in1=y, op0=ALU.mult, op1=ALU.subtract))
    chain.link(nc.vector.tensor_scalar(y.bitcast(I32), y.bitcast(I32), -(1 << 18), None, ALU.bitwise_and))
    return nc.vector.scalar_tensor_tensor(out=y, in0=step, scalar=6.0, in1=y, op0=ALU.mult, op1=ALU.subtract)


SCALE_LINKS = 2
ROUND_LINKS = 4


def power_scale(nc, chain, largest, low, scale, inverse, top):
    chain.link(nc.vector.tensor_scalar(low, largest, 2.0 ** -100, None, ALU.max))
    chain.link(nc.vector.tensor_scalar(low.bitcast(I32), low.bitcast(I32), EXPONENT, None, ALU.bitwise_and))
    chain.link(nc.vector.tensor_scalar(scale.bitcast(I32), low.bitcast(I32), -1.0, float((254 + top) << 23), ALU.mult, ALU.add))
    chain.link(nc.vector.tensor_scalar(inverse.bitcast(I32), low.bitcast(I32), float(-(top << 23)), None, ALU.add))


def inverse_root(nc, chain, root, value, out, tmp):
    chain.link(nc.vector.reciprocal(out, root))
    chain.link(nc.vector.tensor_scalar(tmp, out, out, value, ALU.mult, ALU.mult))
    chain.link(nc.vector.tensor_scalar(tmp, tmp, -0.5, 1.5, ALU.mult, ALU.add))
    chain.link(nc.vector.tensor_tensor(out=out, in0=out, in1=tmp, op=ALU.mult))


STAT_LINKS = 2
ROOT_LINKS = 4


def program(nc, x, src, dst, W, att_src, att_dst, gnn_bias, ffn_w, ffn_bias, out, upto=4):
    d_xnT = nc.dram_tensor("d_xnT", (TILES, P, D), F32, kind="Internal").ap()
    d_xp = nc.dram_tensor("d_xp", (NP, 2 * D), F16, kind="Internal").ap()
    d_own = nc.dram_tensor("d_own", (NP, D), F32, kind="Internal").ap()
    d_asrc = nc.dram_tensor("d_asrc", (NP, HEADS), F32, kind="Internal").ap()
    d_node = nc.dram_tensor("d_node", (NP, 2 * HEADS), F32, kind="Internal").ap()
    d_src = nc.dram_tensor("d_src", (ET, SUB * P), F32, kind="Internal").ap()
    d_dst = nc.dram_tensor("d_dst", (ET, SUB * P), F32, kind="Internal").ap()
    d_segmax = nc.dram_tensor("d_segmax", (EP, HEADS), F32, kind="Internal").ap()
    d_head = nc.dram_tensor("d_head", (EP, 2 * HEADS), F32, kind="Internal").ap()
    d_num = nc.dram_tensor("d_num", (ET, SUB * P * HEADS), F32, kind="Internal").ap()
    d_tile = nc.dram_tensor("d_tile", (KCOLS,), I32, kind="Internal").ap()

    whole = ExitStack()

    def maker(ctx):
        def sb(name, shape, dt=F32):
            return ctx.enter_context(nc.sbuf_tensor(name, shape, dt))

        def ps(name, shape, dt=F32):
            return ctx.enter_context(nc.psum_tensor(name, shape, dt))

        def sem(name):
            return ctx.enter_context(nc.semaphore(name))
        return sb, ps, sem

    with whole:
        sb, ps, sem = maker(whole)
        ident = sb("ident", [P, P])
        logits = sb("logits", [P, TILES, 2 * HEADS])
        self_num = sb("self_num", [P, TILES, HEADS])
        tables = sb("tables", [P, 14 * SUB * KCOLS])
        part = lambda a, b: tables[:, a * SUB * KCOLS:b * SUB * KCOLS]
        dstT = part(0, 1)
        srcT = part(1, 2).bitcast(I32)
        numT = part(2, 6).rearrange("p (h k) -> p h k", h=HEADS)
        numT16 = part(6, 14).bitcast(F16).rearrange("p (k v b) -> p k v b", v=2 * HEADS, b=2)
        xp_scale = sb("xp_scale", [P, 1])
        xp_inverse = sb("xp_inverse", [P, 1])
        wd_scale = sb("wd_scale", [P, 1])
        wd_inverse = sb("wd_inverse", [P, 1])
        tile_row = sb("tile_row", [1, KCOLS], I32)
        wdT = sb("wdT", [P, KC, 2, D], F16)
        front = ExitStack()
        with front:
            sb, ps, sem = maker(front)
            w = sb("w", [P, KC, D])
            dst1 = sb("dst1", [P, HPAD], I32)
            src1 = sb("src1", [P, GPAD], I32)
            dfirst = sb("dfirst", [1, ET], I32)
            wf = sb("wf", [P, KC, D])
            largest = sb("largest", [P, 2])
            count = sb("count", [P, TILES])
            ones = sb("ones", [P, P])
            upper = sb("upper", [P, P])
            wf_in = sem("wf_in")
            normalise(nc, maker, locals())
            if upto >= 2:
                project(nc, maker, locals())
        if upto >= 3:
            back = ExitStack()
            with back:
                sb, ps, sem = maker(back)
                acc = sb("acc", [P, TILES, D])
                zsum = sb("zsum", [P, TILES, 2 * HEADS])
                aggregate(nc, maker, locals())
                if upto >= 4:
                    finish(nc, maker, locals())


def normalise(nc, maker, g):
    x, src, dst, W, att_src, att_dst = g["x"], g["src"], g["dst"], g["W"], g["att_src"], g["att_dst"]
    ident, logits = g["ident"], g["logits"]
    w, dst1, src1, dfirst, count, ones, upper = (g[k] for k in ("w", "dst1", "src1", "dfirst", "count", "ones", "upper"))
    XS = 4
    ctx = ExitStack()
    with ctx:
        sb, ps, sem = maker(ctx)
        att_row = sb("att_row", [2 * KC, P])
        att_cols = sb("att_cols", [P, KC, 2 * HEADS])
        waT = sb("waT", [2 * HEADS, D])
        logitsT = sb("logitsT", [2 * HEADS, TILES, P])
        wa = sb("wa", [P, KC, 2 * HEADS])
        digit = sb("digit", [P, HPAD], I32)
        dlo = sb("dlo", [P, HPAD, 2], BF16)
        dhi = sb("dhi", [P, HPAD, 2], BF16)
        iota_b = sb("iota_b", [P, P], BF16)
        hot_hi = sb("hot_hi", [P, HPAD, 32], BF16)
        hot_lo = [sb(f"hot_lo{j}", [P, HCOLS, P], BF16) for j in range(2)]
        zeros = g["tables"][:, 0:EC * 2 * HEADS]
        xn = [g["tables"][:, EC * 2 * HEADS + j * D:EC * 2 * HEADS + (j + 1) * D] for j in range(2)]
        room = g["wdT"][:, :, :, :].rearrange("p c a n -> p (c a n)").bitcast(F32)
        xt = [room[:, j * D:(j + 1) * D] for j in range(XS)]
        wT = [room[:, (XS + j) * D:(XS + j + 1) * D] for j in range(2)]
        xnT = [sb(f"xnT{j}", [P, KC, P]) for j in range(2)]
        part_max = sb("part_max", [P, KC])
        stats = sb("stats", [P, 2, 6])
        mv = [sb(f"mv{j}", [P, 2]) for j in range(2)]
        std = [sb(f"std{j}", [P, 1]) for j in range(2)]
        rstd = [sb(f"rstd{j}", [P, 1]) for j in range(2)]
        shift = [sb(f"shift{j}", [P, 1]) for j in range(2)]
        newton = sb("newton", [P, 1])
        tr_ps = [ps(f"tr_ps{j}", [P, D]) for j in range(2)]
        lg_ps = [ps(f"lg_ps{j}", [P, 512]) for j in range(2)]
        hist_ps = ps("hist_ps", [P, 512])
        small_ps = ps("small_ps", [P, 512])

        made = sem("made")
        pads_set = sem("pads_set")
        edges_in = sem("edges_in")
        att_in = sem("att_in")
        w_in = [sem(f"w_in{c}") for c in range(KC)]
        zeroed = sem("zeroed")
        att_turned = sem("att_turned")
        att_kept = sem("att_kept")
        wT_done = sem("wT_done")
        wT_kept = sem("wT_kept")
        wa_done = sem("wa_done")
        waT_kept = sem("waT_kept")
        wa_turned = sem("wa_turned")
        wa_kept = sem("wa_kept")
        logits_turned = sem("logits_turned")
        hi_ready = sem("hi_ready")
        lo_ready = sem("lo_ready")
        lo_free = sem("lo_free")
        x_in = [sem(f"x_in{j}") for j in range(XS)]
        var_ready = sem("var_ready")
        std_ready = sem("std_ready")
        rstd_ready = sem("rstd_ready")
        xn_ready = sem("xn_ready")
        tr_done = sem("tr_done")
        xnT_ready = sem("xnT_ready")
        xnT_out = [sem(f"xnT_out{j}") for j in range(2)]
        lg_done = sem("lg_done")
        lg_kept = sem("lg_kept")
        dve_own = sem("dve_own1")
        pool_own = sem("pool_own1")
        dve_turn = sem("dve_turn")
        block = ctx.enter_context(nc.Block())
        TURNS = TILES // XS
        assert TILES == TURNS * XS + 1

        @block.sync
        def _(sp):
            for a, vec in enumerate((att_src, att_dst)):
                sp.dma_start(att_row[a * KC:(a + 1) * KC, :], vec.rearrange("h (u c) -> (h u) c", c=P)).then_inc(att_in, 16)

            def load(t, j, n=P):
                sp.wait_ge(xn_ready, t + 1)
                sp.dma_start(xt[j][0:n, :], x[bass.ds(t * P, n), :]).then_inc(x_in[j], 16)

            for c in range(KC):
                sp.dma_start(w[:, c, :], W[c * P:(c + 1) * P, :]).then_inc(w_in[c], 16)
                if c % 2:
                    load(c // 2, c // 2)
                if c == 1:
                    sp.wait_ge(pads_set, 2)
                    cut = (P - 1) * EC
                    for tile, vec in ((dst1, dst), (src1, src)):
                        sp.dma_start(tile[0:P - 1, 0:EC], vec[0:cut].rearrange("(p c) -> p c", c=EC)).then_inc(edges_in, 16)
                        sp.dma_start(tile[P - 1:P, 0:E - cut], vec[cut:E].unsqueeze(0)).then_inc(edges_in, 16)
            sp.dma_start(dfirst[:, :], dst[0:(ET - 1) * SUB * P + 1:SUB * P].unsqueeze(0),
                         allow_slow_non_contiguous=True).then_inc(edges_in, 16)

            def store(t, j):
                sp.wait_ge(xnT_ready, t + 1)
                sp.dma_start(g["d_xnT"][bass.ds(t, 1), :, :].rearrange("o p n -> (o p) n"),
                             xnT[j][:, :, :].rearrange("p c n -> p (c n)")).then_inc(xnT_out[j], 16)

            with sp.Fori(0, TURNS - 1) as i:
                for j in range(XS):
                    load(XS * i + j + XS, j)
                    store(XS * i + j, j % 2)
            load(TILES - 1, 0, LAST_ROWS)
            sp.dma_start(g["wf"][:, :, :], g["ffn_w"].rearrange("(c p) n -> p c n", p=P)).then_inc(g["wf_in"], 16)
            for t in range(TILES - 1 - XS, TILES):
                store(t, t % 2)
            sp.wait_ge(xnT_out[0], 16 * (TILES // 2 + 1))
            sp.wait_ge(xnT_out[1], 16 * (TILES // 2))

        @block.gpsimd
        def _(pool):
            own = Chain(pool, pool_own)
            own.link(nc.gpsimd.memset(ident[:, :], 0.0))
            nc.gpsimd.affine_select(out=ident[:, :], in_=ident[:, :], compare_op=ALU.not_equal, fill=1.0, base=0,
                                    pattern=[[-1, P]], channel_multiplier=1).then_inc(made, 1)
            nc.gpsimd.iota(iota_b[:, :], pattern=[[1, P]], base=0, channel_multiplier=0,
                           allow_small_or_imprecise_dtypes=True).then_inc(made, 1)
            own.link(nc.gpsimd.memset(upper[:, :], 1.0))
            nc.gpsimd.affine_select(out=upper[:, :], in_=upper[:, :], compare_op=ALU.is_ge, fill=0.0, base=0,
                                    pattern=[[1, P]], channel_multiplier=-1)
            own.link(nc.gpsimd.memset(zeros[:, :], 0.0))
            nc.gpsimd.dma_start(g["d_head"].rearrange("(p c) v -> p (c v)", c=EC), zeros[:, :]).then_inc(zeroed, 16)
            pool.wait_ge(zeroed, 16)

        @block.vector
        def _(dve):
            own = Chain(dve, dve_own)
            nc.vector.memset(dst1[:, :], NP - 1).then_inc(pads_set, 1)
            nc.vector.memset(src1[:, :], 0).then_inc(pads_set, 1)
            nc.vector.memset(ones[:, :], 1.0)
            dve.sem_inc(xn_ready, XS)
            own.link(nc.vector.memset(att_cols[:, :, :], 0.0))
            dve.wait_ge(att_turned, 1)
            per = KC // HEADS
            for h in range(HEADS):
                last = nc.vector.tensor_copy(
                    att_cols[:, h * per:(h + 1) * per, h:h + HEADS + 1:HEADS],
                    hist_ps[:, 0:2 * KC].rearrange("p (a c) -> p c a", a=2)[:, h * per:(h + 1) * per, :])
            last.then_inc(att_kept, 1)

            def stat(t, j, n):
                dve.wait_ge(x_in[j], 16 * (n + 1))
                nc.vector.bn_stats(stats[:, 0, :], xt[j][:, 0:512])
                own.link(nc.vector.bn_stats(stats[:, 1, :], xt[j][:, 512:1024]))
                dve.sem_inc(dve_turn, 1)
                own.link(nc.vector.bn_aggr(mv[j % 2][:, :], stats[:, :, :].rearrange("p a b -> p (a b)")))
                nc.vector.tensor_scalar(mv[j % 2][:, 1:2], mv[j % 2][:, 1:2], EPS, None, ALU.add).then_inc(var_ready, 1)

            def root(t, s):
                dve.wait_ge(std_ready, t + 1)
                dve.wait_ge(xn_ready, t + XS - 1)
                inverse_root(nc, own, std[s][:, :], mv[s][:, 1:2], rstd[s][:, :], newton[:, :])
                nc.vector.scalar_tensor_tensor(out=shift[s][:, :], in0=mv[s][:, 0:1], scalar=-1.0, in1=rstd[s][:, :],
                                               op0=ALU.mult, op1=ALU.mult).then_inc(rstd_ready, 1)

            stat(0, 0, 0)
            for c in range(KC):
                dve.wait_ge(w_in[c], 16)
                last = nc.vector.tensor_reduce(out=part_max[:, c:c + 1], in_=w[:, c, :], axis=AX.X, op=ALU.max,
                                               apply_absolute_value=True)
            own.link(last)
            nc.vector.tensor_reduce(out=g["largest"][:, 0:1], in_=part_max[:, :], axis=AX.X, op=ALU.max)
            dve.wait_ge(edges_in, 16 * 5)
            own.link(nc.vector.tensor_scalar(digit[:, :], dst1[:, :], P - 1, None, ALU.bitwise_and))
            own.link(nc.vector.tensor_copy(dlo[:, :, :], digit[:, :].unsqueeze(2).to_broadcast([P, HPAD, 2])))
            own.link(nc.vector.memset(dlo[:, EC:HPAD, :], 255.0))
            own.link(nc.vector.tensor_scalar(digit[:, :], dst1[:, :], 7, None, ALU.logical_shift_right))
            own.link(nc.vector.tensor_copy(dhi[:, :, :], digit[:, :].unsqueeze(2).to_broadcast([P, HPAD, 2])))
            dve.wait_ge(made, 2)

            def hots(out, digits, cols, width):
                shape = [P, cols, width // 2, 2]
                return nc.vector.tensor_tensor(
                    out=out.rearrange("p c (n b) -> p c n b", b=2), in0=digits.unsqueeze(2).to_broadcast(shape),
                    in1=iota_b[:, 0:width].rearrange("p (n b) -> p n b", b=2).unsqueeze(1).to_broadcast(shape), op=ALU.is_equal)

            hots(hot_hi[:, :, :], dhi[:, :, :], HPAD, 32).then_inc(hi_ready, 1)

            def one_hot(b, s):
                dve.wait_ge(lo_free, b + 1)
                hots(hot_lo[s][:, :, :], dlo[:, bass.ds(b * HCOLS, HCOLS), :], HCOLS, P).then_inc(lo_ready, 1)

            with dve.Fori(0, TURNS) as i:
                back = own.enter(i, XS * (STAT_LINKS + ROOT_LINKS))
                for j in range(XS):
                    t = XS * i + j
                    stat(t + 1, (j + 1) % XS, i + (j + 1) // XS)
                    root(t, j % 2)
                    one_hot(t, j % 2)
            own.leave(back, TURNS)
            root(TILES - 1, 0)
            dve.wait_ge(lo_free, SLOTS + HBATCH)
            nc.vector.tensor_copy(count[:, :], hist_ps[:, 0:TILES])

        @block.scalar
        def _(act):
            def root(t, s):
                act.wait_ge(var_ready, t + 1)
                nc.scalar.activation(std[s][:, :], mv[s][:, 1:2], ACT.Sqrt).then_inc(std_ready, 1)

            def norm(t, j):
                act.wait_ge(rstd_ready, t + 1)
                act.wait_ge(tr_done, t + 1)
                nc.scalar.activation(xn[j % 2][:, :], xt[j][:, :], ACT.Identity, bias=shift[j % 2][:, :],
                                     scale=rstd[j % 2][:, :]).then_inc(xn_ready, 1)

            def tile(t, s, n):
                act.wait_ge(tr_done, t + 1 + SLOTS)
                act.wait_ge(lg_done, t + 1)
                if n is not None:
                    act.wait_ge(xnT_out[s], n)
                nc.scalar.activation(xnT[s][:, :, :].rearrange("p c n -> p (c n)"), tr_ps[s][:, :],
                                     ACT.Copy).then_inc(xnT_ready, 1)

            def keep(t, s):
                act.wait_ge(lg_done, t + 1 + SLOTS)
                nc.scalar.activation(logitsT[:, bass.ds(t, 1), :].rearrange("v o n -> v (o n)"), lg_ps[s][0:2 * HEADS, 0:P],
                                     ACT.Copy).then_inc(lg_kept, 1)

            root(0, 0)
            def keep_wa(c):
                act.wait_ge(wa_done, c + 1)
                nc.scalar.activation(waT[:, c * P:(c + 1) * P], lg_ps[c % 2][0:2 * HEADS, 0:P], ACT.Copy).then_inc(waT_kept, 1)

            for c in range(KC):
                act.wait_ge(wT_done, c + 1)
                if c >= 2:
                    act.wait_ge(wa_done, c - 1)
                nc.scalar.activation(wT[c % 2][:, :], tr_ps[c % 2][:, :], ACT.Copy).then_inc(wT_kept, 1)
                if c >= 1:
                    keep_wa(c - 1)
            keep_wa(KC - 1)
            act.wait_ge(wa_turned, 1)
            nc.scalar.activation(wa[:, :, :].rearrange("p c v -> p (c v)"), small_ps[:, 0:KC * 2 * HEADS], ACT.Copy).then_inc(wa_kept, 1)

            def turn(t, j, n, first=None):
                root(t + 1, (j + 1) % 2)
                norm(t, j)
                if first is None or first >= 1:
                    tile(t - 1, (j + 1) % 2, n)
                if first is None or first >= 2:
                    keep(t - 2, j % 2)

            for t in range(XS):
                turn(t, t, 16 if t == 3 else None, first=t)
            with act.Fori(1, TURNS) as i:
                for j in range(XS):
                    turn(XS * i + j, j, 16 * (2 * i + (j - 1) // 2))
            norm(TILES - 1, 0)
            tile(TILES - 2, 1, 16 * (TILES // 2 - 1))
            keep(TILES - 3, 0)
            tile(TILES - 1, 0, 16 * (TILES // 2))
            keep(TILES - 2, 1)
            keep(TILES - 1, 0)
            act.wait_ge(logits_turned, 1)
            nc.scalar.activation(logits[:, :, :].rearrange("p t v -> p (t v)"), small_ps[:, 0:TILES * 2 * HEADS], ACT.Copy)

        @block.tensor
        def _(pe):
            pe.sem_inc(tr_done, SLOTS)
            pe.sem_inc(lg_done, SLOTS)
            pe.sem_inc(lo_free, SLOTS)
            pe.wait_ge(made, 2)
            pe.wait_ge(att_in, 32)
            nc.tensor.transpose(hist_ps[:, 0:2 * KC], att_row[:, :], ident[0:2 * KC, 0:2 * KC]).then_inc(att_turned, 1)

            def turn_w(c):
                pe.wait_ge(w_in[c], 16)
                if c >= 2:
                    pe.wait_ge(wT_kept, c - 1)
                for n in range(KC):
                    last = nc.tensor.transpose(tr_ps[c % 2][:, n * P:(n + 1) * P], w[:, c, n * P:(n + 1) * P], ident[:, :])
                last.then_inc(wT_done, 1)

            def apply_w(c):
                pe.wait_ge(wT_kept, c + 1)
                if c >= 2:
                    pe.wait_ge(waT_kept, c - 1)
                for n in range(KC):
                    last = nc.tensor.matmul(lg_ps[c % 2][0:2 * HEADS, 0:P], att_cols[:, n, :], wT[c % 2][:, n * P:(n + 1) * P],
                                            start=(n == 0), stop=(n == KC - 1))
                last.then_inc(wa_done, 1)

            turn_w(0)
            pe.wait_ge(att_kept, 1)
            for c in range(KC):
                if c + 1 < KC:
                    turn_w(c + 1)
                apply_w(c)
            pe.wait_ge(waT_kept, KC)
            for c in range(KC):
                last = nc.tensor.transpose(small_ps[:, c * 2 * HEADS:(c + 1) * 2 * HEADS], waT[:, c * P:(c + 1) * P],
                                           ident[0:2 * HEADS, 0:2 * HEADS])
            last.then_inc(wa_turned, 1)

            def tile(t, s):
                pe.wait_ge(xn_ready, t + 1 + XS)
                for c in range(KC):
                    last = nc.tensor.transpose(tr_ps[s][:, c * P:(c + 1) * P], xn[s][:, c * P:(c + 1) * P], ident[:, :])
                last.then_inc(tr_done, 1)

            def logit(t, s):
                pe.wait_ge(xnT_ready, t + 1)
                for c in range(KC):
                    last = nc.tensor.matmul(lg_ps[s][0:2 * HEADS, 0:P], wa[:, c, :], xnT[s][:, c, :], start=(c == 0),
                                            stop=(c == KC - 1))
                last.then_inc(lg_done, 1)

            def counts(b, s, start, stop):
                pe.wait_ge(lo_ready, b + 1)
                for c in range(HCOLS):
                    last = nc.tensor.matmul(
                        hist_ps[:, 0:32], hot_lo[s][:, c, :],
                        hot_hi[:, bass.ds(b * HCOLS + c, 1), :].rearrange("p o v -> p (o v)"),
                        start=(start and c == 0), stop=(stop and c == HCOLS - 1))
                last.then_inc(lo_free, 1)

            def turn(t, s, start=False, stop=False):
                tile(t + 1, 1 - s)
                counts(t, s, start, stop)
                logit(t, s)

            tile(0, 0)
            pe.wait_ge(wa_kept, 1)
            pe.wait_ge(hi_ready, 1)
            turn(0, 0, start=True)
            turn(1, 1)
            with pe.Fori(1, TILES // 2 - 1) as i:
                for j in range(2):
                    t = 2 * i + j
                    pe.wait_ge(lg_kept, t - 1)
                    turn(t, j)
            for t in range(TILES - 3, TILES - 1):
                pe.wait_ge(lg_kept, t - 1)
                turn(t, t % 2, stop=(t == HBATCH - 1))
            pe.wait_ge(lg_kept, TILES - 2)
            logit(TILES - 1, 0)
            pe.wait_ge(lg_kept, TILES)
            for t in range(TILES):
                last = nc.tensor.transpose(small_ps[:, t * 2 * HEADS:(t + 1) * 2 * HEADS], logitsT[:, t, :],
                                           ident[0:2 * HEADS, 0:2 * HEADS])
            last.then_inc(logits_turned, 1)


def project(nc, maker, g):
    ident, logits, self_num = g["ident"], g["logits"], g["self_num"]
    srcT, dstT, numT, tile_row, wdT = (g[k] for k in ("srcT", "dstT", "numT", "tile_row", "wdT"))
    w, dst1, src1, dfirst, count, ones, upper = (g[k] for k in ("w", "dst1", "src1", "dfirst", "count", "ones", "upper"))
    d_xnT, d_xp, d_asrc, d_node, d_src, d_dst = (g[k] for k in ("d_xnT", "d_xp", "d_asrc", "d_node", "d_src", "d_dst"))
    d_segmax, d_head, d_num, d_tile, ffn_w = (g[k] for k in ("d_segmax", "d_head", "d_num", "d_tile", "ffn_w"))
    d_own, wf, largest = g["d_own"], g["wf"], g["largest"]
    numT16, xp_scale, xp_inverse, wd_scale, wd_inverse = (
        g[k] for k in ("numT16", "xp_scale", "xp_inverse", "wd_scale", "wd_inverse"))
    CH = KCOLS // P
    ctx = ExitStack()
    with ctx:
        sb, ps, sem = maker(ctx)
        xnT = [sb(f"pxnT{j}", [P, KC, P]) for j in range(3)]
        xp = [sb(f"xp{j}", [P, 2, D], F16) for j in range(3)]
        own_row = [sb(f"xp_own{j}", [P, D]) for j in range(3)]
        wq = sb("wq", [P, D])
        step = sb("q_step", [P, D])
        scale = sb("q_scale", [P, QB])
        inv = sb("q_inv", [P, QB])
        most = sb("most", [2, 1])
        most_row = sb("most_row", [2, 2])
        low = sb("low", [P, 2])
        dstf = sb("dstf", [P, EC])
        srcf = sb("srcf", [P, EC])
        same = sb("same", [P, EC])
        fence = sb("fence", [P, EC])
        tmp = sb("tmp", [P, EC])
        idx = [sb(f"idx{j}", [P, GCOLS], I32) for j in range(GSLOTS)]
        got = [sb(f"got{j}", [P, GCOLS * HEADS]) for j in range(GSLOTS)]
        asrc = sb("asrc", [P, GCOLS * GFILLS, HEADS])
        segmax = sb("segmax", [P, EC, HEADS])
        tables, at = g["tables"], [EC * 2 * HEADS + n * CH * SUB * P for n in (0, 1, 2, 2 + HEADS)]
        head = tables[:, 0:at[0]].rearrange("p (c v) -> p c v", v=2 * HEADS)
        srow, drow, nrow = (tables[:, a:b].rearrange("p (c e) -> p c e", c=CH) for a, b in zip(at, at[1:]))
        first = sb("first", [P, 2 * HEADS])
        cinc = sb("cinc", [P, TILES])
        zero_t = sb("zero_t", [P, TILES])
        startf = sb("startf", [P, TILES])
        lastf = sb("lastf", [P, TILES])
        has = sb("has", [P, TILES])
        start_i = sb("start_i", [P, TILES], I32)
        last_i = sb("last_i", [P, TILES], I32)
        node = sb("node", [P, TILES, 2 * HEADS])
        nmax = sb("nmax", [P, TILES, HEADS])
        nself = sb("nself", [P, TILES, HEADS])
        tf_i = sb("tf_i", [1, ET], I32)
        tf = sb("tf", [1, ET])
        irow = sb("irow", [1, ET])
        kcol = sb("kcol", [P, CH])
        etile = sb("etile", [P, CH])
        ntile = sb("ntile", [P, CH])
        ntile128 = sb("ntile128", [P, CH])
        step_i = sb("step_i", [P, CH], I32)
        ntile_i = sb("ntile_i", [P, CH], I32)
        far = segmax[:, :, :].rearrange("p c h -> p (c h)")[:, 0:SUB * KCOLS]
        ends = sb("ends", [P, 3, HEADS])
        erow = sb("erow", [HEADS, 3, P])
        whole = sb("whole_run", [HEADS, P])
        joins = sb("joins", [HEADS, P])
        carry = sb("carry", [HEADS, P])
        cin = sb("cin", [HEADS, P])
        cinT = sb("cinT", [P, HEADS])
        xp_ps = [ps(f"xp_ps{j}", [P, D]) for j in range(3)]
        g_ps = ps("g_ps", [P, D])

        asrc_out = sem("asrc_out")
        flat_ready = sem("flat_ready")
        flat_out = sem("flat_out")
        iotas = sem("iotas")
        idx_ready = sem("idx_ready")
        gathered = [sem(f"gathered{j}") for j in range(GSLOTS)]
        xnT_in = [sem(f"pxnT_in{j}") for j in range(3)]
        xp_done = sem("xp_done")
        xp_kept = sem("xp_kept")
        xp_out = [sem(f"xp_out{j}") for j in range(3)]
        largest_ready = sem("largest_ready")
        most_turned = sem("most_turned")
        most_row_ready = sem("most_row_ready")
        most_spread = sem("most_spread")
        powers_ready = sem("powers_ready")
        xp_low = sem("xp_low")
        wd_high = sem("wd_high")
        num_high = sem("num_high")
        num_low = sem("num_low")
        wq_ready = sem("wq_ready")
        wtr_done = sem("wtr_done")
        wtr_kept = sem("wtr_kept")
        cexc_ready = sem("cexc_ready")
        cum_done = sem("cum_done")
        tf_ready = sem("tf_ready")
        stair_done = sem("stair_done")
        plan_read = sem("plan_read")
        plan_ready = sem("plan_ready")
        tile_out = sem("tile_out")
        ends_ready = sem("ends_ready")
        erow_done = sem("erow_done")
        cin_ready = sem("cin_ready")
        cinT_done = sem("cinT_done")
        segmax_ready = sem("segmax_ready")
        segmax_out = sem("segmax_out")
        nmax_in = sem("nmax_in")
        node_ready = sem("node_ready")
        node_out = sem("node_out")
        scattered = sem("scattered")
        first_in = sem("first_in")
        head_in = sem("head_in")
        nself_ready = sem("nself_ready")
        self_kept = sem("self_kept")
        logit_ready = sem("logit_ready")
        num_ready = sem("num_ready")
        num_out = sem("num_out")
        rows_in = sem("rows_in")
        rows_ready = sem("rows_ready")
        steps_done = sem("steps_done")
        dve_own = sem("dve_own2")
        pool_turn = sem("pool_turn2")
        block = ctx.enter_context(nc.Block())
        lines = lambda d: d.rearrange("i e -> (i e)").rearrange("(p c) -> p c", c=EC)

        @block.sync
        def _(sp):
            def load(t, j):
                sp.wait_ge(xp_done, t + 1)
                sp.dma_start(xnT[j][:, :, :].rearrange("p c n -> p (c n)"),
                             d_xnT[bass.ds(t, 1), :, :].rearrange("o p n -> (o p) n")).then_inc(xnT_in[j], 16)

            def store(t, j):
                sp.wait_ge(xp_low, t + 1 + 3)
                sp.dma_start(d_xp[bass.ds(t * P, P), :], xp[j][:, :, :].rearrange("p a n -> p (a n)")).then_inc(xp_out[j], 16)
                sp.dma_start(d_own[bass.ds(t * P, P), :], own_row[j][:, :]).then_inc(xp_out[j], 16)

            for t in range(3):
                load(t, t)
            with sp.Fori(0, KC - 1) as i:
                for j in range(3):
                    load(3 * i + j + 3, j)
                    store(3 * i + j, j)
            load(TILES - 1, 0)
            for t in range(TILES - 4, TILES):
                store(t, t % 3)
            for j in range(3):
                sp.wait_ge(xp_out[j], 32 * len(range(j, TILES, 3)))

        @block.gpsimd
        def _(pool):
            def gather(out, table, index, signal):
                nc.gpsimd.indirect_dma_start(
                    out=out, out_offset=None, in_=table,
                    in_offset=bass.IndirectOffsetOnAxis(ap=index, axis=0)).then_inc(signal, 16)

            nc.gpsimd.dma_start(d_asrc.rearrange("(t p) h -> p t h", p=P), logits[:, :, 0:HEADS]).then_inc(asrc_out, 16)
            nc.gpsimd.iota(irow[:, :], pattern=[[1, ET]], base=0, channel_multiplier=0,
                           allow_small_or_imprecise_dtypes=True).then_inc(iotas, 1)
            nc.gpsimd.iota(kcol[:, :], pattern=[[P, CH]], base=0, channel_multiplier=1,
                           allow_small_or_imprecise_dtypes=True).then_inc(iotas, 1)
            pool.wait_ge(asrc_out, 16)
            with pool.Fori(0, GFILLS // GSLOTS) as i:
                for s in range(GSLOTS):
                    pool.wait_ge(idx_ready, i * GSLOTS + s + 1)
                    pool.sem_inc(pool_turn, 1)
                    for c in range(GCOLS):
                        gather(got[s][:, c * HEADS:(c + 1) * HEADS], d_asrc, idx[s][:, c:c + 1], gathered[s])
            pool.wait_ge(flat_ready, 1)
            nc.gpsimd.dma_start(lines(d_dst), dstf[:, :]).then_inc(flat_out, 16)
            nc.gpsimd.dma_start(lines(d_src), srcf[:, :]).then_inc(flat_out, 16)
            pool.wait_ge(plan_ready, 1)
            nc.gpsimd.dma_start(d_tile.rearrange("(c p) -> p c", p=P), ntile_i[:, :],
                                allow_slow_non_contiguous=True).then_inc(tile_out, 16)
            pool.wait_ge(flat_out, 32)
            for c in range(CH):
                gather(srow[:, c, :], d_src, step_i[:, c:c + 1], rows_in)
                gather(drow[:, c, :], d_dst, step_i[:, c:c + 1], rows_in)
            pool.wait_ge(tile_out, 16)
            nc.gpsimd.dma_start(tile_row[:, :], d_tile.unsqueeze(0)).then_inc(tile_out, 16)
            pool.wait_ge(segmax_ready, 1)
            nc.gpsimd.dma_start(d_segmax.rearrange("(p c) h -> p (c h)", c=EC),
                                segmax[:, :, :].rearrange("p c h -> p (c h)")).then_inc(segmax_out, 16)
            pool.wait_ge(segmax_out, 16)
            for t in range(TILES):
                gather(nmax[:, t, :], d_segmax, last_i[:, t:t + 1], nmax_in)
            pool.wait_ge(node_ready, 1)
            nc.gpsimd.dma_start(d_node.rearrange("(t p) v -> p t v", p=P), node[:, :, :]).then_inc(node_out, 16)
            for t in range(TILES):
                nc.gpsimd.indirect_dma_start(
                    out=d_head, out_offset=bass.IndirectOffsetOnAxis(ap=start_i[:, t:t + 1], axis=0),
                    in_=node[:, t, :], in_offset=None, bounds_check=EP - 1, oob_is_err=False).then_inc(scattered, 16)
            pool.wait_ge(node_out, 16)
            gather(first[:, :], d_node, dst1[:, 0:1], first_in)
            pool.wait_ge(scattered, 16 * TILES)
            nc.gpsimd.dma_start(head[:, :, :].rearrange("p c v -> p (c v)"),
                                d_head.rearrange("(p c) v -> p (c v)", c=EC)).then_inc(head_in, 16)
            pool.wait_ge(num_ready, 1)
            nc.gpsimd.dma_start(d_num.rearrange("i e -> (i e)").rearrange("(p c) -> p c", c=EC * HEADS),
                                segmax[:, :, :].rearrange("p c h -> p (c h)")).then_inc(num_out, 16)
            pool.wait_ge(num_out, 16)
            for c in range(CH):
                gather(nrow[:, c, :], d_num, step_i[:, c:c + 1], rows_in)
            pool.wait_ge(tile_out, 32)

        @block.vector
        def _(dve):
            own = Chain(dve, dve_own)

            def fill(s, column):
                nc.vector.tensor_copy(idx[s][:, :], src1[:, bass.ds(column, GCOLS)]).then_inc(idx_ready, 1)

            nc.vector.sem_inc(xp_low, 3)
            for s in range(GSLOTS):
                fill(s, s * GCOLS)
            dve.wait_ge(g["wf_in"], 16)
            nc.vector.tensor_reduce(out=largest[:, 1:2], in_=wf[:, :, :].rearrange("p c n -> p (c n)"), axis=AX.X, op=ALU.max,
                                    apply_absolute_value=True).then_inc(largest_ready, 1)
            dve.wait_ge(most_turned, 1)
            own.link(nc.vector.tensor_reduce(out=most[:, :], in_=g_ps[0:2, 2 * P:3 * P], axis=AX.X, op=ALU.max))
            nc.vector.tensor_scalar(most_row[:, :], ident[0:2, 0:2], most[:, :], None, ALU.mult).then_inc(most_row_ready, 1)
            dve.wait_ge(most_spread, 1)
            power_scale(nc, own, g_ps[:, 2 * P:2 * P + 1], low[:, 0:1], xp_scale[:, :], xp_inverse[:, :], 4)
            power_scale(nc, own, g_ps[:, 2 * P + 1:2 * P + 2], low[:, 1:2], wd_scale[:, :], wd_inverse[:, :], 13)
            nc.vector.sem_inc(powers_ready, 1)
            nc.vector.memset(zero_t[:, :], 0.0)
            nc.vector.tensor_copy(dstf[:, :], dst1[:, 0:EC])
            own.link(nc.vector.tensor_copy(srcf[:, :], src1[:, 0:EC]))
            nc.vector.sem_inc(flat_ready, 1)
            own.link(nc.vector.tensor_tensor_scan(cinc[:, :], count[:, :], zero_t[:, :], 0.0, ALU.add, ALU.add))
            nc.vector.tensor_tensor(out=cinc[:, :], in0=cinc[:, :], in1=count[:, :], op=ALU.subtract).then_inc(cexc_ready, 1)
            own.link(nc.vector.tensor_scalar(tf_i[:, :], dfirst[:, :], 7, None, ALU.logical_shift_right))
            own.link(nc.vector.tensor_copy(tf[:, :], tf_i[:, :]))
            dve.wait_ge(iotas, 2)
            nc.vector.tensor_tensor(out=tf[:, :], in0=tf[:, :], in1=irow[:, :], op=ALU.add).then_inc(tf_ready, 1)
            dve.wait_ge(cum_done, 1)
            own.link(nc.vector.tensor_scalar(has[:, :], count[:, :], 0.0, None, ALU.is_gt))
            own.link(nc.vector.tensor_tensor(out=startf[:, :], in0=g_ps[:, 0:TILES], in1=count[:, :], op=ALU.subtract))
            own.link(nc.vector.scalar_tensor_tensor(out=startf[:, :], in0=has[:, :], scalar=-float(2 * EP), in1=startf[:, :],
                                                    op0=ALU.mult, op1=ALU.add))
            own.link(nc.vector.tensor_scalar(startf[:, :], startf[:, :], float(2 * EP), None, ALU.add))
            own.link(nc.vector.tensor_scalar(lastf[:, :], g_ps[:, 0:TILES], -1.0, 0.0, ALU.add, ALU.max))
            nc.vector.tensor_copy(start_i[:, :], startf[:, :])
            own.link(nc.vector.tensor_copy(last_i[:, :], lastf[:, :]))
            own.link(nc.vector.tensor_scalar(has[:, :], has[:, :], -1.0, BIG, ALU.add, ALU.mult))
            dve.wait_ge(stair_done, 1)
            for c in range(CH):
                own.link(nc.vector.tensor_scalar(tmp[:, 0:ET], g_ps[:, 512:512 + ET], kcol[:, c:c + 1], None, ALU.is_le))
                own.link(nc.vector.tensor_reduce(out=etile[:, c:c + 1], in_=tmp[:, 0:ET], axis=AX.X, op=ALU.add))
            nc.vector.sem_inc(plan_read, 1)
            own.link(nc.vector.tensor_scalar(etile[:, :], etile[:, :], -1.0, 0.0, ALU.add, ALU.max))
            own.link(nc.vector.tensor_tensor(out=ntile[:, :], in0=kcol[:, :], in1=etile[:, :], op=ALU.subtract))
            nc.vector.tensor_scalar(ntile128[:, :], ntile[:, :], float(P), None, ALU.mult)
            own.link(nc.vector.tensor_scalar(ntile[:, :], ntile[:, :], float(TILES - 1), None, ALU.min))
            nc.vector.tensor_copy(step_i[:, :], etile[:, :])
            own.link(nc.vector.tensor_copy(ntile_i[:, :], ntile[:, :]))
            nc.vector.sem_inc(plan_ready, 1)
            nc.vector.memset(same[:, 0:1], 0.0)
            own.link(nc.vector.tensor_tensor(out=same[:, 1:EC], in0=dstf[:, 1:EC], in1=dstf[:, 0:EC - 1], op=ALU.is_equal))
            own.link(nc.vector.tensor_scalar(fence[:, :], same[:, :], -1.0, BIG, ALU.add, ALU.mult))
            own.link(nc.vector.memset(fence[:, 0:1], 0.0))

            rounds = GFILLS // KC

            def split(t, j):
                dve.wait_ge(xp_kept, t + 1 + 3)
                nc.vector.scalar_tensor_tensor(out=xp[j][:, 1, :], in0=xp_ps[j][:, :], scalar=xp_scale[:, :],
                                               in1=xp[j][:, 0, :], op0=ALU.mult, op1=ALU.subtract).then_inc(xp_low, 1)

            with dve.Fori(0, KC) as o:
                back = own.enter(o, SCALE_LINKS + 3 + ROUND_LINKS)
                row = wf[:, bass.ds(o, 1), :].rearrange("p o n -> p (o n)")
                own.link(block_scales(nc, own, row, scale[:, :], inv[:, :]))
                dve.wait_ge(wtr_done, o + 1)
                own.link(nc.vector.tensor_tensor(out=blocks(wq[:, :]), in0=blocks(row), in1=spread(inv[:, :]), op=ALU.mult))
                own.link(round_to_grid(nc, own, wq[:, :], step[:, :]))
                nc.vector.tensor_tensor(out=blocks(wq[:, :]), in0=blocks(wq[:, :]), in1=spread(scale[:, :]),
                                        op=ALU.mult).then_inc(wq_ready, 1)
                for f in range(rounds):
                    s = f % GSLOTS
                    dve.wait_ge(gathered[s], 16 * GCOLS * (o * (rounds // GSLOTS) + f // GSLOTS + 1))
                    nc.vector.tensor_copy(
                        asrc[:, bass.ds((o * rounds + f) * GCOLS, GCOLS), :].rearrange("p c h -> p (c h)"), got[s][:, :])
                    fill(s, (o * rounds + f + GSLOTS) * GCOLS)
                    if f % 3 == 2:
                        split(3 * o + f // 3, f // 3)
                dve.wait_ge(wd_high, o + 1)
                cols = bass.ds(o * P, P)
                nc.vector.scalar_tensor_tensor(
                    out=wdT[:, :, 1, cols], in0=g_ps[:, :].rearrange("p (c n) -> p c n", n=P), scalar=wd_scale[:, :],
                    in1=wdT[:, :, 0, cols], op0=ALU.mult, op1=ALU.subtract).then_inc(wtr_kept, 1)
            own.leave(back, KC)
            split(TILES - 1, 0)
            dve.wait_ge(xp_low, TILES + 3)

            for h in range(HEADS):
                last = nc.vector.tensor_tensor_scan(segmax[:, :, h], fence[:, :], asrc[:, 0:EC, h], -BIG, ALU.add, ALU.max)
            own.link(last)
            nc.vector.tensor_copy(ends[:, 0, :], segmax[:, EC - 1, :])
            nc.vector.tensor_copy(ends[:, 1, :], dstf[:, 0:1].to_broadcast([P, HEADS]))
            nc.vector.tensor_copy(ends[:, 2, :], dstf[:, EC - 1:EC].to_broadcast([P, HEADS])).then_inc(ends_ready, 1)
            dve.wait_ge(erow_done, 1)
            own.link(nc.vector.tensor_copy(erow[:, :, :].rearrange("h a p -> h (a p)"), g_ps[0:HEADS, 0:3 * P]))
            nc.vector.memset(joins[:, 0:1], 0.0)
            own.link(nc.vector.tensor_tensor(out=joins[:, 1:P], in0=erow[:, 1, 1:P], in1=erow[:, 2, 0:P - 1], op=ALU.is_equal))
            own.link(nc.vector.tensor_tensor(out=whole[:, :], in0=erow[:, 1, :], in1=erow[:, 2, :], op=ALU.is_equal))
            own.link(nc.vector.tensor_tensor(out=whole[:, :], in0=whole[:, :], in1=joins[:, :], op=ALU.mult))
            own.link(nc.vector.tensor_scalar(whole[:, :], whole[:, :], -1.0, BIG, ALU.add, ALU.mult))
            own.link(nc.vector.tensor_scalar(joins[:, :], joins[:, :], -1.0, BIG, ALU.add, ALU.mult))
            own.link(nc.vector.tensor_tensor_scan(carry[:, :], whole[:, :], erow[:, 0, :], -BIG, ALU.add, ALU.max))
            own.link(nc.vector.memset(cin[:, 0:1], -BIG))
            nc.vector.tensor_tensor(out=cin[:, 1:P], in0=carry[:, 0:P - 1], in1=joins[:, 1:P], op=ALU.add).then_inc(cin_ready, 1)
            dve.wait_ge(cinT_done, 1)
            own.link(nc.vector.tensor_copy(cinT[:, :], g_ps[:, 512:512 + HEADS]))
            for h in range(HEADS):
                last = nc.vector.tensor_tensor_scan(segmax[:, :, h], fence[:, :], asrc[:, 0:EC, h], cinT[:, h:h + 1],
                                                    ALU.add, ALU.max)
            last.then_inc(segmax_ready, 1)
            nself_v, node_src, node_dst = nself[:, :, :], logits[:, :, 0:HEADS], logits[:, :, HEADS:2 * HEADS]
            own.link(nc.vector.tensor_tensor(out=nself_v, in0=node_src, in1=node_dst, op=ALU.add))
            own.link(nc.vector.scalar_tensor_tensor(out=nself_v, in0=nself_v, scalar=SLOPE, in1=nself_v, op0=ALU.mult, op1=ALU.max))
            nc.vector.tensor_copy(node[:, :, 0:HEADS], node_dst)
            dve.wait_ge(nmax_in, 16 * TILES)
            own.link(nc.vector.tensor_tensor(out=nmax[:, :, :], in0=nmax[:, :, :],
                                             in1=has[:, :].unsqueeze(2).to_broadcast([P, TILES, HEADS]), op=ALU.add))
            own.link(nc.vector.tensor_tensor(out=nmax[:, :, :], in0=nmax[:, :, :], in1=node_src, op=ALU.max))
            own.link(nc.vector.tensor_tensor(out=nmax[:, :, :], in0=nmax[:, :, :], in1=node_dst, op=ALU.add))
            own.link(nc.vector.scalar_tensor_tensor(out=node[:, :, HEADS:2 * HEADS], in0=nmax[:, :, :], scalar=SLOPE,
                                                    in1=nmax[:, :, :], op0=ALU.mult, op1=ALU.max))
            nc.vector.sem_inc(node_ready, 1)
            nc.vector.tensor_tensor(out=nself_v, in0=nself_v, in1=node[:, :, HEADS:2 * HEADS],
                                    op=ALU.subtract).then_inc(nself_ready, 1)
            dve.wait_ge(first_in, 16)
            dve.wait_ge(head_in, 16)
            own.link(nc.vector.tensor_copy(head[:, 0, :], first[:, :]))
            for v in range(2 * HEADS):
                last = nc.vector.tensor_tensor_scan(head[:, :, v], same[:, :], head[:, :, v], 0.0, ALU.mult, ALU.add)
            own.link(last)
            edge = asrc[:, 0:EC, :]
            own.link(nc.vector.tensor_tensor(out=edge, in0=edge, in1=head[:, :, 0:HEADS], op=ALU.add))
            own.link(nc.vector.scalar_tensor_tensor(out=edge, in0=edge, scalar=SLOPE, in1=edge, op0=ALU.mult, op1=ALU.max))
            nc.vector.tensor_tensor(out=edge, in0=edge, in1=head[:, :, HEADS:2 * HEADS], op=ALU.subtract).then_inc(logit_ready, 1)
            dve.wait_ge(rows_in, 16 * 3 * CH)
            for c in range(CH):
                last = nc.vector.tensor_scalar(drow[:, c, :], drow[:, c, :], ntile128[:, c:c + 1], None, ALU.subtract)
            last.then_inc(rows_ready, 1)
            dve.wait_ge(steps_done, 1)
            own.link(nc.vector.tensor_copy(dstT, xp_ps[0][:, SUB * KCOLS:2 * SUB * KCOLS]))
            own.link(nc.vector.scalar_tensor_tensor(out=far, in0=dstT, scalar=-float(P - 1), in1=dstT, op0=ALU.add, op1=ALU.mult))
            own.link(nc.vector.tensor_scalar(far, far, 0.0, float(FAR), ALU.is_gt, ALU.mult))
            nc.vector.tensor_tensor(out=srcT, in0=xp_ps[0][:, 0:SUB * KCOLS], in1=far, op=ALU.add)
            by_head = lambda v, b: numT16[:, :, v:v + HEADS, b].rearrange("p k h -> p h k")
            dve.wait_ge(num_high, 1)
            own.link(nc.vector.tensor_copy(by_head(0, 0), numT[:, :, :]))
            nc.vector.tensor_tensor(out=by_head(HEADS, 0), in0=numT[:, :, :], in1=by_head(0, 0),
                                    op=ALU.subtract).then_inc(num_low, 1)

        @block.scalar
        def _(act):
            act.sem_inc(xp_kept, 3)

            def keep(t, j, n):
                act.wait_ge(xp_done, t + 1 + 3)
                if n is not None:
                    act.wait_ge(xp_out[j], n)
                nc.scalar.activation(own_row[j][:, :], xp_ps[j][:, :], ACT.Copy)
                nc.scalar.activation(xp[j][:, 0, :], xp_ps[j][:, :], ACT.Copy, scale=xp_scale[:, :]).then_inc(xp_kept, 1)

            def keep_w(o):
                act.wait_ge(wtr_done, o + 1 + 1)
                nc.scalar.activation(wdT[:, :, 0, bass.ds(o * P, P)], g_ps[:, :].rearrange("p (c n) -> p c n", n=P),
                                     ACT.Copy, scale=wd_scale[:, :]).then_inc(wd_high, 1)

            act.wait_ge(powers_ready, 1)
            for t in range(3):
                keep(t, t, None)
            keep_w(0)
            with act.Fori(1, KC) as i:
                for j in range(3):
                    keep(3 * i + j, j, 32 * i)
                keep_w(i)
            keep(TILES - 1, 0, 32 * KC)
            act.wait_ge(nself_ready, 1)
            nc.scalar.activation(self_num[:, :, :], nself[:, :, :], ACT.Exp)
            act.wait_ge(segmax_out, 16)
            act.wait_ge(logit_ready, 1)
            nc.scalar.activation(segmax[:, :, :], asrc[:, 0:EC, :], ACT.Exp).then_inc(num_ready, 1)
            act.wait_ge(steps_done, 1)
            for h in range(HEADS):
                half = slice((h % 2) * SUB * KCOLS, (h % 2 + 1) * SUB * KCOLS)
                last = nc.scalar.activation(numT[:, h, :], xp_ps[1 + h // 2][:, half], ACT.Copy, scale=NUM_SCALE)
            last.then_inc(num_high, 1)
            act.wait_ge(num_low, 1)
            nc.scalar.activation(numT[:, :, :], numT16[:, :, 0:HEADS, 0].rearrange("p k h -> p h k"), ACT.Copy)
            nc.scalar.activation(numT16[:, :, HEADS:2 * HEADS, 1], numT16[:, :, HEADS:2 * HEADS, 0], ACT.Copy)

        @block.tensor
        def _(pe):
            pe.sem_inc(xp_done, 3)
            pe.sem_inc(wtr_done, 1)
            pe.sem_inc(wtr_kept, 1)
            pe.wait_ge(largest_ready, 1)
            nc.tensor.transpose(g_ps[0:2, 2 * P:3 * P], largest[:, :], ident[:, :]).then_inc(most_turned, 1)
            pe.wait_ge(most_row_ready, 1)
            nc.tensor.matmul(g_ps[:, 2 * P:2 * P + 2], ones[0:2, :], most_row[:, :], start=True, stop=True).then_inc(most_spread, 1)
            pe.wait_ge(cexc_ready, 1)
            nc.tensor.matmul(g_ps[:, 0:TILES], upper[:, :], count[:, :], start=True, stop=False)
            nc.tensor.matmul(g_ps[:, 0:TILES], ones[:, :], cinc[:, :], start=False, stop=True).then_inc(cum_done, 1)
            pe.wait_ge(tf_ready, 1)
            nc.tensor.matmul(g_ps[:, 512:512 + ET], ones[0:1, :], tf[:, :], start=True, stop=True).then_inc(stair_done, 1)

            def tile(t, j, n):
                pe.wait_ge(xnT_in[j], n)
                pe.wait_ge(xp_low, t + 1)
                for c in range(KC):
                    for half in range(2):
                        last = nc.tensor.matmul(xp_ps[j][:, half * 512:(half + 1) * 512], xnT[j][:, c, :],
                                                w[:, c, half * 512:(half + 1) * 512], start=(c == 0), stop=(c == KC - 1))
                last.then_inc(xp_done, 1)

            pe_tiles = 3
            with pe.Fori(0, KC) as i:
                for j in range(pe_tiles):
                    tile(pe_tiles * i + j, j, 16 * (i + 1))
                pe.wait_ge(plan_read, 1)
                pe.wait_ge(wq_ready, i + 1)
                pe.wait_ge(wtr_kept, i + 1)
                for c in range(KC):
                    last = nc.tensor.transpose(g_ps[:, c * P:(c + 1) * P], wq[:, c * P:(c + 1) * P], ident[:, :])
                last.then_inc(wtr_done, 1)
            tile(TILES - 1, 0, 16 * (KC + 1))

            pe.wait_ge(ends_ready, 1)
            pe.wait_ge(wtr_kept, KC + 1)
            for a in range(3):
                last = nc.tensor.transpose(g_ps[0:HEADS, a * P:(a + 1) * P], ends[:, a, :], ident[:, :])
            last.then_inc(erow_done, 1)
            pe.wait_ge(cin_ready, 1)
            nc.tensor.transpose(g_ps[:, 512:512 + HEADS], cin[:, :], ident[0:HEADS, 0:HEADS]).then_inc(cinT_done, 1)
            pe.wait_ge(rows_ready, 1)
            pe.wait_ge(xp_low, TILES + 3)
            for c in range(CH):
                for u in range(SUB):
                    sub = slice(u * P, (u + 1) * P)
                    at = u * KCOLS + c * P
                    nc.tensor.transpose(xp_ps[0][:, at:at + P], srow[:, c, sub], ident[:, :])
                    nc.tensor.transpose(xp_ps[0][:, SUB * KCOLS + at:SUB * KCOLS + at + P], drow[:, c, sub], ident[:, :])
                    for h in range(HEADS):
                        to = (h % 2) * SUB * KCOLS + at
                        last = nc.tensor.transpose(
                            xp_ps[1 + h // 2][:, to:to + P],
                            nrow[:, c, :].rearrange("p (e h) -> p e h", h=HEADS)[:, sub, h], ident[:, :])
            last.then_inc(steps_done, 1)


def aggregate(nc, maker, g):
    tables, srcT, dstT, numT, numT16, tile_row, acc, zsum, d_xp = (
        g[k] for k in ("tables", "srcT", "dstT", "numT", "numT16", "tile_row", "acc", "zsum", "d_xp"))
    TURN = 4
    V = 2 * HEADS
    ctx = ExitStack()
    with ctx:
        sb, ps, sem = maker(ctx)
        iota16 = sb("iota16", [P, P], F16)
        idx = [sb(f"sidx{j}", [P, SUB], I32) for j in range(TURN)]
        xg = [[sb(f"xg{j}_{u}", [P, 2, D], F16) for u in range(SUB)] for j in range(TURN)]
        hot = [[sb(f"hot{j}_{u}", [P, P], F16) for u in range(SUB)] for j in range(TURN)]
        wgt = [[sb(f"wgt{j}_{u}", [P, V, P], F16) for u in range(SUB)] for j in range(2)]
        sum_ps = [ps(f"sum_ps{j}", [P, D]) for j in range(2)]
        z_ps = [ps(f"z_ps{j}", [P, 512]) for j in range(2)]

        iota_made = sem("iota_made")
        cleared = sem("cleared")
        idx_ready = sem("sidx_ready")
        arrived = [sem(f"arrived{j}") for j in range(TURN)]
        hot_ready = sem("hot_ready")
        low_ready = sem("low_ready")
        high_ready = sem("high_ready")
        mm_done = sem("mm_done")
        added = sem("added")
        pool_turn = sem("pool_turn3")
        block = ctx.enter_context(nc.Block())
        flat = acc[:, :, :].rearrange("p t n -> p (t n)")
        cut = TILES * D // 2
        col = lambda table, u, k, n=1: table.rearrange("p (u k) -> p u k", u=SUB)[:, u, bass.ds(k, n)]

        @block.gpsimd
        def _(pool):
            def gather(s):
                for u in range(SUB):
                    nc.gpsimd.indirect_dma_start(
                        out=xg[s][u][:, :, :].rearrange("p a n -> p (a n)"), out_offset=None, in_=d_xp,
                        in_offset=bass.IndirectOffsetOnAxis(ap=idx[s][:, u:u + 1], axis=0),
                        bounds_check=NP - 1, oob_is_err=False).then_inc(arrived[s], 16)

            def refill(k, s):
                pool.wait_ge(idx_ready, k + 1)
                pool.wait_ge(mm_done, SUB * (k + 1))
                pool.sem_inc(pool_turn, 1)
                gather(s)

            nc.gpsimd.iota(iota16[:, :], pattern=[[1, P]], base=0, channel_multiplier=0,
                           allow_small_or_imprecise_dtypes=True).then_inc(iota_made, 1)
            pool.wait_ge(idx_ready, TURN)
            for s in range(TURN):
                gather(s)
            nc.gpsimd.memset(flat[:, cut:], 0.0).then_inc(cleared, 1)
            with pool.Fori(1, STEPS // TURN) as i:
                for j in range(TURN):
                    refill(TURN * i + j, j)

        @block.vector
        def _(dve):
            def indices(k):
                return srcT.rearrange("p (u k) -> p u k", u=SUB)[:, :, bass.ds(k, 1)].rearrange("p u o -> p (u o)")

            def one_hots(k, j):
                dve.wait_ge(mm_done, SUB * (k + 1))
                for u in range(SUB):
                    nc.vector.tensor_scalar(hot[j][u][:, :], iota16[:, :], col(dstT, u, k), None,
                                            ALU.is_equal).then_inc(hot_ready, 1)

            def weights(k, j, s):
                for u in range(SUB):
                    dve.wait_ge(hot_ready, SUB * k + u + 1)
                    dve.wait_ge(mm_done, SUB * (k + 2) + u + 1)
                    nc.vector.tensor_tensor(
                        out=wgt[s][u][:, HEADS:V, :].rearrange("p v (n b) -> p v n b", b=2),
                        in0=hot[j][u][:, :].rearrange("p (n b) -> p n b", b=2).unsqueeze(1).to_broadcast([P, HEADS, P // 2, 2]),
                        in1=numT16[:, bass.ds(u * KCOLS + k, 1), HEADS:V, :].rearrange("p o v b -> p (o v) b").unsqueeze(2)
                        .to_broadcast([P, HEADS, P // 2, 2]), op=ALU.mult).then_inc(low_ready, 1)

            for k in range(TURN):
                nc.vector.tensor_scalar(idx[k][:, :], indices(k), NP - 1, None, ALU.min).then_inc(idx_ready, 1)
            dve.wait_ge(iota_made, 1)
            one_hots(0, 0)
            one_hots(1, 1)
            weights(0, 0, 0)
            nc.vector.memset(flat[:, 0:cut], 0.0)
            nc.vector.memset(zsum[:, :, :], 0.0).then_inc(cleared, 1)
            dve.wait_ge(cleared, 2)
            with dve.Fori(0, STEPS // TURN) as i:
                for j in range(TURN):
                    k = TURN * i + j
                    one_hots(k + 2, (j + 2) % TURN)
                    weights(k + 1, (j + 1) % TURN, (j + 1) % 2)
                    t = dve.value_load(tile_row[0:1, bass.ds(k, 1)], min_val=0, max_val=TILES - 1)
                    dve.wait_ge(mm_done, SUB * (k + 1 + TURN))
                    nc.vector.tensor_copy(idx[j][:, :], indices(k + TURN)).then_inc(idx_ready, 1)
                    dve.wait_ge(added, k + 2)
                    s_acc = acc[:, bass.ds(t, 1), :].rearrange("p o n -> p (o n)")
                    z_acc = zsum[:, bass.ds(t, 1), :].rearrange("p o n -> p (o n)")
                    nc.vector.tensor_tensor(out=z_acc, in0=z_ps[j % 2][:, 0:V], in1=z_acc, op=ALU.add)
                    nc.vector.tensor_tensor(out=s_acc, in0=sum_ps[j % 2][:, :], in1=s_acc, op=ALU.add).then_inc(added, 1)

        @block.scalar
        def _(act):
            with act.Fori(0, STEPS // TURN) as i:
                for j in range(TURN):
                    k = TURN * i + j
                    for u in range(SUB):
                        act.wait_ge(hot_ready, SUB * k + u + 1)
                        act.wait_ge(mm_done, SUB * (k + 2) + u + 1)
                        for h in range(HEADS):
                            last = nc.scalar.activation(wgt[j % 2][u][:, h, :], hot[j][u][:, :], ACT.Copy,
                                                        scale=col(numT[:, h, :], u, k))
                        last.then_inc(high_ready, 1)

        @block.tensor
        def _(pe):
            pe.sem_inc(mm_done, SUB * TURN)
            pe.sem_inc(added, 2)
            with pe.Fori(0, STEPS // TURN) as i:
                for j in range(TURN):
                    k, s = TURN * i + j, j % 2
                    pe.wait_ge(arrived[j], 16 * SUB * (i + 1))
                    pe.wait_ge(added, k + 1)
                    for u in range(SUB):
                        pe.wait_ge(high_ready, SUB * k + u + 1)
                        pe.wait_ge(low_ready, SUB * k + u + 1)
                        nc.tensor.matmul(z_ps[s][:, 0:V], hot[j][u][:, :],
                                         numT16[:, bass.ds(u * KCOLS + k, 1), :, 0].rearrange("p o v -> p (o v)"),
                                         start=(u == 0), stop=(u == SUB - 1))
                        for h in range(HEADS):
                            for n, (a, b) in enumerate(((0, 0), (0, 1), (1, 0))):
                                last = nc.tensor.matmul(
                                    sum_ps[s][:, h * C:(h + 1) * C], wgt[s][u][:, a * HEADS + h, :],
                                    xg[j][u][:, b, h * C:(h + 1) * C],
                                    start=(u == 0 and h % 2 == 0 and n == 0), stop=(u == SUB - 1 and h % 2 == 1 and n == 2),
                                    skip_group_check=True)
                        last.then_inc(mm_done, 1)


def finish(nc, maker, g):
    x, gnn_bias, ffn_bias, out, d_own = (g[k] for k in ("x", "gnn_bias", "ffn_bias", "out", "d_own"))
    ident, self_num, wdT, acc, zsum, tables = (g[k] for k in ("ident", "self_num", "wdT", "acc", "zsum", "tables"))
    xp_inverse, wd_inverse = g["xp_inverse"], g["wd_inverse"]
    LAST = TILES - 1
    ctx = ExitStack()
    with ctx:
        sb, ps, sem = maker(ctx)
        h1 = [tables[:, j * D:(j + 1) * D] for j in range(2)]
        xn = [tables[:, j * D:(j + 1) * D] for j in range(2, 4)]
        xqT = [tables[:, j * D:(j + 1) * D].bitcast(F16).rearrange("p (v c n) -> p v c n", v=2, c=KC) for j in range(4, 6)]
        step = tables[:, 6 * D:7 * D]
        biasb = sb("biasb", [P, 2, D])
        z32 = sb("z32", [P, TILES, HEADS])
        inv_z = sb("inv_z", [P, TILES, HEADS])
        acc_w = sb("acc_w", [P, TILES, HEADS])
        self_w = sb("self_w", [P, TILES, HEADS])
        out_scale = sb("out_scale", [P, 1])
        xr = [sb(f"xr{j}", [P, D]) for j in range(2)]
        own_row = [sb(f"own_row{j}", [P, D]) for j in range(2)]
        lin = [sb(f"lin{j}", [P, D]) for j in range(2)]
        stats = sb("fstats", [P, 2, 6])
        mv = [sb(f"fmv{j}", [P, 2]) for j in range(2)]
        std = [sb(f"fstd{j}", [P, 1]) for j in range(2)]
        rstd = [sb(f"frstd{j}", [P, 1]) for j in range(2)]
        shift = [sb(f"fshift{j}", [P, 1]) for j in range(2)]
        newton = sb("fnewton", [P, 1])
        scale = [sb(f"fscale{j}", [P, QB]) for j in range(2)]
        inv = [sb(f"finv{j}", [P, QB]) for j in range(2)]
        tr_ps = [ps(f"ftr_ps{j}", [P, D]) for j in range(2)]
        mm_ps = [ps(f"fmm_ps{j}", [P, D]) for j in range(2)]

        bias_in = sem("bias_in")
        x_in = [sem(f"fx_in{j}") for j in range(2)]
        own_in = [sem(f"own_in{j}") for j in range(2)]
        ratios_ready = sem("ratios_ready")
        own_scaled = sem("own_scaled")
        own_biased = sem("own_biased")
        mixed = sem("mixed")
        x1_ready = sem("x1_ready")
        x1b_ready = sem("x1b_ready")
        var_ready = sem("fvar_ready")
        std_ready = sem("fstd_ready")
        rstd_ready = sem("frstd_ready")
        xn_ready = sem("fxn_ready")
        scales_ready = sem("scales_ready")
        y_ready = sem("y_ready")
        grid_ready = sem("grid_ready")
        xq_ready = sem("xq_ready")
        tr_done = sem("ftr_done")
        high_ready = sem("fhigh_ready")
        low_ready = sem("flow_ready")
        mm_done = sem("fmm_done")
        lin_ready = sem("lin_ready")
        summed = sem("summed")
        stored = [sem(f"stored{j}") for j in range(2)]
        dve_own = sem("dve_own4")
        dve_turn = sem("dve_turn4")
        pool_turn = sem("pool_turn4")
        block = ctx.enter_context(nc.Block())
        kept = lambda t: acc[:, bass.ds(t, 1), :].rearrange("p o n -> p (o n)")

        @block.sync
        def _(sp):
            sp.dma_start(biasb[:, 0, :], gnn_bias.partition_broadcast(P)).then_inc(bias_in, 16)
            sp.dma_start(biasb[:, 1, :], ffn_bias.partition_broadcast(P)).then_inc(bias_in, 16)

            def load(t, j, n=P):
                sp.wait_ge(x1_ready, t + 1)
                sp.dma_start(own_row[j][:, :], d_own[bass.ds(t * P, P), :]).then_inc(own_in[j], 16)
                sp.dma_start(xr[j][0:n, :], x[bass.ds(t * P, n), :]).then_inc(x_in[j], 16)

            def store(t, j, n=P):
                sp.wait_ge(summed, t + 1)
                sp.dma_start(out[bass.ds(t * P, n), :], lin[j][0:n, :]).then_inc(stored[j], 16)

            for t in range(6):
                load(t, t % 2)
            with sp.Fori(0, TILES // 2 - 3) as i:
                for j in range(2):
                    store(2 * i + j, j)
                    load(2 * i + j + 6, j)
            store(LAST - 6, 0)
            load(LAST, 0, LAST_ROWS)
            for t in range(LAST - 5, LAST + 1):
                store(t, t % 2, P if t < LAST else LAST_ROWS)
            sp.wait_ge(stored[0], 16 * (TILES // 2 + 1))
            sp.wait_ge(stored[1], 16 * (TILES // 2))

        @block.gpsimd
        def _(pool):
            def bias(t, j):
                pool.wait_ge(own_scaled, t + 1)
                nc.gpsimd.tensor_tensor(out=own_row[j][:, :], in0=own_row[j][:, :], in1=biasb[:, 0, :],
                                        op=ALU.add).then_inc(own_biased, 1)

            def unscale(t, j):
                pool.wait_ge(scales_ready, t + 1)
                nc.gpsimd.tensor_tensor(out=blocks(xn[j]), in0=blocks(xn[j]), in1=spread(inv[j][:, :]),
                                        op=ALU.mult).then_inc(y_ready, 1)

            def rescale(t, j):
                pool.wait_ge(grid_ready, t + 1)
                nc.gpsimd.tensor_tensor(out=blocks(xn[j]), in0=blocks(xn[j]), in1=spread(scale[j][:, :]),
                                        op=ALU.mult).then_inc(xq_ready, 1)

            def residual(t, j):
                pool.wait_ge(x1_ready, t + 1 + SLOTS)
                pool.sem_inc(pool_turn, 1)
                nc.gpsimd.tensor_tensor(out=kept(t), in0=h1[j], in1=biasb[:, 1, :], op=ALU.add).then_inc(x1b_ready, 1)

            def total(t, j):
                pool.wait_ge(x1b_ready, t + 1 + SLOTS)
                pool.wait_ge(lin_ready, t + 1 + SLOTS)
                pool.sem_inc(pool_turn, 1)
                nc.gpsimd.tensor_tensor(out=lin[j][:, :], in0=lin[j][:, :], in1=kept(t), op=ALU.add).then_inc(summed, 1)

            pool.sem_inc(x1b_ready, SLOTS)
            pool.wait_ge(bias_in, 32)
            bias(0, 0)
            bias(1, 1)
            residual(0, 0)

            def turn(t, j):
                unscale(t, j)
                bias(t + 2, j)
                total(t - 3, 1 - j)
                rescale(t, j)
                residual(t + 1, 1 - j)

            for t in range(4):
                unscale(t, t % 2)
                bias(t + 2, t % 2)
                if t == 3:
                    total(0, 0)
                rescale(t, t % 2)
                residual(t + 1, (t + 1) % 2)
            with pool.Fori(2, TILES // 2 - 1) as i:
                for j in range(2):
                    turn(2 * i + j, j)
            turn(LAST - 2, 0)
            unscale(LAST - 1, 1)
            total(LAST - 4, 0)
            rescale(LAST - 1, 1)
            residual(LAST, 0)
            unscale(LAST, 0)
            total(LAST - 3, 1)
            rescale(LAST, 0)
            for t in range(LAST - 2, LAST + 1):
                total(t, t % 2)

        @block.vector
        def _(dve):
            own = Chain(dve, dve_own)
            dve.sem_inc(x1_ready, SLOTS)
            own.link(nc.vector.tensor_tensor(out=z32[:, :, :], in0=zsum[:, :, 0:HEADS], in1=zsum[:, :, HEADS:2 * HEADS], op=ALU.add))
            own.link(nc.vector.scalar_tensor_tensor(out=z32[:, :, :], in0=z32[:, :, :], scalar=1.0 / NUM_SCALE,
                                                    in1=self_num[:, :, :], op0=ALU.mult, op1=ALU.add))
            own.link(nc.vector.reciprocal(inv_z[:, :, :], z32[:, :, :]))
            nc.vector.tensor_scalar(acc_w[:, :, :], inv_z[:, :, :], xp_inverse[:, :], 1.0 / NUM_SCALE, ALU.mult, ALU.mult)
            nc.vector.tensor_scalar(out_scale[:, :], wd_inverse[:, :], 1.0 / ROW_SCALE, None, ALU.mult)
            own.link(nc.vector.tensor_tensor(out=self_w[:, :, :], in0=self_num[:, :, :], in1=inv_z[:, :, :], op=ALU.mult))
            dve.sem_inc(ratios_ready, 1)

            def mix(t, j):
                dve.wait_ge(own_biased, t + 1)
                dve.wait_ge(x1b_ready, t + 1)
                for h in range(HEADS):
                    cols = slice(h * C, (h + 1) * C)
                    last = nc.vector.scalar_tensor_tensor(
                        out=h1[j][:, cols], in0=acc[:, bass.ds(t, 1), cols].rearrange("p o n -> p (o n)"),
                        scalar=acc_w[:, bass.ds(t, 1), h:h + 1].rearrange("p o h -> p (o h)"),
                        in1=own_row[j][:, cols], op0=ALU.mult, op1=ALU.add)
                last.then_inc(mixed, 1)

            def x1(t, j, n):
                dve.wait_ge(mixed, t + 1)
                dve.wait_ge(x_in[j], 16 * (n + 1))
                nc.vector.scalar_tensor_tensor(out=h1[j], in0=h1[j], scalar=0.0, in1=xr[j][:, :], op0=ALU.max,
                                               op1=ALU.add).then_inc(x1_ready, 1)
                dve.wait_ge(x1_ready, t + 1 + SLOTS)
                nc.vector.bn_stats(stats[:, 0, :], h1[j][:, 0:512])
                own.link(nc.vector.bn_stats(stats[:, 1, :], h1[j][:, 512:1024]))
                dve.sem_inc(dve_turn, 1)
                own.link(nc.vector.bn_aggr(mv[j][:, :], stats[:, :, :].rearrange("p a b -> p (a b)")))
                nc.vector.tensor_scalar(mv[j][:, 1:2], mv[j][:, 1:2], EPS, None, ALU.add).then_inc(var_ready, 1)

            def root(t, j):
                dve.wait_ge(std_ready, t + 1)
                inverse_root(nc, own, std[j][:, :], mv[j][:, 1:2], rstd[j][:, :], newton[:, :])
                nc.vector.scalar_tensor_tensor(out=shift[j][:, :], in0=mv[j][:, 0:1], scalar=-1.0, in1=rstd[j][:, :],
                                               op0=ALU.mult, op1=ALU.mult).then_inc(rstd_ready, 1)

            def scales(t, j):
                dve.wait_ge(xn_ready, t + 1)
                block_scales(nc, own, xn[j], scale[j][:, :], inv[j][:, :]).then_inc(scales_ready, 1)

            def grid(t, j):
                dve.wait_ge(y_ready, t + 1)
                round_to_grid(nc, own, xn[j], step).then_inc(grid_ready, 1)

            def low(t, j):
                dve.wait_ge(high_ready, t + 1 + SLOTS)
                nc.vector.scalar_tensor_tensor(
                    out=xqT[j][:, 1, :, :].rearrange("p c n -> p (c n)"), in0=tr_ps[j][:, :], scalar=ROW_SCALE,
                    in1=xqT[j][:, 0, :, :].rearrange("p c n -> p (c n)"), op0=ALU.mult, op1=ALU.subtract).then_inc(low_ready, 1)

            def turn(t, j, n, first=False, last=False):
                if not last:
                    mix(t + 1, 1 - j)
                scales(t, j)
                if not last:
                    x1(t + 1, 1 - j, n)
                if not first:
                    low(t - 1, 1 - j)
                grid(t, j)
                if not last:
                    root(t + 1, 1 - j)

            mix(0, 0)
            x1(0, 0, 0)
            root(0, 0)
            turn(0, 0, 0, first=True)
            links = STAT_LINKS + ROOT_LINKS + SCALE_LINKS + ROUND_LINKS
            with dve.Fori(0, TILES // 2 - 1) as i:
                back = own.enter(i, 2 * links)
                turn(2 * i + 1, 1, i + 1)
                turn(2 * i + 2, 0, i + 1)
            own.leave(back, TILES // 2 - 1)
            turn(LAST - 1, 1, TILES // 2)
            turn(LAST, 0, None, last=True)
            low(LAST, 0)

        @block.scalar
        def _(act):
            act.sem_inc(high_ready, SLOTS)
            act.sem_inc(lin_ready, SLOTS)
            act.wait_ge(ratios_ready, 1)

            def scale_own(t, j, n):
                act.wait_ge(own_in[j], 16 * (n + 1))
                for h in range(HEADS):
                    cols = slice(h * C, (h + 1) * C)
                    last = nc.scalar.activation(own_row[j][:, cols], own_row[j][:, cols], ACT.Copy,
                                                scale=self_w[:, bass.ds(t, 1), h:h + 1].rearrange("p o h -> p (o h)"))
                last.then_inc(own_scaled, 1)

            def norm(t, j):
                act.wait_ge(var_ready, t + 1)
                nc.scalar.activation(std[j][:, :], mv[j][:, 1:2], ACT.Sqrt).then_inc(std_ready, 1)
                act.wait_ge(tr_done, t + 1)
                act.wait_ge(rstd_ready, t + 1)
                nc.scalar.activation(xn[j], h1[j], ACT.Identity, bias=shift[j][:, :], scale=rstd[j][:, :]).then_inc(xn_ready, 1)

            def high(t, j):
                act.wait_ge(tr_done, t + 1 + SLOTS)
                act.wait_ge(mm_done, t + 1)
                nc.scalar.activation(xqT[j][:, 0, :, :].rearrange("p c n -> p (c n)"), tr_ps[j][:, :], ACT.Copy,
                                     scale=ROW_SCALE).then_inc(high_ready, 1)

            def linear(t, j, n):
                act.wait_ge(mm_done, t + 1 + SLOTS)
                if n is not None:
                    act.wait_ge(stored[j], n)
                nc.scalar.activation(lin[j][:, :], mm_ps[j][:, :], ACT.Copy, scale=out_scale[:, :]).then_inc(lin_ready, 1)

            scale_own(0, 0, 0)
            scale_own(1, 1, 0)
            norm(0, 0)

            for t in range(6):
                if t >= 1:
                    high(t - 1, (t - 1) % 2)
                if t >= 3:
                    linear(t - 3, (t - 3) % 2, 16 if t == 5 else None)
                scale_own(t + 2, t % 2, t // 2 + 1)
                norm(t + 1, (t + 1) % 2)
            with act.Fori(3, TILES // 2 - 1) as i:
                for j in range(2):
                    t = 2 * i + j
                    high(t - 1, 1 - j)
                    linear(t - 3, 1 - j, 16 * (i - 2 + j))
                    scale_own(t + 2, j, i + 1)
                    norm(t + 1, 1 - j)
            for t in range(LAST - 2, LAST + 1):
                high(t - 1, (t - 1) % 2)
                linear(t - 3, (t - 3) % 2, 16 * ((t - 3) // 2))
                if t + 2 <= LAST:
                    scale_own(t + 2, t % 2, t // 2 + 1)
                if t + 1 <= LAST:
                    norm(t + 1, (t + 1) % 2)
            high(LAST, 0)
            for t in range(LAST - 2, LAST + 1):
                linear(t, t % 2, 16 * (t // 2))

        @block.tensor
        def _(pe):
            pe.sem_inc(tr_done, SLOTS)
            pe.sem_inc(mm_done, SLOTS)

            def turned(t, j):
                pe.wait_ge(xq_ready, t + 1)
                for c in range(KC):
                    last = nc.tensor.transpose(tr_ps[j][:, c * P:(c + 1) * P], xn[j][:, c * P:(c + 1) * P], ident[:, :])
                last.then_inc(tr_done, 1)

            def products(t, j):
                pe.wait_ge(low_ready, t + 1)
                pe.wait_ge(lin_ready, t + 1)
                for c in range(KC):
                    for a, b in ((0, 0), (0, 1), (1, 0)):
                        for half in range(2):
                            cols = slice(half * 512, (half + 1) * 512)
                            last = nc.tensor.matmul(mm_ps[j][:, cols], xqT[j][:, a, c, :], wdT[:, c, b, cols],
                                                    start=(c == 0 and a + b == 0), stop=(c == KC - 1 and a == 1))
                last.then_inc(mm_done, 1)

            turned(0, 0)
            with pe.Fori(0, TILES // 2) as i:
                for j in range(2):
                    turned(2 * i + j + 1, 1 - j)
                    products(2 * i + j, j)
            products(LAST, 0)


_INS = ['x', 'src', 'dst', 'L0_gnn_W', 'L0_gnn_att_src', 'L0_gnn_att_dst', 'L0_gnn_bias', 'L0_ffn_weight', 'L0_ffn_bias']


def kernel(**inputs):
    import numpy as _np
    import concourse.bacc as _bacc
    from concourse import mybir as _mybir
    from concourse.bass_utils import run_bass_kernel_spmd as _run

    nc = _bacc.Bacc("TRN2", target_bir_lowering=False, num_devices=1)
    arrays, args = {}, []
    for name in _INS:
        a = _np.ascontiguousarray(inputs[name])
        arrays[f"in_{name}_dram"] = a
        args.append(nc.dram_tensor(f"in_{name}_dram", a.shape, _mybir.dt.from_np(a.dtype), kind="ExternalInput").ap())
    args.append(nc.dram_tensor("out_0_dram", (N, D), F32, kind="ExternalOutput").ap())
    program(nc, *args)
    r = _run(nc, [arrays], core_ids=[0])
    return r.results[0]["out_0_dram"]
```

```python
import concourse.bass as bass
from concourse import mybir
from contextlib import ExitStack

F32 = mybir.dt.float32
BF16 = mybir.dt.bfloat16
I32 = mybir.dt.int32
ALU = mybir.AluOpType
ACT = mybir.ActivationFunctionType
AX = mybir.AxisListType

P = 128
N = 3125
D = 1024
E = 50000
HEADS = 4
C = D // HEADS
KC = D // P
TILES = -(-N // P)
NP = TILES * P
LAST_ROWS = N - (TILES - 1) * P
SUB = 2
ET = -(-E // (SUB * P))
EC = ET * SUB
EP = EC * P
STEPS = -(-(ET + TILES - 1) // 4) * 4
KCOLS = 2 * P
assert STEPS <= KCOLS
HCOLS = 17
HBATCH = 24
HPAD = HCOLS * HBATCH
GCOLS = 7
GSLOTS = 7
GFILLS = 56
assert GCOLS * GFILLS >= EC
GPAD = GCOLS * (GFILLS + GSLOTS)
BIG = 1e38
FAR = 1 << 20
SLOTS = 2
EPS = 1e-5
SLOPE = 0.2
QBLOCK = 32
QB = D // QBLOCK
QMAX = 7.5
EXPONENT = 0x7F800000
F16 = mybir.dt.float16
NUM_SCALE = 2.0 ** 14
ROW_SCALE = 2.0 ** 9


class Chain:

    def __init__(self, eng, sem):
        self.eng, self.sem, self.base, self.n = eng, sem, 0, 0

    def mark(self, ins):
        ins.then_inc(self.sem, 1)
        self.n += 1
        return self.base + self.n

    def until(self, count):
        self.eng.wait_ge(self.sem, count)

    def link(self, ins):
        self.until(self.mark(ins))

    def enter(self, i, per):
        back = (self.base, self.n, per)
        self.base = i * per + (self.base + self.n)
        self.n = 0
        return back

    def leave(self, back, turns):
        base, n, per = back
        assert self.n == per, (self.n, per)
        self.base, self.n = base, n + per * turns


def blocks(a):
    return a.rearrange("p (b k) -> p b k", k=QBLOCK)


def spread(a):
    return a.unsqueeze(2).to_broadcast([P, QB, QBLOCK])


def block_scales(nc, chain, src, scale, inv):
    chain.link(nc.vector.tensor_reduce(out=scale, in_=blocks(src), axis=AX.X, op=ALU.max, apply_absolute_value=True))
    chain.link(nc.vector.tensor_scalar(scale, scale, 1.0 / QMAX, 1e-30, ALU.mult, ALU.max))
    return nc.vector.reciprocal(inv, scale)


def round_to_grid(nc, chain, y, step):
    chain.link(nc.vector.tensor_scalar(step.bitcast(I32), y.bitcast(I32), EXPONENT, None, ALU.bitwise_and))
    chain.link(nc.vector.tensor_scalar(step, step, 1.0, None, ALU.max))
    chain.link(nc.vector.scalar_tensor_tensor(out=y, in0=step, scalar=6.0625, in1=y, op0=ALU.mult, op1=ALU.subtract))
    chain.link(nc.vector.tensor_scalar(y.bitcast(I32), y.bitcast(I32), -(1 << 18), None, ALU.bitwise_and))
    return nc.vector.scalar_tensor_tensor(out=y, in0=step, scalar=6.0, in1=y, op0=ALU.mult, op1=ALU.subtract)


SCALE_LINKS = 2
ROUND_LINKS = 4


def power_scale(nc, chain, largest, low, scale, inverse, top):
    chain.link(nc.vector.tensor_scalar(low, largest, 2.0 ** -100, None, ALU.max))
    chain.link(nc.vector.tensor_scalar(low.bitcast(I32), low.bitcast(I32), EXPONENT, None, ALU.bitwise_and))
    chain.link(nc.vector.tensor_scalar(scale.bitcast(I32), low.bitcast(I32), -1.0, float((254 + top) << 23), ALU.mult, ALU.add))
    chain.link(nc.vector.tensor_scalar(inverse.bitcast(I32), low.bitcast(I32), float(-(top << 23)), None, ALU.add))


def inverse_root(nc, chain, root, value, out, tmp):
    chain.link(nc.vector.reciprocal(out, root))
    chain.link(nc.vector.tensor_scalar(tmp, out, out, value, ALU.mult, ALU.mult))
    chain.link(nc.vector.tensor_scalar(tmp, tmp, -0.5, 1.5, ALU.mult, ALU.add))
    chain.link(nc.vector.tensor_tensor(out=out, in0=out, in1=tmp, op=ALU.mult))


STAT_LINKS = 2
ROOT_LINKS = 4


def program(nc, x, src, dst, W, att_src, att_dst, gnn_bias, ffn_w, ffn_bias, out):
    d_xnT = nc.dram_tensor("d_xnT", (TILES, P, D), F32, kind="Internal").ap()
    d_xp = nc.dram_tensor("d_xp", (NP, 2 * D), F16, kind="Internal").ap()
    d_own = nc.dram_tensor("d_own", (NP, D), F32, kind="Internal").ap()
    d_asrc = nc.dram_tensor("d_asrc", (NP, HEADS), F32, kind="Internal").ap()
    d_node = nc.dram_tensor("d_node", (NP, 2 * HEADS), F32, kind="Internal").ap()
    d_src = nc.dram_tensor("d_src", (ET, SUB * P), F32, kind="Internal").ap()
    d_dst = nc.dram_tensor("d_dst", (ET, SUB * P), F32, kind="Internal").ap()
    d_segmax = nc.dram_tensor("d_segmax", (EP, HEADS), F32, kind="Internal").ap()
    d_head = nc.dram_tensor("d_head", (EP, 2 * HEADS), F32, kind="Internal").ap()
    d_num = nc.dram_tensor("d_num", (ET, SUB * P * HEADS), F32, kind="Internal").ap()
    d_tile = nc.dram_tensor("d_tile", (KCOLS,), I32, kind="Internal").ap()

    whole = ExitStack()

    def maker(ctx):
        def sb(name, shape, dt=F32):
            return ctx.enter_context(nc.sbuf_tensor(name, shape, dt))

        def ps(name, shape, dt=F32):
            return ctx.enter_context(nc.psum_tensor(name, shape, dt))

        def sem(name):
            return ctx.enter_context(nc.semaphore(name))
        return sb, ps, sem

    with whole:
        sb, ps, sem = maker(whole)
        ident = sb("ident", [P, P])
        logits = sb("logits", [P, TILES, 2 * HEADS])
        self_num = sb("self_num", [P, TILES, HEADS])
        tables = sb("tables", [P, 14 * SUB * KCOLS])
        part = lambda a, b: tables[:, a * SUB * KCOLS:b * SUB * KCOLS]
        dstT = part(0, 1)
        srcT = part(1, 2).bitcast(I32)
        numT = part(2, 6).rearrange("p (h k) -> p h k", h=HEADS)
        numT16 = part(6, 14).bitcast(F16).rearrange("p (k v b) -> p k v b", v=2 * HEADS, b=2)
        xp_scale = sb("xp_scale", [P, 1])
        xp_inverse = sb("xp_inverse", [P, 1])
        wd_scale = sb("wd_scale", [P, 1])
        wd_inverse = sb("wd_inverse", [P, 1])
        tile_row = sb("tile_row", [1, KCOLS], I32)
        wdT = sb("wdT", [P, KC, 2, D], F16)
        front = ExitStack()
        with front:
            sb, ps, sem = maker(front)
            w = sb("w", [P, KC, D])
            dst1 = sb("dst1", [P, HPAD], I32)
            src1 = sb("src1", [P, GPAD], I32)
            dfirst = sb("dfirst", [1, ET], I32)
            wf = sb("wf", [P, KC, D])
            largest = sb("largest", [P, 2])
            count = sb("count", [P, TILES])
            ones = sb("ones", [P, P])
            upper = sb("upper", [P, P])
            wf_in = sem("wf_in")
            asrc_out = sem("asrc_out")
            node_out = sem("node_out")
            normalise(nc, maker, locals())
            project(nc, maker, locals())
        back = ExitStack()
        with back:
            sb, ps, sem = maker(back)
            acc = sb("acc", [P, TILES, D])
            zsum = sb("zsum", [P, TILES, 2 * HEADS])
            aggregate(nc, maker, locals())
            finish(nc, maker, locals())


def normalise(nc, maker, g):
    x, src, dst, W, att_src, att_dst = g["x"], g["src"], g["dst"], g["W"], g["att_src"], g["att_dst"]
    ident, logits = g["ident"], g["logits"]
    w, dst1, src1, dfirst, count, ones, upper = (g[k] for k in ("w", "dst1", "src1", "dfirst", "count", "ones", "upper"))
    XS = 4
    ctx = ExitStack()
    with ctx:
        sb, ps, sem = maker(ctx)
        att_row = sb("att_row", [2 * KC, P])
        att_cols = sb("att_cols", [P, KC, 2 * HEADS])
        waT = sb("waT", [2 * HEADS, D])
        logitsT = sb("logitsT", [2 * HEADS, TILES, P])
        wa = sb("wa", [P, KC, 2 * HEADS])
        digit = sb("digit", [P, HPAD], I32)
        dlo = sb("dlo", [P, HPAD, 2], BF16)
        dhi = sb("dhi", [P, HPAD, 2], BF16)
        iota_b = sb("iota_b", [P, P], BF16)
        hot_hi = sb("hot_hi", [P, HPAD, 32], BF16)
        hot_lo = [sb(f"hot_lo{j}", [P, HCOLS, P], BF16) for j in range(2)]
        zeros = g["tables"][:, 0:EC * 2 * HEADS]
        xn = [g["tables"][:, EC * 2 * HEADS + j * D:EC * 2 * HEADS + (j + 1) * D] for j in range(2)]
        room = g["wdT"][:, :, :, :].rearrange("p c a n -> p (c a n)").bitcast(F32)
        xt = [room[:, j * D:(j + 1) * D] for j in range(XS)]
        wT = [room[:, (XS + j) * D:(XS + j + 1) * D] for j in range(2)]
        xnT = [sb(f"xnT{j}", [P, KC, P]) for j in range(2)]
        part_max = sb("part_max", [P, KC])
        stats = sb("stats", [P, 2, 6])
        mv = [sb(f"mv{j}", [P, 2]) for j in range(2)]
        std = [sb(f"std{j}", [P, 1]) for j in range(2)]
        rstd = [sb(f"rstd{j}", [P, 1]) for j in range(2)]
        shift = [sb(f"shift{j}", [P, 1]) for j in range(2)]
        newton = sb("newton", [P, 1])
        tr_ps = [ps(f"tr_ps{j}", [P, D]) for j in range(2)]
        lg_ps = [ps(f"lg_ps{j}", [P, 512]) for j in range(2)]
        hist_ps = ps("hist_ps", [P, 512])
        small_ps = ps("small_ps", [P, 512])

        made = sem("made")
        pads_set = sem("pads_set")
        edges_in = sem("edges_in")
        att_in = sem("att_in")
        w_in = [sem(f"w_in{c}") for c in range(KC)]
        zeroed = sem("zeroed")
        att_turned = sem("att_turned")
        att_kept = sem("att_kept")
        wT_done = sem("wT_done")
        wT_kept = sem("wT_kept")
        wa_done = sem("wa_done")
        waT_kept = sem("waT_kept")
        wa_turned = sem("wa_turned")
        wa_kept = sem("wa_kept")
        logits_turned = sem("logits_turned")
        logits_kept = sem("logits_kept")
        hi_ready = sem("hi_ready")
        lo_ready = sem("lo_ready")
        lo_free = sem("lo_free")
        x_in = [sem(f"x_in{j}") for j in range(XS)]
        var_ready = sem("var_ready")
        std_ready = sem("std_ready")
        rstd_ready = sem("rstd_ready")
        xn_ready = sem("xn_ready")
        tr_done = sem("tr_done")
        xnT_ready = sem("xnT_ready")
        xnT_out = [sem(f"xnT_out{j}") for j in range(2)]
        lg_done = sem("lg_done")
        lg_kept = sem("lg_kept")
        dve_own = sem("dve_own1")
        pool_own = sem("pool_own1")
        dve_turn = sem("dve_turn")
        block = ctx.enter_context(nc.Block())
        TURNS = TILES // XS
        assert TILES == TURNS * XS + 1

        @block.sync
        def _(sp):
            for a, vec in enumerate((att_src, att_dst)):
                sp.dma_start(att_row[a * KC:(a + 1) * KC, :], vec.rearrange("h (u c) -> (h u) c", c=P)).then_inc(att_in, 16)

            def load(t, j, n=P):
                sp.wait_ge(xn_ready, t + 1)
                sp.dma_start(xt[j][0:n, :], x[bass.ds(t * P, n), :]).then_inc(x_in[j], 16)

            sp.wait_ge(pads_set, 2)
            cut = (P - 1) * EC
            for tile, vec in ((dst1, dst), (src1, src)):
                sp.dma_start(tile[0:P - 1, 0:EC], vec[0:cut].rearrange("(p c) -> p c", c=EC)).then_inc(edges_in, 16)
                sp.dma_start(tile[P - 1:P, 0:E - cut], vec[cut:E].unsqueeze(0)).then_inc(edges_in, 16)
            sp.dma_start(dfirst[:, :], dst[0:(ET - 1) * SUB * P + 1:SUB * P].unsqueeze(0),
                         allow_slow_non_contiguous=True).then_inc(edges_in, 16)
            for c in range(KC):
                sp.dma_start(w[:, c, :], W[c * P:(c + 1) * P, :]).then_inc(w_in[c], 16)
                if c % 2:
                    load(c // 2, c // 2)

            def store(t, j):
                sp.wait_ge(xnT_ready, t + 1)
                sp.dma_start(g["d_xnT"][bass.ds(t, 1), :, :].rearrange("o p n -> (o p) n"),
                             xnT[j][:, :, :].rearrange("p c n -> p (c n)")).then_inc(xnT_out[j], 16)

            with sp.Fori(0, TURNS - 1) as i:
                for j in range(XS):
                    load(XS * i + j + XS, j)
                    store(XS * i + j, j % 2)
            load(TILES - 1, 0, LAST_ROWS)
            sp.dma_start(g["wf"][:, :, :], g["ffn_w"].rearrange("(c p) n -> p c n", p=P)).then_inc(g["wf_in"], 16)
            for t in range(TILES - 1 - XS, TILES):
                store(t, t % 2)
            sp.wait_ge(xnT_out[0], 16 * (TILES // 2 + 1))
            sp.wait_ge(xnT_out[1], 16 * (TILES // 2))

        @block.gpsimd
        def _(pool):
            own = Chain(pool, pool_own)
            own.link(nc.gpsimd.memset(ident[:, :], 0.0))
            nc.gpsimd.affine_select(out=ident[:, :], in_=ident[:, :], compare_op=ALU.not_equal, fill=1.0, base=0,
                                    pattern=[[-1, P]], channel_multiplier=1).then_inc(made, 1)
            nc.gpsimd.iota(iota_b[:, :], pattern=[[1, P]], base=0, channel_multiplier=0,
                           allow_small_or_imprecise_dtypes=True).then_inc(made, 1)
            own.link(nc.gpsimd.memset(upper[:, :], 1.0))
            nc.gpsimd.affine_select(out=upper[:, :], in_=upper[:, :], compare_op=ALU.is_ge, fill=0.0, base=0,
                                    pattern=[[1, P]], channel_multiplier=-1)
            own.link(nc.gpsimd.memset(zeros[:, :], 0.0))
            nc.gpsimd.dma_start(g["d_head"].rearrange("(p c) v -> p (c v)", c=EC), zeros[:, :]).then_inc(zeroed, 16)
            pool.wait_ge(zeroed, 16)

        @block.vector
        def _(dve):
            own = Chain(dve, dve_own)
            nc.vector.memset(dst1[:, :], NP - 1).then_inc(pads_set, 1)
            nc.vector.memset(src1[:, :], 0).then_inc(pads_set, 1)
            nc.vector.memset(ones[:, :], 1.0)
            dve.sem_inc(xn_ready, XS)
            own.link(nc.vector.memset(att_cols[:, :, :], 0.0))
            dve.wait_ge(att_turned, 1)
            per = KC // HEADS
            for h in range(HEADS):
                last = nc.vector.tensor_copy(
                    att_cols[:, h * per:(h + 1) * per, h:h + HEADS + 1:HEADS],
                    hist_ps[:, 0:2 * KC].rearrange("p (a c) -> p c a", a=2)[:, h * per:(h + 1) * per, :])
            last.then_inc(att_kept, 1)

            def stat(t, j, n):
                dve.wait_ge(x_in[j], 16 * (n + 1))
                nc.vector.bn_stats(stats[:, 0, :], xt[j][:, 0:512])
                own.link(nc.vector.bn_stats(stats[:, 1, :], xt[j][:, 512:1024]))
                dve.sem_inc(dve_turn, 1)
                own.link(nc.vector.bn_aggr(mv[j % 2][:, :], stats[:, :, :].rearrange("p a b -> p (a b)")))
                nc.vector.tensor_scalar(mv[j % 2][:, 1:2], mv[j % 2][:, 1:2], EPS, None, ALU.add).then_inc(var_ready, 1)

            def root(t, s):
                dve.wait_ge(std_ready, t + 1)
                dve.wait_ge(xn_ready, t + XS - 1)
                inverse_root(nc, own, std[s][:, :], mv[s][:, 1:2], rstd[s][:, :], newton[:, :])
                nc.vector.scalar_tensor_tensor(out=shift[s][:, :], in0=mv[s][:, 0:1], scalar=-1.0, in1=rstd[s][:, :],
                                               op0=ALU.mult, op1=ALU.mult).then_inc(rstd_ready, 1)

            dve.wait_ge(edges_in, 16 * 5)
            own.link(nc.vector.tensor_scalar(digit[:, :], dst1[:, :], P - 1, None, ALU.bitwise_and))
            own.link(nc.vector.tensor_copy(dlo[:, :, :], digit[:, :].unsqueeze(2).to_broadcast([P, HPAD, 2])))
            own.link(nc.vector.memset(dlo[:, EC:HPAD, :], 255.0))
            own.link(nc.vector.tensor_scalar(digit[:, :], dst1[:, :], 7, None, ALU.logical_shift_right))
            own.link(nc.vector.tensor_copy(dhi[:, :, :], digit[:, :].unsqueeze(2).to_broadcast([P, HPAD, 2])))
            dve.wait_ge(made, 2)

            def hots(out, digits, cols, width):
                shape = [P, cols, width // 2, 2]
                return nc.vector.tensor_tensor(
                    out=out.rearrange("p c (n b) -> p c n b", b=2), in0=digits.unsqueeze(2).to_broadcast(shape),
                    in1=iota_b[:, 0:width].rearrange("p (n b) -> p n b", b=2).unsqueeze(1).to_broadcast(shape), op=ALU.is_equal)

            hots(hot_hi[:, :, :], dhi[:, :, :], HPAD, 32).then_inc(hi_ready, 1)

            stat(0, 0, 0)
            for c in range(KC):
                dve.wait_ge(w_in[c], 16)
                last = nc.vector.tensor_reduce(out=part_max[:, c:c + 1], in_=w[:, c, :], axis=AX.X, op=ALU.max,
                                               apply_absolute_value=True)
            own.link(last)
            nc.vector.tensor_reduce(out=g["largest"][:, 0:1], in_=part_max[:, :], axis=AX.X, op=ALU.max)

            def one_hot(b, s):
                dve.wait_ge(lo_free, b + 1)
                hots(hot_lo[s][:, :, :], dlo[:, bass.ds(b * HCOLS, HCOLS), :], HCOLS, P).then_inc(lo_ready, 1)

            def turn(i, j):
                t, s, to = XS * i + j, j % 2, (j + 1) % XS
                mv_to = mv[to % 2]
                dve.wait_ge(x_in[to], 16 * (i + (j + 1) // XS + 1))
                nc.vector.bn_stats(stats[:, 0, :], xt[to][:, 0:512])
                dve.wait_ge(std_ready, t + 1)
                dve.wait_ge(xn_ready, t + XS - 1)
                guess = own.mark(nc.vector.reciprocal(rstd[s][:, :], std[s][:, :]))
                both = own.mark(nc.vector.bn_stats(stats[:, 1, :], xt[to][:, 512:1024]))
                own.until(guess)
                square = own.mark(nc.vector.tensor_scalar(newton[:, :], rstd[s][:, :], rstd[s][:, :], mv[s][:, 1:2], ALU.mult, ALU.mult))
                own.until(square)
                factor = own.mark(nc.vector.tensor_scalar(newton[:, :], newton[:, :], -0.5, 1.5, ALU.mult, ALU.add))
                own.until(both)
                dve.sem_inc(dve_turn, 1)
                moments = own.mark(nc.vector.bn_aggr(mv_to[:, :], stats[:, :, :].rearrange("p a b -> p (a b)")))
                own.until(factor)
                better = own.mark(nc.vector.tensor_tensor(out=rstd[s][:, :], in0=rstd[s][:, :], in1=newton[:, :], op=ALU.mult))
                own.until(moments)
                nc.vector.tensor_scalar(mv_to[:, 1:2], mv_to[:, 1:2], EPS, None, ALU.add).then_inc(var_ready, 1)
                own.until(better)
                nc.vector.scalar_tensor_tensor(out=shift[s][:, :], in0=mv[s][:, 0:1], scalar=-1.0, in1=rstd[s][:, :],
                                               op0=ALU.mult, op1=ALU.mult).then_inc(rstd_ready, 1)
                one_hot(t, s)

            with dve.Fori(0, TURNS) as i:
                back = own.enter(i, XS * (STAT_LINKS + ROOT_LINKS))
                for j in range(XS):
                    turn(i, j)
            own.leave(back, TURNS)
            root(TILES - 1, 0)
            dve.wait_ge(lo_free, SLOTS + HBATCH)
            nc.vector.tensor_copy(count[:, :], hist_ps[:, 0:TILES])

        @block.scalar
        def _(act):
            def root(t, s):
                act.wait_ge(var_ready, t + 1)
                nc.scalar.activation(std[s][:, :], mv[s][:, 1:2], ACT.Sqrt).then_inc(std_ready, 1)

            def norm(t, j):
                act.wait_ge(rstd_ready, t + 1)
                act.wait_ge(tr_done, t + 1)
                nc.scalar.activation(xn[j % 2][:, :], xt[j][:, :], ACT.Identity, bias=shift[j % 2][:, :],
                                     scale=rstd[j % 2][:, :]).then_inc(xn_ready, 1)

            def tile(t, s, n):
                act.wait_ge(tr_done, t + 1 + SLOTS)
                act.wait_ge(lg_done, t + 1)
                if n is not None:
                    act.wait_ge(xnT_out[s], n)
                nc.scalar.activation(xnT[s][:, :, :].rearrange("p c n -> p (c n)"), tr_ps[s][:, :],
                                     ACT.Copy).then_inc(xnT_ready, 1)

            def keep(t, s):
                act.wait_ge(lg_done, t + 1 + SLOTS)
                nc.scalar.activation(logitsT[:, bass.ds(t, 1), :].rearrange("v o n -> v (o n)"), lg_ps[s][0:2 * HEADS, 0:P],
                                     ACT.Copy).then_inc(lg_kept, 1)

            def keep_wa(c):
                act.wait_ge(wa_done, c + 1)
                nc.scalar.activation(waT[:, c * P:(c + 1) * P], lg_ps[c % 2][0:2 * HEADS, 0:P], ACT.Copy).then_inc(waT_kept, 1)

            for c in range(KC):
                act.wait_ge(wT_done, c + 1)
                if c >= 2:
                    act.wait_ge(wa_done, c - 1)
                nc.scalar.activation(wT[c % 2][:, :], tr_ps[c % 2][:, :], ACT.Copy).then_inc(wT_kept, 1)
                if c >= 1:
                    keep_wa(c - 1)
                if c == KC // 2:
                    root(0, 0)
            keep_wa(KC - 1)
            act.wait_ge(wa_turned, 1)
            nc.scalar.activation(wa[:, :, :].rearrange("p c v -> p (c v)"), small_ps[:, 0:KC * 2 * HEADS], ACT.Copy).then_inc(wa_kept, 1)

            def turn(t, j, n, first=None):
                root(t + 1, (j + 1) % 2)
                norm(t, j)
                if first is None or first >= 1:
                    tile(t - 1, (j + 1) % 2, n)
                if first is None or first >= 2:
                    keep(t - 2, j % 2)

            for t in range(XS):
                turn(t, t, 16 if t == 3 else None, first=t)
            with act.Fori(1, TURNS) as i:
                for j in range(XS):
                    turn(XS * i + j, j, 16 * (2 * i + (j - 1) // 2))
            norm(TILES - 1, 0)
            tile(TILES - 2, 1, 16 * (TILES // 2 - 1))
            keep(TILES - 3, 0)
            tile(TILES - 1, 0, 16 * (TILES // 2))
            keep(TILES - 2, 1)
            keep(TILES - 1, 0)
            act.wait_ge(logits_turned, 1)
            nc.scalar.activation(logits[:, :, :].rearrange("p t v -> p (t v)"), small_ps[:, 0:TILES * 2 * HEADS],
                                 ACT.Copy).then_inc(logits_kept, 1)
            act.wait_ge(logits_kept, 1)
            nc.scalar.dma_start(g["d_asrc"].rearrange("(t p) h -> p t h", p=P), logits[:, :, 0:HEADS]).then_inc(g["asrc_out"], 16)
            nc.scalar.dma_start(g["d_node"].rearrange("(t p) v -> p t v", p=P), logits[:, :, :]).then_inc(g["node_out"], 16)

        @block.tensor
        def _(pe):
            pe.sem_inc(tr_done, SLOTS)
            pe.sem_inc(lg_done, SLOTS)
            pe.sem_inc(lo_free, SLOTS)
            pe.wait_ge(made, 2)
            pe.wait_ge(att_in, 32)
            nc.tensor.transpose(hist_ps[:, 0:2 * KC], att_row[:, :], ident[0:2 * KC, 0:2 * KC]).then_inc(att_turned, 1)

            def turn_w(c):
                pe.wait_ge(w_in[c], 16)
                if c >= 2:
                    pe.wait_ge(wT_kept, c - 1)
                for n in range(KC):
                    last = nc.tensor.transpose(tr_ps[c % 2][:, n * P:(n + 1) * P], w[:, c, n * P:(n + 1) * P], ident[:, :])
                last.then_inc(wT_done, 1)

            def apply_w(c):
                pe.wait_ge(wT_kept, c + 1)
                if c >= 2:
                    pe.wait_ge(waT_kept, c - 1)
                for n in range(KC):
                    last = nc.tensor.matmul(lg_ps[c % 2][0:2 * HEADS, 0:P], att_cols[:, n, :], wT[c % 2][:, n * P:(n + 1) * P],
                                            start=(n == 0), stop=(n == KC - 1))
                last.then_inc(wa_done, 1)

            turn_w(0)
            pe.wait_ge(att_kept, 1)
            for c in range(KC):
                if c + 1 < KC:
                    turn_w(c + 1)
                apply_w(c)
            pe.wait_ge(waT_kept, KC)
            for c in range(KC):
                last = nc.tensor.transpose(small_ps[:, c * 2 * HEADS:(c + 1) * 2 * HEADS], waT[:, c * P:(c + 1) * P],
                                           ident[0:2 * HEADS, 0:2 * HEADS])
            last.then_inc(wa_turned, 1)

            def tile(t, s):
                pe.wait_ge(xn_ready, t + 1 + XS)
                for c in range(KC):
                    last = nc.tensor.transpose(tr_ps[s][:, c * P:(c + 1) * P], xn[s][:, c * P:(c + 1) * P], ident[:, :])
                last.then_inc(tr_done, 1)

            def logit(t, s):
                pe.wait_ge(xnT_ready, t + 1)
                for c in range(KC):
                    last = nc.tensor.matmul(lg_ps[s][0:2 * HEADS, 0:P], wa[:, c, :], xnT[s][:, c, :], start=(c == 0),
                                            stop=(c == KC - 1))
                last.then_inc(lg_done, 1)

            def counts(b, s, start, stop):
                pe.wait_ge(lo_ready, b + 1)
                for c in range(HCOLS):
                    last = nc.tensor.matmul(
                        hist_ps[:, 0:32], hot_lo[s][:, c, :],
                        hot_hi[:, bass.ds(b * HCOLS + c, 1), :].rearrange("p o v -> p (o v)"),
                        start=(start and c == 0), stop=(stop and c == HCOLS - 1))
                last.then_inc(lo_free, 1)

            def turn(t, s, start=False, stop=False):
                tile(t + 1, 1 - s)
                counts(t, s, start, stop)
                logit(t, s)

            tile(0, 0)
            pe.wait_ge(wa_kept, 1)
            pe.wait_ge(hi_ready, 1)
            turn(0, 0, start=True)
            turn(1, 1)
            with pe.Fori(1, TILES // 2 - 1) as i:
                for j in range(2):
                    t = 2 * i + j
                    pe.wait_ge(lg_kept, t - 1)
                    turn(t, j)
            for t in range(TILES - 3, TILES - 1):
                pe.wait_ge(lg_kept, t - 1)
                turn(t, t % 2, stop=(t == HBATCH - 1))
            pe.wait_ge(lg_kept, TILES - 2)
            logit(TILES - 1, 0)
            pe.wait_ge(lg_kept, TILES)
            for t in range(TILES):
                last = nc.tensor.transpose(small_ps[:, t * 2 * HEADS:(t + 1) * 2 * HEADS], logitsT[:, t, :],
                                           ident[0:2 * HEADS, 0:2 * HEADS])
            last.then_inc(logits_turned, 1)


def project(nc, maker, g):
    ident, logits, self_num = g["ident"], g["logits"], g["self_num"]
    srcT, dstT, numT, tile_row, wdT = (g[k] for k in ("srcT", "dstT", "numT", "tile_row", "wdT"))
    w, dst1, src1, dfirst, count, ones, upper = (g[k] for k in ("w", "dst1", "src1", "dfirst", "count", "ones", "upper"))
    d_xnT, d_xp, d_asrc, d_node, d_src, d_dst = (g[k] for k in ("d_xnT", "d_xp", "d_asrc", "d_node", "d_src", "d_dst"))
    d_segmax, d_head, d_num, d_tile, ffn_w = (g[k] for k in ("d_segmax", "d_head", "d_num", "d_tile", "ffn_w"))
    d_own, wf, largest = g["d_own"], g["wf"], g["largest"]
    numT16, xp_scale, xp_inverse, wd_scale, wd_inverse = (
        g[k] for k in ("numT16", "xp_scale", "xp_inverse", "wd_scale", "wd_inverse"))
    CH = KCOLS // P
    SPLIT = 8
    ctx = ExitStack()
    with ctx:
        sb, ps, sem = maker(ctx)
        xnT = [sb(f"pxnT{j}", [P, KC, P]) for j in range(3)]
        xp = [sb(f"xp{j}", [P, 2, D], F16) for j in range(3)]
        own_row = [sb(f"xp_own{j}", [P, D]) for j in range(3)]
        wq = sb("wq", [P, D])
        step = sb("q_step", [P, D])
        scale = sb("q_scale", [P, QB])
        inv = sb("q_inv", [P, QB])
        most = sb("most", [2, 1])
        most_row = sb("most_row", [2, 2])
        low = sb("low", [P, 2])
        dstf = sb("dstf", [P, EC])
        srcf = sb("srcf", [P, EC])
        same = sb("same", [P, EC])
        fences = sb("fences", [P, EC + 1])
        fence, last_fence = fences[:, 0:EC], fences[:, 1:EC + 1]
        tmp = sb("tmp", [P, EC])
        idx = [sb(f"idx{j}", [P, GCOLS], I32) for j in range(GSLOTS)]
        got = [sb(f"got{j}", [P, GCOLS * HEADS]) for j in range(GSLOTS)]
        asrc = sb("asrc", [P, GCOLS * GFILLS, HEADS])
        segmax = sb("segmax", [P, EC, HEADS])
        tables, at = g["tables"], [EC * 2 * HEADS + n * CH * SUB * P for n in (0, 1, 2, 2 + HEADS)]
        head = tables[:, 0:at[0]].rearrange("p (c v) -> p c v", v=2 * HEADS)
        srow, drow, nrow = (tables[:, a:b].rearrange("p (c e) -> p c e", c=CH) for a, b in zip(at, at[1:]))
        most_edge = tables[:, at[2]:at[2] + EC * HEADS].rearrange("p (c h) -> p c h", h=HEADS)
        first = sb("first", [P, 2 * HEADS])
        cinc = sb("cinc", [P, TILES])
        zero_t = sb("zero_t", [P, TILES])
        startf = sb("startf", [P, TILES])
        lastf = sb("lastf", [P, TILES])
        has = sb("has", [P, TILES])
        start_i = sb("start_i", [P, TILES], I32)
        last_i = sb("last_i", [P, TILES], I32)
        nmax = sb("nmax", [P, TILES, HEADS])
        nself = sb("nself", [P, TILES, HEADS])
        tf_i = sb("tf_i", [1, ET], I32)
        tf = sb("tf", [1, ET])
        irow = sb("irow", [1, ET])
        kcol = sb("kcol", [P, CH])
        etile = sb("etile", [P, CH])
        ntile = sb("ntile", [P, CH])
        ntile128 = sb("ntile128", [P, CH])
        step_i = sb("step_i", [P, CH], I32)
        ntile_i = sb("ntile_i", [P, CH], I32)
        far = segmax[:, :, :].rearrange("p c h -> p (c h)")[:, 0:SUB * KCOLS]
        ends = sb("ends", [P, 4, HEADS])
        erow = sb("erow", [HEADS, 4, P])
        edge_row = [sb(f"edge_row{j}", [HEADS, P]) for j in range(4)]
        whole, joins, carry, back_carry = edge_row
        cin = sb("cin", [HEADS, 2, P])
        cinT = sb("cinT", [P, 2, HEADS])
        xp_ps = [ps(f"xp_ps{j}", [P, D]) for j in range(3)]
        g_ps = ps("g_ps", [P, D])

        flat_ready = sem("flat_ready")
        flat_out = sem("flat_out")
        iotas = sem("iotas")
        idx_ready = sem("idx_ready")
        gathered = [sem(f"gathered{j}") for j in range(GSLOTS)]
        xnT_in = [sem(f"pxnT_in{j}") for j in range(3)]
        xp_done = sem("xp_done")
        xp_kept = sem("xp_kept")
        xp_out = [sem(f"xp_out{j}") for j in range(3)]
        largest_ready = sem("largest_ready")
        most_turned = sem("most_turned")
        most_row_ready = sem("most_row_ready")
        most_spread = sem("most_spread")
        powers_ready = sem("powers_ready")
        xp_low = sem("xp_low")
        wd_high = sem("wd_high")
        num_high = sem("num_high")
        num_low = sem("num_low")
        wq_ready = sem("wq_ready")
        wtr_done = sem("wtr_done")
        wtr_kept = sem("wtr_kept")
        cexc_ready = sem("cexc_ready")
        cum_done = sem("cum_done")
        tf_ready = sem("tf_ready")
        stair_done = sem("stair_done")
        plan_read = sem("plan_read")
        plan_ready = sem("plan_ready")
        tile_out = sem("tile_out")
        ends_ready = sem("ends_ready")
        erow_done = sem("erow_done")
        cin_ready = sem("cin_ready")
        cinT_done = sem("cinT_done")
        segmax_ready = sem("segmax_ready")
        segmax_out = sem("segmax_out")
        nmax_in = sem("nmax_in")
        edge_ready = sem("edge_ready")
        scattered = sem("scattered")
        first_in = sem("first_in")
        head_in = sem("head_in")
        nself_ready = sem("nself_ready")
        logit_ready = sem("logit_ready")
        num_ready = sem("num_ready")
        num_out = sem("num_out")
        ends_in = sem("ends_in")
        rows_in = sem("rows_in")
        rows_ready = sem("rows_ready")
        ends_turned = sem("ends_turned")
        steps_done = sem("steps_done")
        dve_own = sem("dve_own2")
        pool_turn = sem("pool_turn2")
        block = ctx.enter_context(nc.Block())
        edge = asrc[:, 0:EC, :]
        lines = lambda d: d.rearrange("i e -> (i e)").rearrange("(p c) -> p c", c=EC)

        @block.sync
        def _(sp):
            def load(t, j):
                sp.wait_ge(xp_done, t + 1)
                sp.dma_start(xnT[j][:, :, :].rearrange("p c n -> p (c n)"),
                             d_xnT[bass.ds(t, 1), :, :].rearrange("o p n -> (o p) n")).then_inc(xnT_in[j], 16)

            def store(t, j):
                sp.wait_ge(xp_low, t + 1 + 3)
                sp.dma_start(d_xp[bass.ds(t * P, P), :], xp[j][:, :, :].rearrange("p a n -> p (a n)")).then_inc(xp_out[j], 16)
                sp.dma_start(d_own[bass.ds(t * P, P), :], own_row[j][:, :]).then_inc(xp_out[j], 16)

            for t in range(3):
                load(t, t)
            with sp.Fori(0, KC - 1) as i:
                for j in range(3):
                    load(3 * i + j + 3, j)
                    store(3 * i + j, j)
            load(TILES - 1, 0)
            for t in range(TILES - 4, TILES):
                store(t, t % 3)
            sp.wait_ge(segmax_ready, 1)
            sp.dma_start(d_segmax.rearrange("(p c) h -> p (c h)", c=EC),
                         segmax[:, :, :].rearrange("p c h -> p (c h)")).then_inc(segmax_out, 16)
            for j in range(3):
                sp.wait_ge(xp_out[j], 32 * len(range(j, TILES, 3)))

        @block.gpsimd
        def _(pool):
            def gather(out, table, index, signal):
                nc.gpsimd.indirect_dma_start(
                    out=out, out_offset=None, in_=table,
                    in_offset=bass.IndirectOffsetOnAxis(ap=index, axis=0)).then_inc(signal, 16)

            nc.gpsimd.iota(irow[:, :], pattern=[[1, ET]], base=0, channel_multiplier=0,
                           allow_small_or_imprecise_dtypes=True).then_inc(iotas, 1)
            nc.gpsimd.iota(kcol[:, :], pattern=[[P, CH]], base=0, channel_multiplier=1,
                           allow_small_or_imprecise_dtypes=True).then_inc(iotas, 1)
            pool.wait_ge(g["asrc_out"], 16)

            def fill_all(s):
                for c in range(GCOLS):
                    gather(got[s][:, c * HEADS:(c + 1) * HEADS], d_asrc, idx[s][:, c:c + 1], gathered[s])

            pool.wait_ge(idx_ready, GSLOTS)
            for s in range(GSLOTS):
                fill_all(s)
            pool.wait_ge(flat_ready, 1)
            nc.gpsimd.dma_start(lines(d_dst), dstf[:, :]).then_inc(flat_out, 16)
            nc.gpsimd.dma_start(lines(d_src), srcf[:, :]).then_inc(flat_out, 16)
            pool.wait_ge(g["node_out"], 16)
            pool.wait_ge(plan_ready, 1)
            nc.gpsimd.dma_start(d_tile.rearrange("(c p) -> p c", p=P), ntile_i[:, :],
                                allow_slow_non_contiguous=True).then_inc(tile_out, 16)
            for t in range(TILES):
                nc.gpsimd.indirect_dma_start(
                    out=d_head, out_offset=bass.IndirectOffsetOnAxis(ap=start_i[:, t:t + 1], axis=0),
                    in_=logits[:, t, :], in_offset=None, bounds_check=EP - 1, oob_is_err=False).then_inc(scattered, 16)
            gather(first[:, :], d_node, dst1[:, 0:1], first_in)
            pool.wait_ge(flat_out, 32)
            for c in range(CH):
                gather(srow[:, c, :], d_src, step_i[:, c:c + 1], ends_in)
                gather(drow[:, c, :], d_dst, step_i[:, c:c + 1], ends_in)
            pool.wait_ge(tile_out, 16)
            nc.gpsimd.dma_start(tile_row[:, :], d_tile.unsqueeze(0)).then_inc(tile_out, 16)
            pool.wait_ge(scattered, 16 * TILES)
            nc.gpsimd.dma_start(head[:, :, :].rearrange("p c v -> p (c v)"),
                                d_head.rearrange("(p c) v -> p (c v)", c=EC)).then_inc(head_in, 16)
            with pool.Fori(1, GFILLS // GSLOTS) as i:
                for s in range(GSLOTS):
                    pool.wait_ge(idx_ready, i * GSLOTS + s + 1)
                    pool.sem_inc(pool_turn, 1)
                    fill_all(s)
            pool.wait_ge(segmax_ready, 1)
            nc.gpsimd.tensor_tensor(out=edge, in0=edge, in1=head[:, :, HEADS:2 * HEADS], op=ALU.add).then_inc(edge_ready, 1)
            pool.wait_ge(segmax_out, 16)
            for t in range(TILES):
                if t == SPLIT:
                    pool.wait_ge(num_out, 16)
                    for c in range(CH):
                        gather(nrow[:, c, :], d_num, step_i[:, c:c + 1], rows_in)
                gather(nmax[:, t, :], d_segmax, last_i[:, t:t + 1], nmax_in)
            pool.wait_ge(tile_out, 32)

        @block.vector
        def _(dve):
            own = Chain(dve, dve_own)

            def fill(s, column):
                nc.vector.tensor_copy(idx[s][:, :], src1[:, bass.ds(column, GCOLS)]).then_inc(idx_ready, 1)

            nc.vector.sem_inc(xp_low, 3)
            for s in range(GSLOTS):
                fill(s, s * GCOLS)
            dve.wait_ge(g["wf_in"], 16)
            nc.vector.tensor_reduce(out=largest[:, 1:2], in_=wf[:, :, :].rearrange("p c n -> p (c n)"), axis=AX.X, op=ALU.max,
                                    apply_absolute_value=True).then_inc(largest_ready, 1)
            dve.wait_ge(most_turned, 1)
            own.link(nc.vector.tensor_reduce(out=most[:, :], in_=g_ps[0:2, 2 * P:3 * P], axis=AX.X, op=ALU.max))
            nc.vector.tensor_scalar(most_row[:, :], ident[0:2, 0:2], most[:, :], None, ALU.mult).then_inc(most_row_ready, 1)
            dve.wait_ge(most_spread, 1)
            power_scale(nc, own, g_ps[:, 2 * P:2 * P + 1], low[:, 0:1], xp_scale[:, :], xp_inverse[:, :], 4)
            power_scale(nc, own, g_ps[:, 2 * P + 1:2 * P + 2], low[:, 1:2], wd_scale[:, :], wd_inverse[:, :], 13)
            nc.vector.sem_inc(powers_ready, 1)
            nc.vector.memset(zero_t[:, :], 0.0)
            nc.vector.tensor_copy(dstf[:, :], dst1[:, 0:EC])
            own.link(nc.vector.tensor_copy(srcf[:, :], src1[:, 0:EC]))
            nc.vector.sem_inc(flat_ready, 1)
            own.link(nc.vector.tensor_tensor_scan(cinc[:, :], count[:, :], zero_t[:, :], 0.0, ALU.add, ALU.add))
            nc.vector.tensor_tensor(out=cinc[:, :], in0=cinc[:, :], in1=count[:, :], op=ALU.subtract).then_inc(cexc_ready, 1)
            own.link(nc.vector.tensor_scalar(tf_i[:, :], dfirst[:, :], 7, None, ALU.logical_shift_right))
            own.link(nc.vector.tensor_copy(tf[:, :], tf_i[:, :]))
            dve.wait_ge(iotas, 2)
            nc.vector.tensor_tensor(out=tf[:, :], in0=tf[:, :], in1=irow[:, :], op=ALU.add).then_inc(tf_ready, 1)
            dve.wait_ge(cum_done, 1)
            own.link(nc.vector.tensor_scalar(has[:, :], count[:, :], 0.0, None, ALU.is_gt))
            own.link(nc.vector.tensor_tensor(out=startf[:, :], in0=g_ps[:, 0:TILES], in1=count[:, :], op=ALU.subtract))
            own.link(nc.vector.scalar_tensor_tensor(out=startf[:, :], in0=has[:, :], scalar=-float(2 * EP), in1=startf[:, :],
                                                    op0=ALU.mult, op1=ALU.add))
            own.link(nc.vector.tensor_scalar(startf[:, :], startf[:, :], float(2 * EP), None, ALU.add))
            own.link(nc.vector.tensor_scalar(lastf[:, :], g_ps[:, 0:TILES], -1.0, 0.0, ALU.add, ALU.max))
            nc.vector.tensor_copy(start_i[:, :], startf[:, :])
            own.link(nc.vector.tensor_copy(last_i[:, :], lastf[:, :]))
            own.link(nc.vector.tensor_scalar(has[:, :], has[:, :], -1.0, BIG, ALU.add, ALU.mult))
            dve.wait_ge(stair_done, 1)
            for c in range(CH):
                own.link(nc.vector.tensor_scalar(tmp[:, 0:ET], g_ps[:, 512:512 + ET], kcol[:, c:c + 1], None, ALU.is_le))
                own.link(nc.vector.tensor_reduce(out=etile[:, c:c + 1], in_=tmp[:, 0:ET], axis=AX.X, op=ALU.add))
            nc.vector.sem_inc(plan_read, 1)
            own.link(nc.vector.tensor_scalar(etile[:, :], etile[:, :], -1.0, 0.0, ALU.add, ALU.max))
            own.link(nc.vector.tensor_tensor(out=ntile[:, :], in0=kcol[:, :], in1=etile[:, :], op=ALU.subtract))
            nc.vector.tensor_scalar(ntile128[:, :], ntile[:, :], float(P), None, ALU.mult)
            own.link(nc.vector.tensor_scalar(ntile[:, :], ntile[:, :], float(TILES - 1), None, ALU.min))
            nc.vector.tensor_copy(step_i[:, :], etile[:, :])
            own.link(nc.vector.tensor_copy(ntile_i[:, :], ntile[:, :]))
            nc.vector.sem_inc(plan_ready, 1)
            nc.vector.memset(same[:, 0:1], 0.0)
            own.link(nc.vector.tensor_tensor(out=same[:, 1:EC], in0=dstf[:, 1:EC], in1=dstf[:, 0:EC - 1], op=ALU.is_equal))
            own.link(nc.vector.tensor_scalar(fence, same[:, :], -1.0, BIG, ALU.add, ALU.mult))
            nc.vector.memset(fences[:, 0:1], 0.0)
            own.link(nc.vector.memset(fences[:, EC:EC + 1], 0.0))

            rounds = GFILLS // KC

            def split(t, j):
                dve.wait_ge(xp_kept, t + 1 + 3)
                nc.vector.scalar_tensor_tensor(out=xp[j][:, 1, :], in0=xp_ps[j][:, :], scalar=xp_scale[:, :],
                                               in1=xp[j][:, 0, :], op0=ALU.mult, op1=ALU.subtract).then_inc(xp_low, 1)

            def turn(o):
                row = wf[:, bass.ds(o, 1), :].rearrange("p o n -> p (o n)")
                own.link(block_scales(nc, own, row, scale[:, :], inv[:, :]))
                dve.wait_ge(wtr_done, o + 1)
                own.link(nc.vector.tensor_tensor(out=blocks(wq[:, :]), in0=blocks(row), in1=spread(inv[:, :]), op=ALU.mult))
                own.link(round_to_grid(nc, own, wq[:, :], step[:, :]))
                nc.vector.tensor_tensor(out=blocks(wq[:, :]), in0=blocks(wq[:, :]), in1=spread(scale[:, :]),
                                        op=ALU.mult).then_inc(wq_ready, 1)
                for f in range(rounds):
                    s = f % GSLOTS
                    dve.wait_ge(gathered[s], 16 * GCOLS * (o * (rounds // GSLOTS) + f // GSLOTS + 1))
                    nc.vector.tensor_copy(
                        asrc[:, bass.ds((o * rounds + f) * GCOLS, GCOLS), :].rearrange("p c h -> p (c h)"), got[s][:, :])
                    fill(s, (o * rounds + f + GSLOTS) * GCOLS)
                    if f % 2:
                        split(3 * o + f // 2, f // 2)
                dve.wait_ge(wd_high, o + 1)
                cols = bass.ds(o * P, P)
                nc.vector.scalar_tensor_tensor(
                    out=wdT[:, :, 1, cols], in0=g_ps[:, :].rearrange("p (c n) -> p c n", n=P), scalar=wd_scale[:, :],
                    in1=wdT[:, :, 0, cols], op0=ALU.mult, op1=ALU.subtract).then_inc(wtr_kept, 1)
            with dve.Fori(0, 2) as o:
                back = own.enter(o, SCALE_LINKS + 3 + ROUND_LINKS)
                turn(o)
            own.leave(back, 2)
            dve.wait_ge(first_in, 16)
            dve.wait_ge(head_in, 16)
            own.link(nc.vector.tensor_copy(head[:, 0, :], first[:, :]))
            for v in range(2 * HEADS):
                last = nc.vector.tensor_tensor_scan(head[:, :, v], same[:, :], head[:, :, v], 0.0, ALU.mult, ALU.add)
            own.link(last)
            with dve.Fori(2, KC) as o:
                back = own.enter(o - 2, SCALE_LINKS + 3 + ROUND_LINKS)
                turn(o)
            own.leave(back, KC - 2)
            dve.wait_ge(wtr_kept, KC + 1)

            def forward(start):
                for h in range(HEADS):
                    last = nc.vector.tensor_tensor_scan(segmax[:, :, h], fence, edge[:, :, h], start(h), ALU.add, ALU.max)
                own.link(last)

            def backward(start):
                for h in range(HEADS):
                    run = segmax[:, :, h][:, ::-1]
                    last = nc.vector.tensor_tensor_scan(run, last_fence[:, ::-1], run, start(h), ALU.add, ALU.max)
                return last

            forward(lambda h: -BIG)
            own.link(nc.vector.tensor_copy(ends[:, 0, :], segmax[:, EC - 1, :]))
            own.link(backward(lambda h: -BIG))
            nc.vector.tensor_copy(ends[:, 1, :], dstf[:, 0:1].to_broadcast([P, HEADS]))
            nc.vector.tensor_copy(ends[:, 2, :], dstf[:, EC - 1:EC].to_broadcast([P, HEADS]))
            nc.vector.tensor_copy(ends[:, 3, :], segmax[:, 0, :]).then_inc(ends_ready, 1)
            split(TILES - 1, 0)
            dve.wait_ge(ends_in, 16 * 2 * CH)
            for c in range(CH):
                last = nc.vector.tensor_scalar(drow[:, c, :], drow[:, c, :], ntile128[:, c:c + 1], None, ALU.subtract)
            last.then_inc(rows_ready, 1)
            dve.wait_ge(erow_done, 1)
            own.link(nc.vector.tensor_copy(erow[:, :, :].rearrange("h a p -> h (a p)"), g_ps[0:HEADS, 0:4 * P]))
            nc.vector.memset(joins[:, 0:1], 0.0)
            own.link(nc.vector.tensor_tensor(out=joins[:, 1:P], in0=erow[:, 1, 1:P], in1=erow[:, 2, 0:P - 1], op=ALU.is_equal))
            own.link(nc.vector.tensor_tensor(out=whole[:, :], in0=erow[:, 1, :], in1=erow[:, 2, :], op=ALU.is_equal))
            own.link(nc.vector.tensor_scalar(whole[:, :], whole[:, :], -1.0, BIG, ALU.add, ALU.mult))
            own.link(nc.vector.tensor_scalar(joins[:, :], joins[:, :], -1.0, BIG, ALU.add, ALU.mult))
            nc.vector.tensor_tensor(out=carry[:, :], in0=whole[:, :], in1=joins[:, :], op=ALU.min)
            nc.vector.memset(back_carry[:, P - 1:P], -BIG)
            own.link(nc.vector.tensor_tensor(out=back_carry[:, 0:P - 1], in0=whole[:, 0:P - 1], in1=joins[:, 1:P], op=ALU.min))
            nc.vector.tensor_tensor_scan(carry[:, :], carry[:, :], erow[:, 0, :], -BIG, ALU.add, ALU.max)
            own.link(nc.vector.tensor_tensor_scan(back_carry[:, ::-1], back_carry[:, ::-1], erow[:, 3, :][:, ::-1], -BIG,
                                                  ALU.add, ALU.max))
            nc.vector.memset(cin[:, 0, 0:1], -BIG)
            nc.vector.memset(cin[:, 1, P - 1:P], -BIG)
            nc.vector.tensor_tensor(out=cin[:, 0, 1:P], in0=carry[:, 0:P - 1], in1=joins[:, 1:P], op=ALU.add)
            nc.vector.tensor_tensor(out=cin[:, 1, 0:P - 1], in0=back_carry[:, 1:P], in1=joins[:, 1:P], op=ALU.add).then_inc(cin_ready, 1)
            dve.wait_ge(cinT_done, 1)
            own.link(nc.vector.tensor_copy(cinT[:, :, :].rearrange("p a h -> p (a h)"), g_ps[:, 512:512 + 2 * HEADS]))
            forward(lambda h: cinT[:, 0, h:h + 1])
            backward(lambda h: cinT[:, 1, h:h + 1]).then_inc(segmax_ready, 1)
            dve.wait_ge(segmax_ready, 1)
            own.link(nc.vector.tensor_tensor(out=most_edge, in0=segmax[:, :, :], in1=head[:, :, 0:HEADS], op=ALU.max))
            own.link(nc.vector.tensor_tensor(out=most_edge, in0=most_edge, in1=head[:, :, HEADS:2 * HEADS], op=ALU.add))
            own.link(nc.vector.scalar_tensor_tensor(out=most_edge, in0=most_edge, scalar=SLOPE, in1=most_edge, op0=ALU.mult, op1=ALU.max))
            dve.wait_ge(edge_ready, 1)
            own.link(nc.vector.scalar_tensor_tensor(out=edge, in0=edge, scalar=SLOPE, in1=edge, op0=ALU.mult, op1=ALU.max))
            nc.vector.tensor_tensor(out=edge, in0=edge, in1=most_edge, op=ALU.subtract).then_inc(logit_ready, 1)
            dve.wait_ge(logit_ready, 1)
            dve.wait_ge(ends_turned, 1)
            own.link(nc.vector.tensor_copy(dstT, xp_ps[0][:, SUB * KCOLS:2 * SUB * KCOLS]))
            dve.wait_ge(segmax_out, 16)
            own.link(nc.vector.scalar_tensor_tensor(out=far, in0=dstT, scalar=-float(P - 1), in1=dstT, op0=ALU.add, op1=ALU.mult))
            own.link(nc.vector.tensor_scalar(far, far, 0.0, float(FAR), ALU.is_gt, ALU.mult))
            nc.vector.tensor_tensor(out=srcT, in0=xp_ps[0][:, 0:SUB * KCOLS], in1=far, op=ALU.add)
            by_head = lambda v, b: numT16[:, :, v:v + HEADS, b].rearrange("p k h -> p h k")
            dve.wait_ge(num_high, 1)
            own.link(nc.vector.tensor_copy(by_head(0, 0), numT[:, :, :]))
            nc.vector.tensor_tensor(out=by_head(HEADS, 0), in0=numT[:, :, :], in1=by_head(0, 0),
                                    op=ALU.subtract).then_inc(num_low, 1)
            dve.wait_ge(num_low, 1)
            nc.vector.tensor_copy(numT16[:, :, HEADS:2 * HEADS, 1], numT16[:, :, HEADS:2 * HEADS, 0])
            nself_v, nmax_v, node_src, node_dst = nself[:, :, :], nmax[:, :, :], logits[:, :, 0:HEADS], logits[:, :, HEADS:2 * HEADS]
            own.link(nc.vector.tensor_tensor(out=nself_v, in0=node_src, in1=node_dst, op=ALU.add))
            own.link(nc.vector.scalar_tensor_tensor(out=nself_v, in0=nself_v, scalar=SLOPE, in1=nself_v, op0=ALU.mult, op1=ALU.max))
            dve.wait_ge(nmax_in, 16 * TILES)
            own.link(nc.vector.tensor_tensor(out=nmax_v, in0=nmax_v, in1=has[:, :].unsqueeze(2).to_broadcast([P, TILES, HEADS]),
                                             op=ALU.add))
            own.link(nc.vector.tensor_tensor(out=nmax_v, in0=nmax_v, in1=node_src, op=ALU.max))
            own.link(nc.vector.tensor_tensor(out=nmax_v, in0=nmax_v, in1=node_dst, op=ALU.add))
            own.link(nc.vector.scalar_tensor_tensor(out=nmax_v, in0=nmax_v, scalar=SLOPE, in1=nmax_v, op0=ALU.mult, op1=ALU.max))
            nc.vector.tensor_tensor(out=nself_v, in0=nself_v, in1=nmax_v, op=ALU.subtract).then_inc(nself_ready, 1)

        @block.scalar
        def _(act):
            act.sem_inc(xp_kept, 3)

            def keep(t, j, n):
                act.wait_ge(xp_done, t + 1 + 3)
                if n is not None:
                    act.wait_ge(xp_out[j], n)
                nc.scalar.activation(own_row[j][:, :], xp_ps[j][:, :], ACT.Copy)
                nc.scalar.activation(xp[j][:, 0, :], xp_ps[j][:, :], ACT.Copy, scale=xp_scale[:, :]).then_inc(xp_kept, 1)

            def keep_w(o):
                act.wait_ge(wtr_done, o + 1 + 1)
                nc.scalar.activation(wdT[:, :, 0, bass.ds(o * P, P)], g_ps[:, :].rearrange("p (c n) -> p c n", n=P),
                                     ACT.Copy, scale=wd_scale[:, :]).then_inc(wd_high, 1)

            act.wait_ge(powers_ready, 1)
            for t in range(3):
                keep(t, t, None)
            keep_w(0)
            with act.Fori(1, KC) as i:
                for j in range(3):
                    keep(3 * i + j, j, 32 * i)
                keep_w(i)
            keep(TILES - 1, 0, 32 * KC)
            act.wait_ge(logit_ready, 1)
            nc.scalar.activation(edge, edge, ACT.Exp).then_inc(num_ready, 1)
            act.wait_ge(num_ready, 1)
            nc.scalar.dma_start(d_num.rearrange("i e -> (i e)").rearrange("(p c) -> p c", c=EC * HEADS),
                                edge.rearrange("p c h -> p (c h)")).then_inc(num_out, 16)
            act.wait_ge(steps_done, 1)
            for h in range(HEADS):
                half = slice((h % 2) * SUB * KCOLS, (h % 2 + 1) * SUB * KCOLS)
                last = nc.scalar.activation(numT[:, h, :], xp_ps[1 + h // 2][:, half], ACT.Copy, scale=NUM_SCALE)
            last.then_inc(num_high, 1)
            act.wait_ge(num_low, 1)
            nc.scalar.activation(numT[:, :, :], numT16[:, :, 0:HEADS, 0].rearrange("p k h -> p h k"), ACT.Copy)
            act.wait_ge(nself_ready, 1)
            nc.scalar.activation(self_num[:, :, :], nself[:, :, :], ACT.Exp)

        @block.tensor
        def _(pe):
            pe.sem_inc(xp_done, 3)
            pe.sem_inc(wtr_done, 1)
            pe.sem_inc(wtr_kept, 1)
            pe.wait_ge(largest_ready, 1)
            nc.tensor.transpose(g_ps[0:2, 2 * P:3 * P], largest[:, :], ident[:, :]).then_inc(most_turned, 1)
            pe.wait_ge(most_row_ready, 1)
            nc.tensor.matmul(g_ps[:, 2 * P:2 * P + 2], ones[0:2, :], most_row[:, :], start=True, stop=True).then_inc(most_spread, 1)
            pe.wait_ge(cexc_ready, 1)
            nc.tensor.matmul(g_ps[:, 0:TILES], upper[:, :], count[:, :], start=True, stop=False)
            nc.tensor.matmul(g_ps[:, 0:TILES], ones[:, :], cinc[:, :], start=False, stop=True).then_inc(cum_done, 1)
            pe.wait_ge(tf_ready, 1)
            nc.tensor.matmul(g_ps[:, 512:512 + ET], ones[0:1, :], tf[:, :], start=True, stop=True).then_inc(stair_done, 1)

            def tile(t, j, n):
                pe.wait_ge(xnT_in[j], n)
                pe.wait_ge(xp_low, t + 1)
                for c in range(KC):
                    for half in range(2):
                        last = nc.tensor.matmul(xp_ps[j][:, half * 512:(half + 1) * 512], xnT[j][:, c, :],
                                                w[:, c, half * 512:(half + 1) * 512], start=(c == 0), stop=(c == KC - 1))
                last.then_inc(xp_done, 1)

            with pe.Fori(0, KC) as i:
                for j in range(3):
                    tile(3 * i + j, j, 16 * (i + 1))
                pe.wait_ge(plan_read, 1)
                pe.wait_ge(wq_ready, i + 1)
                pe.wait_ge(wtr_kept, i + 1)
                for c in range(KC):
                    last = nc.tensor.transpose(g_ps[:, c * P:(c + 1) * P], wq[:, c * P:(c + 1) * P], ident[:, :])
                last.then_inc(wtr_done, 1)
            tile(TILES - 1, 0, 16 * (KC + 1))

            pe.wait_ge(ends_ready, 1)
            pe.wait_ge(wtr_kept, KC + 1)
            for a in range(4):
                last = nc.tensor.transpose(g_ps[0:HEADS, a * P:(a + 1) * P], ends[:, a, :], ident[:, :])
            last.then_inc(erow_done, 1)
            pe.wait_ge(cin_ready, 1)
            for a in range(2):
                last = nc.tensor.transpose(g_ps[:, 512 + a * HEADS:512 + (a + 1) * HEADS], cin[:, a, :], ident[0:HEADS, 0:HEADS])
            last.then_inc(cinT_done, 1)
            pe.wait_ge(rows_ready, 1)
            pe.wait_ge(xp_low, TILES + 3)
            places = [(c, u, slice(u * P, (u + 1) * P), u * KCOLS + c * P) for c in range(CH) for u in range(SUB)]
            for c, u, sub, at in places:
                nc.tensor.transpose(xp_ps[0][:, at:at + P], srow[:, c, sub], ident[:, :])
                last = nc.tensor.transpose(xp_ps[0][:, SUB * KCOLS + at:SUB * KCOLS + at + P], drow[:, c, sub], ident[:, :])
            last.then_inc(ends_turned, 1)
            pe.wait_ge(rows_in, 16 * CH)
            for c, u, sub, at in places:
                for h in range(HEADS):
                    to = (h % 2) * SUB * KCOLS + at
                    last = nc.tensor.transpose(
                        xp_ps[1 + h // 2][:, to:to + P],
                        nrow[:, c, :].rearrange("p (e h) -> p e h", h=HEADS)[:, sub, h], ident[:, :])
            last.then_inc(steps_done, 1)


def aggregate(nc, maker, g):
    tables, srcT, dstT, numT, numT16, tile_row, acc, zsum, d_xp = (
        g[k] for k in ("tables", "srcT", "dstT", "numT", "numT16", "tile_row", "acc", "zsum", "d_xp"))
    TURN = 4
    V = 2 * HEADS
    ctx = ExitStack()
    with ctx:
        sb, ps, sem = maker(ctx)
        iota16 = sb("iota16", [P, P], F16)
        idx = [sb(f"sidx{j}", [P, SUB], I32) for j in range(TURN)]
        xg = [[sb(f"xg{j}_{u}", [P, 2, D], F16) for u in range(SUB)] for j in range(TURN)]
        hot = [[sb(f"hot{j}_{u}", [P, P], F16) for u in range(SUB)] for j in range(TURN)]
        wgt = [[sb(f"wgt{j}_{u}", [P, V, P], F16) for u in range(SUB)] for j in range(2)]
        sum_ps = [ps(f"sum_ps{j}", [P, D]) for j in range(2)]
        z_ps = [ps(f"z_ps{j}", [P, 512]) for j in range(2)]

        iota_made = sem("iota_made")
        cleared = sem("cleared")
        idx_ready = sem("sidx_ready")
        arrived = [sem(f"arrived{j}") for j in range(TURN)]
        hot_ready = sem("hot_ready")
        low_ready = sem("low_ready")
        high_ready = sem("high_ready")
        mm_done = sem("mm_done")
        added = sem("added")
        pool_turn = sem("pool_turn3")
        block = ctx.enter_context(nc.Block())
        EARLY = TILES // TURN * TURN
        col = lambda table, u, k, n=1: table.rearrange("p (u k) -> p u k", u=SUB)[:, u, bass.ds(k, n)]

        @block.gpsimd
        def _(pool):
            def gather(s):
                for u in range(SUB):
                    nc.gpsimd.indirect_dma_start(
                        out=xg[s][u][:, :, :].rearrange("p a n -> p (a n)"), out_offset=None, in_=d_xp,
                        in_offset=bass.IndirectOffsetOnAxis(ap=idx[s][:, u:u + 1], axis=0),
                        bounds_check=NP - 1, oob_is_err=False).then_inc(arrived[s], 16)

            def refill(k, s):
                pool.wait_ge(idx_ready, k + 1)
                pool.wait_ge(mm_done, SUB * (k + 1))
                pool.sem_inc(pool_turn, 1)
                gather(s)

            nc.gpsimd.iota(iota16[:, :], pattern=[[1, P]], base=0, channel_multiplier=0,
                           allow_small_or_imprecise_dtypes=True).then_inc(iota_made, 1)
            pool.wait_ge(idx_ready, TURN)
            for s in range(TURN):
                gather(s)
            for k in range(TURN, EARLY):
                refill(k, k % TURN)
                nc.gpsimd.memset(acc[:, k, :], 0.0).then_inc(cleared, 1)
            with pool.Fori(EARLY // TURN, STEPS // TURN) as i:
                for j in range(TURN):
                    refill(TURN * i + j, j)

        @block.vector
        def _(dve):
            def indices(k):
                return srcT.rearrange("p (u k) -> p u k", u=SUB)[:, :, bass.ds(k, 1)].rearrange("p u o -> p (u o)")

            def one_hots(k, j):
                dve.wait_ge(mm_done, SUB * (k + 1))
                for u in range(SUB):
                    nc.vector.tensor_scalar(hot[j][u][:, :], iota16[:, :], col(dstT, u, k), None,
                                            ALU.is_equal).then_inc(hot_ready, 1)

            def weights(k, j, s):
                for u in range(SUB):
                    dve.wait_ge(hot_ready, SUB * k + u + 1)
                    dve.wait_ge(mm_done, SUB * (k + 2) + u + 1)
                    nc.vector.tensor_tensor(
                        out=wgt[s][u][:, HEADS:V, :].rearrange("p v (n b) -> p v n b", b=2),
                        in0=hot[j][u][:, :].rearrange("p (n b) -> p n b", b=2).unsqueeze(1).to_broadcast([P, HEADS, P // 2, 2]),
                        in1=numT16[:, bass.ds(u * KCOLS + k, 1), HEADS:V, :].rearrange("p o v b -> p (o v) b").unsqueeze(2)
                        .to_broadcast([P, HEADS, P // 2, 2]), op=ALU.mult).then_inc(low_ready, 1)

            for k in range(TURN):
                nc.vector.tensor_scalar(idx[k][:, :], indices(k), NP - 1, None, ALU.min).then_inc(idx_ready, 1)
            dve.wait_ge(iota_made, 1)
            one_hots(0, 0)
            one_hots(1, 1)
            weights(0, 0, 0)
            nc.vector.memset(zsum[:, :, :], 0.0)
            nc.vector.memset(acc[:, EARLY:TILES, :], 0.0)
            nc.vector.memset(acc[:, 0:TURN, :], 0.0).then_inc(cleared, TURN)

            def turn(i, early):
                for j in range(TURN):
                    k = TURN * i + j
                    if early:
                        dve.wait_ge(cleared, k + 1)
                    one_hots(k + 2, (j + 2) % TURN)
                    weights(k + 1, (j + 1) % TURN, (j + 1) % 2)
                    t = dve.value_load(tile_row[0:1, bass.ds(k, 1)], min_val=0, max_val=TILES - 1)
                    dve.wait_ge(mm_done, SUB * (k + 1 + TURN))
                    nc.vector.tensor_copy(idx[j][:, :], indices(k + TURN)).then_inc(idx_ready, 1)
                    dve.wait_ge(added, k + 2)
                    s_acc = acc[:, bass.ds(t, 1), :].rearrange("p o n -> p (o n)")
                    z_acc = zsum[:, bass.ds(t, 1), :].rearrange("p o n -> p (o n)")
                    nc.vector.tensor_tensor(out=z_acc, in0=z_ps[j % 2][:, 0:V], in1=z_acc, op=ALU.add)
                    nc.vector.tensor_tensor(out=s_acc, in0=sum_ps[j % 2][:, :], in1=s_acc, op=ALU.add).then_inc(added, 1)

            with dve.Fori(0, EARLY // TURN) as i:
                turn(i, True)
            with dve.Fori(EARLY // TURN, STEPS // TURN) as i:
                turn(i, False)

        @block.scalar
        def _(act):
            with act.Fori(0, STEPS // TURN) as i:
                for j in range(TURN):
                    k = TURN * i + j
                    for u in range(SUB):
                        act.wait_ge(hot_ready, SUB * k + u + 1)
                        act.wait_ge(mm_done, SUB * (k + 2) + u + 1)
                        for h in range(HEADS):
                            last = nc.scalar.activation(wgt[j % 2][u][:, h, :], hot[j][u][:, :], ACT.Copy,
                                                        scale=col(numT[:, h, :], u, k))
                        last.then_inc(high_ready, 1)

        @block.tensor
        def _(pe):
            pe.sem_inc(mm_done, SUB * TURN)
            pe.sem_inc(added, 2)
            with pe.Fori(0, STEPS // TURN) as i:
                for j in range(TURN):
                    k, s = TURN * i + j, j % 2
                    pe.wait_ge(arrived[j], 16 * SUB * (i + 1))
                    pe.wait_ge(added, k + 1)
                    for u in range(SUB):
                        pe.wait_ge(high_ready, SUB * k + u + 1)
                        pe.wait_ge(low_ready, SUB * k + u + 1)
                        nc.tensor.matmul(z_ps[s][:, 0:V], hot[j][u][:, :],
                                         numT16[:, bass.ds(u * KCOLS + k, 1), :, 0].rearrange("p o v -> p (o v)"),
                                         start=(u == 0), stop=(u == SUB - 1))
                        for h in range(HEADS):
                            for n, (a, b) in enumerate(((0, 0), (0, 1), (1, 0))):
                                last = nc.tensor.matmul(
                                    sum_ps[s][:, h * C:(h + 1) * C], wgt[s][u][:, a * HEADS + h, :],
                                    xg[j][u][:, b, h * C:(h + 1) * C],
                                    start=(u == 0 and h % 2 == 0 and n == 0), stop=(u == SUB - 1 and h % 2 == 1 and n == 2),
                                    skip_group_check=True)
                        last.then_inc(mm_done, 1)


def finish(nc, maker, g):
    x, gnn_bias, ffn_bias, out, d_own = (g[k] for k in ("x", "gnn_bias", "ffn_bias", "out", "d_own"))
    ident, self_num, wdT, acc, zsum, tables = (g[k] for k in ("ident", "self_num", "wdT", "acc", "zsum", "tables"))
    xp_inverse, wd_inverse = g["xp_inverse"], g["wd_inverse"]
    LAST = TILES - 1
    ctx = ExitStack()
    with ctx:
        sb, ps, sem = maker(ctx)
        h1 = [tables[:, j * D:(j + 1) * D] for j in range(2)]
        xn = [tables[:, j * D:(j + 1) * D] for j in range(2, 4)]
        xqT = [tables[:, j * D:(j + 1) * D].bitcast(F16).rearrange("p (v c n) -> p v c n", v=2, c=KC) for j in range(4, 6)]
        step = tables[:, 6 * D:7 * D]
        biasb = sb("biasb", [P, 2, D])
        z32 = sb("z32", [P, TILES, HEADS])
        inv_z = sb("inv_z", [P, TILES, HEADS])
        acc_w = sb("acc_w", [P, TILES, HEADS])
        self_w = sb("self_w", [P, TILES, HEADS])
        out_scale = sb("out_scale", [P, 1])
        xr = [sb(f"xr{j}", [P, D]) for j in range(2)]
        own_row = [sb(f"own_row{j}", [P, D]) for j in range(2)]
        lin = [sb(f"lin{j}", [P, D]) for j in range(2)]
        stats = sb("fstats", [P, 2, 6])
        mv = [sb(f"fmv{j}", [P, 2]) for j in range(2)]
        std = [sb(f"fstd{j}", [P, 1]) for j in range(2)]
        rstd = [sb(f"frstd{j}", [P, 1]) for j in range(2)]
        shift = [sb(f"fshift{j}", [P, 1]) for j in range(2)]
        newton = sb("fnewton", [P, 1])
        scale = [sb(f"fscale{j}", [P, QB]) for j in range(2)]
        inv = [sb(f"finv{j}", [P, QB]) for j in range(2)]
        tr_ps = [ps(f"ftr_ps{j}", [P, D]) for j in range(2)]
        mm_ps = [ps(f"fmm_ps{j}", [P, D]) for j in range(2)]

        bias_in = sem("bias_in")
        x_in = [sem(f"fx_in{j}") for j in range(2)]
        own_in = [sem(f"own_in{j}") for j in range(2)]
        ratios_ready = sem("ratios_ready")
        own_scaled = sem("own_scaled")
        own_biased = sem("own_biased")
        mixed = sem("mixed")
        x1_ready = sem("x1_ready")
        x1b_ready = sem("x1b_ready")
        var_ready = sem("fvar_ready")
        std_ready = sem("fstd_ready")
        rstd_ready = sem("frstd_ready")
        xn_ready = sem("fxn_ready")
        scales_ready = sem("scales_ready")
        y_ready = sem("y_ready")
        grid_ready = sem("grid_ready")
        xq_ready = sem("xq_ready")
        tr_done = sem("ftr_done")
        high_ready = sem("fhigh_ready")
        low_ready = sem("flow_ready")
        mm_done = sem("fmm_done")
        lin_ready = sem("lin_ready")
        summed = sem("summed")
        stored = [sem(f"stored{j}") for j in range(2)]
        dve_own = sem("dve_own4")
        dve_turn = sem("dve_turn4")
        pool_turn = sem("pool_turn4")
        block = ctx.enter_context(nc.Block())
        kept = lambda t: acc[:, bass.ds(t, 1), :].rearrange("p o n -> p (o n)")

        @block.sync
        def _(sp):
            def load(t, j, n=P):
                sp.wait_ge(x1_ready, t + 1)
                sp.dma_start(own_row[j][:, :], d_own[bass.ds(t * P, P), :]).then_inc(own_in[j], 16)
                sp.dma_start(xr[j][0:n, :], x[bass.ds(t * P, n), :]).then_inc(x_in[j], 16)

            def store(t, j, n=P):
                sp.wait_ge(summed, t + 1)
                sp.dma_start(out[bass.ds(t * P, n), :], lin[j][0:n, :]).then_inc(stored[j], 16)

            load(0, 0)
            sp.dma_start(biasb[:, 0, :], gnn_bias.partition_broadcast(P)).then_inc(bias_in, 16)
            sp.dma_start(biasb[:, 1, :], ffn_bias.partition_broadcast(P)).then_inc(bias_in, 16)
            for t in range(1, 6):
                load(t, t % 2)
            with sp.Fori(0, TILES // 2 - 3) as i:
                for j in range(2):
                    store(2 * i + j, j)
                    load(2 * i + j + 6, j)
            store(LAST - 6, 0)
            load(LAST, 0, LAST_ROWS)
            for t in range(LAST - 5, LAST + 1):
                store(t, t % 2, P if t < LAST else LAST_ROWS)
            sp.wait_ge(stored[0], 16 * (TILES // 2 + 1))
            sp.wait_ge(stored[1], 16 * (TILES // 2))

        @block.gpsimd
        def _(pool):
            def bias(t, j):
                pool.wait_ge(own_scaled, t + 1)
                nc.gpsimd.tensor_tensor(out=own_row[j][:, :], in0=own_row[j][:, :], in1=biasb[:, 0, :],
                                        op=ALU.add).then_inc(own_biased, 1)

            def unscale(t, j):
                pool.wait_ge(scales_ready, t + 1)
                nc.gpsimd.tensor_tensor(out=blocks(xn[j]), in0=blocks(xn[j]), in1=spread(inv[j][:, :]),
                                        op=ALU.mult).then_inc(y_ready, 1)

            def rescale(t, j):
                pool.wait_ge(grid_ready, t + 1)
                nc.gpsimd.tensor_tensor(out=blocks(xn[j]), in0=blocks(xn[j]), in1=spread(scale[j][:, :]),
                                        op=ALU.mult).then_inc(xq_ready, 1)

            def residual(t, j):
                pool.wait_ge(x1_ready, t + 1 + SLOTS)
                pool.sem_inc(pool_turn, 1)
                nc.gpsimd.tensor_tensor(out=kept(t), in0=h1[j], in1=biasb[:, 1, :], op=ALU.add).then_inc(x1b_ready, 1)

            def total(t, j):
                pool.wait_ge(x1b_ready, t + 1 + SLOTS)
                pool.wait_ge(lin_ready, t + 1 + SLOTS)
                pool.sem_inc(pool_turn, 1)
                nc.gpsimd.tensor_tensor(out=lin[j][:, :], in0=lin[j][:, :], in1=kept(t), op=ALU.add).then_inc(summed, 1)

            pool.sem_inc(x1b_ready, SLOTS)
            pool.wait_ge(bias_in, 32)
            bias(0, 0)
            bias(1, 1)
            residual(0, 0)

            def turn(t, j):
                unscale(t, j)
                bias(t + 2, j)
                total(t - 3, 1 - j)
                rescale(t, j)
                residual(t + 1, 1 - j)

            for t in range(4):
                unscale(t, t % 2)
                bias(t + 2, t % 2)
                if t == 3:
                    total(0, 0)
                rescale(t, t % 2)
                residual(t + 1, (t + 1) % 2)
            with pool.Fori(2, TILES // 2 - 1) as i:
                for j in range(2):
                    turn(2 * i + j, j)
            turn(LAST - 2, 0)
            unscale(LAST - 1, 1)
            total(LAST - 4, 0)
            rescale(LAST - 1, 1)
            residual(LAST, 0)
            unscale(LAST, 0)
            total(LAST - 3, 1)
            rescale(LAST, 0)
            for t in range(LAST - 2, LAST + 1):
                total(t, t % 2)

        @block.vector
        def _(dve):
            own = Chain(dve, dve_own)
            dve.sem_inc(x1_ready, SLOTS)
            own.link(nc.vector.tensor_tensor(out=z32[:, :, :], in0=zsum[:, :, 0:HEADS], in1=zsum[:, :, HEADS:2 * HEADS], op=ALU.add))
            own.link(nc.vector.scalar_tensor_tensor(out=z32[:, :, :], in0=z32[:, :, :], scalar=1.0 / NUM_SCALE,
                                                    in1=self_num[:, :, :], op0=ALU.mult, op1=ALU.add))
            own.link(nc.vector.reciprocal(inv_z[:, :, :], z32[:, :, :]))
            nc.vector.tensor_scalar(acc_w[:, :, :], inv_z[:, :, :], xp_inverse[:, :], 1.0 / NUM_SCALE, ALU.mult, ALU.mult)
            nc.vector.tensor_scalar(out_scale[:, :], wd_inverse[:, :], 1.0 / ROW_SCALE, None, ALU.mult)
            own.link(nc.vector.tensor_tensor(out=self_w[:, :, :], in0=self_num[:, :, :], in1=inv_z[:, :, :], op=ALU.mult))
            dve.sem_inc(ratios_ready, 1)

            def mix(t, j):
                dve.wait_ge(own_biased, t + 1)
                dve.wait_ge(x1b_ready, t + 1)
                for h in range(HEADS):
                    cols = slice(h * C, (h + 1) * C)
                    last = nc.vector.scalar_tensor_tensor(
                        out=h1[j][:, cols], in0=acc[:, bass.ds(t, 1), cols].rearrange("p o n -> p (o n)"),
                        scalar=acc_w[:, bass.ds(t, 1), h:h + 1].rearrange("p o h -> p (o h)"),
                        in1=own_row[j][:, cols], op0=ALU.mult, op1=ALU.add)
                last.then_inc(mixed, 1)

            def x1(t, j, n):
                dve.wait_ge(mixed, t + 1)
                dve.wait_ge(x_in[j], 16 * (n + 1))
                nc.vector.scalar_tensor_tensor(out=h1[j], in0=h1[j], scalar=0.0, in1=xr[j][:, :], op0=ALU.max,
                                               op1=ALU.add).then_inc(x1_ready, 1)
                dve.wait_ge(x1_ready, t + 1 + SLOTS)
                nc.vector.bn_stats(stats[:, 0, :], h1[j][:, 0:512])
                own.link(nc.vector.bn_stats(stats[:, 1, :], h1[j][:, 512:1024]))
                dve.sem_inc(dve_turn, 1)
                own.link(nc.vector.bn_aggr(mv[j][:, :], stats[:, :, :].rearrange("p a b -> p (a b)")))
                nc.vector.tensor_scalar(mv[j][:, 1:2], mv[j][:, 1:2], EPS, None, ALU.add).then_inc(var_ready, 1)

            def root(t, j):
                dve.wait_ge(std_ready, t + 1)
                inverse_root(nc, own, std[j][:, :], mv[j][:, 1:2], rstd[j][:, :], newton[:, :])
                nc.vector.scalar_tensor_tensor(out=shift[j][:, :], in0=mv[j][:, 0:1], scalar=-1.0, in1=rstd[j][:, :],
                                               op0=ALU.mult, op1=ALU.mult).then_inc(rstd_ready, 1)

            def scales(t, j):
                dve.wait_ge(xn_ready, t + 1)
                block_scales(nc, own, xn[j], scale[j][:, :], inv[j][:, :]).then_inc(scales_ready, 1)

            def grid(t, j):
                dve.wait_ge(y_ready, t + 1)
                round_to_grid(nc, own, xn[j], step).then_inc(grid_ready, 1)

            def grid_and_root(t, j):
                y, s = xn[j], 1 - j
                dve.wait_ge(y_ready, t + 1)
                power = own.mark(nc.vector.tensor_scalar(step.bitcast(I32), y.bitcast(I32), EXPONENT, None, ALU.bitwise_and))
                dve.wait_ge(std_ready, t + 2)
                guess = own.mark(nc.vector.reciprocal(rstd[s][:, :], std[s][:, :]))
                own.until(power)
                least = own.mark(nc.vector.tensor_scalar(step, step, 1.0, None, ALU.max))
                own.until(guess)
                square = own.mark(nc.vector.tensor_scalar(newton[:, :], rstd[s][:, :], rstd[s][:, :], mv[s][:, 1:2], ALU.mult, ALU.mult))
                own.until(least)
                moved = own.mark(nc.vector.scalar_tensor_tensor(out=y, in0=step, scalar=6.0625, in1=y, op0=ALU.mult, op1=ALU.subtract))
                own.until(square)
                factor = own.mark(nc.vector.tensor_scalar(newton[:, :], newton[:, :], -0.5, 1.5, ALU.mult, ALU.add))
                own.until(moved)
                cut = own.mark(nc.vector.tensor_scalar(y.bitcast(I32), y.bitcast(I32), -(1 << 18), None, ALU.bitwise_and))
                own.until(factor)
                better = own.mark(nc.vector.tensor_tensor(out=rstd[s][:, :], in0=rstd[s][:, :], in1=newton[:, :], op=ALU.mult))
                own.until(cut)
                nc.vector.scalar_tensor_tensor(out=y, in0=step, scalar=6.0, in1=y, op0=ALU.mult, op1=ALU.subtract).then_inc(grid_ready, 1)
                own.until(better)
                nc.vector.scalar_tensor_tensor(out=shift[s][:, :], in0=mv[s][:, 0:1], scalar=-1.0, in1=rstd[s][:, :],
                                               op0=ALU.mult, op1=ALU.mult).then_inc(rstd_ready, 1)

            def low(t, j):
                dve.wait_ge(high_ready, t + 1 + SLOTS)
                nc.vector.scalar_tensor_tensor(
                    out=xqT[j][:, 1, :, :].rearrange("p c n -> p (c n)"), in0=tr_ps[j][:, :], scalar=ROW_SCALE,
                    in1=xqT[j][:, 0, :, :].rearrange("p c n -> p (c n)"), op0=ALU.mult, op1=ALU.subtract).then_inc(low_ready, 1)

            def turn(t, j, n, first=False, last=False):
                if not last:
                    mix(t + 1, 1 - j)
                scales(t, j)
                if not last:
                    x1(t + 1, 1 - j, n)
                if not first:
                    low(t - 1, 1 - j)
                if last:
                    grid(t, j)
                else:
                    grid_and_root(t, j)

            mix(0, 0)
            x1(0, 0, 0)
            root(0, 0)
            turn(0, 0, 0, first=True)
            links = STAT_LINKS + ROOT_LINKS + SCALE_LINKS + ROUND_LINKS
            with dve.Fori(0, TILES // 2 - 1) as i:
                back = own.enter(i, 2 * links)
                turn(2 * i + 1, 1, i + 1)
                turn(2 * i + 2, 0, i + 1)
            own.leave(back, TILES // 2 - 1)
            turn(LAST - 1, 1, TILES // 2)
            turn(LAST, 0, None, last=True)
            low(LAST, 0)

        @block.scalar
        def _(act):
            act.sem_inc(high_ready, SLOTS)
            act.sem_inc(lin_ready, SLOTS)
            act.wait_ge(ratios_ready, 1)

            def scale_own(t, j, n):
                act.wait_ge(own_in[j], 16 * (n + 1))
                for h in range(HEADS):
                    cols = slice(h * C, (h + 1) * C)
                    last = nc.scalar.activation(own_row[j][:, cols], own_row[j][:, cols], ACT.Copy,
                                                scale=self_w[:, bass.ds(t, 1), h:h + 1].rearrange("p o h -> p (o h)"))
                last.then_inc(own_scaled, 1)

            def norm(t, j):
                act.wait_ge(var_ready, t + 1)
                nc.scalar.activation(std[j][:, :], mv[j][:, 1:2], ACT.Sqrt).then_inc(std_ready, 1)
                act.wait_ge(tr_done, t + 1)
                act.wait_ge(rstd_ready, t + 1)
                nc.scalar.activation(xn[j], h1[j], ACT.Identity, bias=shift[j][:, :], scale=rstd[j][:, :]).then_inc(xn_ready, 1)

            def high(t, j):
                act.wait_ge(tr_done, t + 1 + SLOTS)
                act.wait_ge(mm_done, t + 1)
                nc.scalar.activation(xqT[j][:, 0, :, :].rearrange("p c n -> p (c n)"), tr_ps[j][:, :], ACT.Copy,
                                     scale=ROW_SCALE).then_inc(high_ready, 1)

            def linear(t, j, n):
                act.wait_ge(mm_done, t + 1 + SLOTS)
                if n is not None:
                    act.wait_ge(stored[j], n)
                nc.scalar.activation(lin[j][:, :], mm_ps[j][:, :], ACT.Copy, scale=out_scale[:, :]).then_inc(lin_ready, 1)

            scale_own(0, 0, 0)
            scale_own(1, 1, 0)
            norm(0, 0)

            for t in range(6):
                if t >= 1:
                    high(t - 1, (t - 1) % 2)
                if t >= 3:
                    linear(t - 3, (t - 3) % 2, 16 if t == 5 else None)
                scale_own(t + 2, t % 2, t // 2 + 1)
                norm(t + 1, (t + 1) % 2)
            with act.Fori(3, TILES // 2 - 1) as i:
                for j in range(2):
                    t = 2 * i + j
                    high(t - 1, 1 - j)
                    linear(t - 3, 1 - j, 16 * (i - 2 + j))
                    scale_own(t + 2, j, i + 1)
                    norm(t + 1, 1 - j)
            for t in range(LAST - 2, LAST + 1):
                high(t - 1, (t - 1) % 2)
                linear(t - 3, (t - 3) % 2, 16 * ((t - 3) // 2))
                if t + 2 <= LAST:
                    scale_own(t + 2, t % 2, t // 2 + 1)
                if t + 1 <= LAST:
                    norm(t + 1, (t + 1) % 2)
            high(LAST, 0)
            for t in range(LAST - 2, LAST + 1):
                linear(t, t % 2, 16 * (t // 2))

        @block.tensor
        def _(pe):
            pe.sem_inc(tr_done, SLOTS)
            pe.sem_inc(mm_done, SLOTS)

            def turned(t, j):
                pe.wait_ge(xq_ready, t + 1)
                for c in range(KC):
                    last = nc.tensor.transpose(tr_ps[j][:, c * P:(c + 1) * P], xn[j][:, c * P:(c + 1) * P], ident[:, :])
                last.then_inc(tr_done, 1)

            def products(t, j):
                pe.wait_ge(low_ready, t + 1)
                pe.wait_ge(lin_ready, t + 1)
                for c in range(KC):
                    for a, b in ((0, 0), (0, 1), (1, 0)):
                        for half in range(2):
                            cols = slice(half * 512, (half + 1) * 512)
                            last = nc.tensor.matmul(mm_ps[j][:, cols], xqT[j][:, a, c, :], wdT[:, c, b, cols],
                                                    start=(c == 0 and a + b == 0), stop=(c == KC - 1 and a == 1))
                last.then_inc(mm_done, 1)

            turned(0, 0)
            with pe.Fori(0, TILES // 2) as i:
                for j in range(2):
                    turned(2 * i + j + 1, 1 - j)
                    products(2 * i + j, j)
            products(LAST, 0)


_INS = ['x', 'src', 'dst', 'L0_gnn_W', 'L0_gnn_att_src', 'L0_gnn_att_dst', 'L0_gnn_bias', 'L0_ffn_weight', 'L0_ffn_bias']


def kernel(**inputs):
    import numpy as _np
    import concourse.bacc as _bacc
    from concourse import mybir as _mybir
    from concourse.bass_utils import run_bass_kernel_spmd as _run

    nc = _bacc.Bacc("TRN2", target_bir_lowering=False, num_devices=1)
    arrays, args = {}, []
    for name in _INS:
        a = _np.ascontiguousarray(inputs[name])
        arrays[f"in_{name}_dram"] = a
        args.append(nc.dram_tensor(f"in_{name}_dram", a.shape, _mybir.dt.from_np(a.dtype), kind="ExternalInput").ap())
    args.append(nc.dram_tensor("out_0_dram", (N, D), F32, kind="ExternalOutput").ap())
    program(nc, *args)
    r = _run(nc, [arrays], core_ids=[0])
    return r.results[0]["out_0_dram"]
```
